# Optimizing a Trainium2 kernel written in Bass

```python
import numpy as np
import jax
import jax.numpy as jnp

def _softmax(x, axis=-1):
    return jax.nn.softmax(x, axis=axis)

def _gelu(x):
    return jax.nn.gelu(x, approximate=True)

def _silu(x):
    return jax.nn.silu(x)

def _sigmoid(x):
    return jax.nn.sigmoid(x)

def _layernorm(x, axis=-1, eps=1e-05):
    m = jnp.mean(x, axis=axis, keepdims=True)
    v = jnp.var(x, axis=axis, keepdims=True)
    return (x - m) / jnp.sqrt(v + eps)

def _scatter_add(tgt, idx, src, axis=0):
    return tgt.at[idx].add(src)

def _segment_sum(src, seg, n):
    return jax.ops.segment_sum(src, seg, n)
kernel_name = 'mk_xattn_ffn_d4_seqx_r8_c213b9'

def setup_inputs(seed: int=0):
    np.random.seed(seed)
    _w = jnp.asarray

    def _rec_inputs():
        import jax
        import jax.numpy as jnp
        _rk = jax.random.key(seed)
        x = -0.0002928 + 1 * jax.random.normal(jax.random.fold_in(_rk, 1), (32, 64, 128), jnp.float32)
        _lenS = 64 - jax.random.randint(jax.random.fold_in(_rk, 7), (32,), 0, max(1, 64 // 4) + 1, jnp.int32)
        _lenS2 = 64 - jax.random.randint(jax.random.fold_in(_rk, 8), (32,), 0, max(1, 64 // 4) + 1, jnp.int32)
        _ctx_1024P = jax.random.normal(jax.random.fold_in(_rk, 11), (32, 16, 128), jnp.float32)
        _ctx_1024c = jax.random.dirichlet(jax.random.fold_in(_rk, 511), 0.3 * jnp.ones((16,), jnp.float32), (32, 64))
        _ctx_1024t = jnp.einsum('bsk,bkd->bsd', _ctx_1024c, _ctx_1024P)
        _ctx_1024t = _ctx_1024t * jax.lax.rsqrt(jnp.mean(jnp.square(_ctx_1024t)) + 1e-12) * 0.953939
        ctx_1024 = -1.39393e-06 + 0.999914 * (_ctx_1024t + 0.3 * jax.random.normal(jax.random.fold_in(_rk, 611), (32, 64, 128), jnp.float32))
        _validS = jnp.arange(64)[None, :] < _lenS[:, None]
        _validS2 = jnp.arange(64)[None, :] < _lenS2[:, None]
        _causal = jnp.tril(jnp.ones((64, 64), dtype=bool))
        mask_BxS2_bk0 = jnp.logical_not(jnp.broadcast_to(_validS2[:, :], (32, 64)))
        return (x, ctx_1024, _lenS2, mask_BxS2_bk0)
    x, ctx_1024, _lenS2, mask_BxS2_bk0 = _rec_inputs()

    def _L0_xattn_setup():
        import jax, jax.numpy as jnp
        import numpy as np
        import math
        EPS = 1e-08
        LN_EPS = 1e-05
        B, S, E, NH = (2, 256, 128, 4)
        DH = E // NH

        def _mlstm_cell(q, k, v, igate_w, igate_b, fgate_w, fgate_b, out_w):
            Bq, Sq, Eq = q.shape
            if_in = jnp.concatenate([q, k, v], axis=-1)
            ig = jnp.einsum('bsf,hf->bsh', if_in, igate_w) + igate_b
            fg = jnp.einsum('bsf,hf->bsh', if_in, fgate_w) + fgate_b
            ig = jnp.transpose(ig, (0, 2, 1))[..., None]
            fg = jnp.transpose(fg, (0, 2, 1))[..., None]
            qh = q.reshape(Bq, Sq, NH, DH).transpose(0, 2, 1, 3)
            kh = k.reshape(Bq, Sq, NH, DH).transpose(0, 2, 1, 3)
            vh = v.reshape(Bq, Sq, NH, DH).transpose(0, 2, 1, 3)
            log_fg = jax.nn.log_sigmoid(fg)
            cs = jnp.cumsum(log_fg, axis=2)
            cs_shift = jnp.concatenate([jnp.zeros_like(cs[:, :, :1]), cs[:, :, :-1]], axis=2)
            logfg_mat = cs - jnp.swapaxes(cs_shift, -2, -1)
            ltr = jnp.tril(jnp.ones((Sq, Sq), dtype=bool))
            logfg_mat = jnp.where(ltr, logfg_mat, -jnp.inf)
            log_D = logfg_mat + jnp.swapaxes(ig, -2, -1)
            max_log_D = jnp.max(log_D, axis=-1, keepdims=True)
            D = jnp.exp(log_D - max_log_D)
            qk = jnp.einsum('bhsd,bhtd->bhst', qh, kh / math.sqrt(DH))
            C = qk * D
            sum_C_abs = jnp.abs(jnp.sum(C, axis=-1, keepdims=True))
            normaliser = jnp.maximum(sum_C_abs, jnp.exp(-max_log_D))
            C_norm = C / (normaliser + EPS)
            h = jnp.einsum('bhst,bhtd->bhsd', C_norm, vh)
            mean = jnp.mean(h, axis=-1, keepdims=True)
            var = jnp.mean((h - mean) ** 2, axis=-1, keepdims=True)
            h_norm = (h - mean) / jnp.sqrt(var + LN_EPS)
            scale = (1.0 + out_w).reshape(1, NH, 1, DH)
            h_norm = h_norm * scale
            return h_norm.transpose(0, 2, 1, 3).reshape(Bq, Sq, Eq)
        key = jax.random.key(seed)
        ks = jax.random.split(key, 7)
        std_g = math.sqrt(2.0 / (5.0 * 3 * E))
        return {'q': jax.random.normal(ks[0], (B, S, E), dtype=jnp.float32), 'k': jax.random.normal(ks[1], (B, S, E), dtype=jnp.float32), 'v': jax.random.normal(ks[2], (B, S, E), dtype=jnp.float32), 'igate_w': jax.random.normal(ks[3], (NH, 3 * E), dtype=jnp.float32) * std_g, 'igate_b': jax.random.normal(ks[4], (NH,), dtype=jnp.float32) * 0.1, 'fgate_w': jax.random.normal(ks[5], (NH, 3 * E), dtype=jnp.float32) * std_g, 'fgate_b': jnp.linspace(3.4, 6.0, NH, dtype=jnp.float32), 'out_w': jnp.zeros((E,), dtype=jnp.float32)}
    _L0_xattn_all = _L0_xattn_setup()
    _L0_xattn_in = {k: v for k, v in _L0_xattn_all.items() if k in ('igate_w', 'igate_b', 'fgate_w', 'fgate_b', 'out_w')}
    del _L0_xattn_all

    def _L0_ffn_setup():
        import jax, jax.numpy as jnp
        import numpy as np
        S, B, H, F, E, K = (256, 2, 128, 256, 8, 2)

        def _moe_forward(hidden_states, router_w, w1, b1, w2, b2):
            s, b, h = hidden_states.shape
            T = s * b
            x = hidden_states.reshape(T, h)
            logits = jnp.einsum('th,eh->te', x, router_w)
            topk_logits, topk_idx = jax.lax.top_k(logits, K)
            probs = jax.nn.softmax(topk_logits, axis=-1)
            combine = jnp.zeros((T, E), dtype=x.dtype)
            combine = combine.at[jnp.arange(T)[:, None], topk_idx].add(probs.astype(x.dtype))
            hmid = jnp.einsum('th,efh->etf', x, w1) + b1[:, None, :]
            hmid = jax.nn.gelu(hmid, approximate=False)
            y = jnp.einsum('etf,ehf->eth', hmid, w2) + b2[:, None, :]
            out = jnp.einsum('eth,te->th', y, combine)
            return out.reshape(s, b, h)
        key = jax.random.key(seed)
        ks = jax.random.split(key, 6)
        std = 0.02
        return {'hidden_states': jax.random.normal(ks[0], (S, B, H), dtype=jnp.float32), 'router_w': jax.random.normal(ks[1], (E, H), dtype=jnp.float32) * std, 'w1': jax.random.normal(ks[2], (E, F, H), dtype=jnp.float32) * (1.0 / np.sqrt(H)), 'b1': jnp.zeros((E, F), dtype=jnp.float32), 'w2': jax.random.normal(ks[3], (E, H, F), dtype=jnp.float32) * (1.0 / np.sqrt(F)), 'b2': jnp.zeros((E, H), dtype=jnp.float32)}
    _L0_ffn_all = _L0_ffn_setup()
    _L0_ffn_in = {k: v for k, v in _L0_ffn_all.items() if k in ('router_w', 'w1', 'b1', 'w2', 'b2')}
    del _L0_ffn_all

    def _L1_xattn_setup():
        import jax, jax.numpy as jnp
        import numpy as np
        DIM, HEADS, HEAD_DIM = (128, 16, 64)
        B, L, S = (4, 256, 256)
        EPS = 1e-05
        NEG_INF = -1000000000.0

        def rms_norm(x, w):
            var = jnp.mean(jnp.square(x), axis=-1, keepdims=True)
            return x * jax.lax.rsqrt(var + EPS) * w
        key = jax.random.key(seed)
        ks = jax.random.split(key, 9)
        hd = HEADS * HEAD_DIM
        scale = 1.0 / np.sqrt(DIM)
        return {'q': jax.random.normal(ks[0], (B, L, DIM), dtype=jnp.float32), 'kv': jax.random.normal(ks[1], (B, S, DIM), dtype=jnp.float32), 'x_seqlens': jax.random.randint(ks[2], (B,), 1, S + 1, dtype=jnp.int32), 'Wq': jax.random.normal(ks[3], (DIM, hd), dtype=jnp.float32) * scale, 'Wk': jax.random.normal(ks[4], (DIM, hd), dtype=jnp.float32) * scale, 'Wv': jax.random.normal(ks[5], (DIM, hd), dtype=jnp.float32) * scale, 'Wo': jax.random.normal(ks[6], (hd, DIM), dtype=jnp.float32) * (1.0 / np.sqrt(hd)), 'q_norm_w': jnp.ones((HEAD_DIM,), dtype=jnp.float32), 'k_norm_w': jnp.ones((HEAD_DIM,), dtype=jnp.float32)}
    _L1_xattn_all = _L1_xattn_setup()
    _L1_xattn_in = {k: v for k, v in _L1_xattn_all.items() if k in ('Wq', 'Wk', 'Wv', 'Wo', 'q_norm_w', 'k_norm_w')}
    del _L1_xattn_all

    def _L1_ffn_setup():
        import jax, jax.numpy as jnp
        import numpy as np
        D_MODEL = 128
        HIDDEN = 128
        NUM_EXPERTS = 8
        TOP_K = 2
        key = jax.random.key(seed)
        ks = jax.random.split(key, 10)
        s = 0.02
        return {'x': jax.random.normal(ks[0], (2, 256, D_MODEL), dtype=jnp.float32), 'gate_w': jax.random.normal(ks[1], (NUM_EXPERTS, D_MODEL), dtype=jnp.float32) * s, 'up_w': jax.random.normal(ks[2], (NUM_EXPERTS, D_MODEL, HIDDEN), dtype=jnp.float32) * s, 'up_b': jnp.zeros((NUM_EXPERTS, HIDDEN), dtype=jnp.float32), 'down_w': jax.random.normal(ks[3], (NUM_EXPERTS, HIDDEN, D_MODEL), dtype=jnp.float32) * s, 'down_b': jnp.zeros((NUM_EXPERTS, D_MODEL), dtype=jnp.float32), 'sh_up_w': jax.random.normal(ks[4], (D_MODEL, HIDDEN), dtype=jnp.float32) * s, 'sh_up_b': jnp.zeros((HIDDEN,), dtype=jnp.float32), 'sh_down_w': jax.random.normal(ks[5], (HIDDEN, D_MODEL), dtype=jnp.float32) * s, 'sh_down_b': jnp.zeros((D_MODEL,), dtype=jnp.float32)}
    _L1_ffn_all = _L1_ffn_setup()
    _L1_ffn_in = {k: v for k, v in _L1_ffn_all.items() if k in ('gate_w', 'up_w', 'up_b', 'down_w', 'down_b', 'sh_up_w', 'sh_up_b', 'sh_down_w', 'sh_down_b')}
    del _L1_ffn_all

    def _L2_xattn_setup():
        import jax, jax.numpy as jnp
        import numpy as np
        B, S, D = (2, 256, 128)
        H, DH = (16, 64)
        INNER = H * DH
        FF = 512
        SCALE = DH ** (-0.5)
        EPS = 1e-05

        def layernorm(x, g, b):
            m = jnp.mean(x, axis=-1, keepdims=True)
            v = jnp.var(x, axis=-1, keepdims=True)
            return (x - m) * jax.lax.rsqrt(v + EPS) * g + b

        def attention(x, ctx, mask, wq, wk, wv, wo, bo):
            b, n, _ = x.shape
            j = ctx.shape[1]
            q = (x @ wq).reshape(b, n, H, DH).transpose(0, 2, 1, 3)
            k = (ctx @ wk).reshape(b, j, H, DH).transpose(0, 2, 1, 3)
            v = (ctx @ wv).reshape(b, j, H, DH).transpose(0, 2, 1, 3)
            sim = jnp.einsum('bhid,bhjd->bhij', q, k) * SCALE
            if mask is not None:
                neg = -jnp.finfo(sim.dtype).max
                sim = jnp.where(mask[:, None, None, :], neg, sim)
            attn = jax.nn.softmax(sim, axis=-1)
            out = jnp.einsum('bhij,bhjd->bhid', attn, v)
            out = out.transpose(0, 2, 1, 3).reshape(b, n, INNER)
            return out @ wo + bo
        key = jax.random.key(seed)
        ks = jax.random.split(key, 26)
        w = lambda k, shp, fan: (jax.random.normal(k, shp, jnp.float32) / np.sqrt(fan)).astype(jnp.float32)
        return {'x': jax.random.normal(ks[0], (B, S, D), jnp.float32), 'enc_output': jax.random.normal(ks[1], (B, S, D), jnp.float32), 'sa_wq': w(ks[2], (D, INNER), D), 'sa_wk': w(ks[3], (D, INNER), D), 'sa_wv': w(ks[4], (D, INNER), D), 'sa_wo': w(ks[5], (INNER, D), INNER), 'sa_bo': jnp.zeros((D,), jnp.float32), 'ca_wq': w(ks[6], (D, INNER), D), 'ca_wk': w(ks[7], (D, INNER), D), 'ca_wv': w(ks[8], (D, INNER), D), 'ca_wo': w(ks[9], (INNER, D), INNER), 'ca_bo': jnp.zeros((D,), jnp.float32), 'ln1_g': jnp.ones((D,), jnp.float32), 'ln1_b': jnp.zeros((D,), jnp.float32), 'ln2_g': jnp.ones((D,), jnp.float32), 'ln2_b': jnp.zeros((D,), jnp.float32), 'ln3_g': jnp.ones((D,), jnp.float32), 'ln3_b': jnp.zeros((D,), jnp.float32), 'fc1_w': w(ks[10], (D, FF), D), 'fc1_b': jnp.zeros((FF,), jnp.float32), 'fc2_w': w(ks[11], (FF, D), FF), 'fc2_b': jnp.zeros((D,), jnp.float32), 'tgt_mask': jax.random.bernoulli(ks[12], 0.1, (B, S)), 'src_mask': jax.random.bernoulli(ks[13], 0.1, (B, S))}
    _L2_xattn_all = _L2_xattn_setup()
    _L2_xattn_in = {k: v for k, v in _L2_xattn_all.items() if k in ('sa_wq', 'sa_wk', 'sa_wv', 'sa_wo', 'sa_bo', 'ca_wq', 'ca_wk', 'ca_wv', 'ca_wo', 'ca_bo', 'ln1_g', 'ln1_b', 'ln2_g', 'ln2_b', 'ln3_g', 'ln3_b', 'fc1_w', 'fc1_b', 'fc2_w', 'fc2_b')}
    del _L2_xattn_all

    def _L2_ffn_setup():
        import jax, jax.numpy as jnp
        import numpy as np
        B, S, D_IN, D_OUT = (16, 512, 128, 128)
        ACT_BITS = 8
        QB = float(2 ** (ACT_BITS - 1) - 1)
        key = jax.random.key(seed)
        k1, k2, k3 = jax.random.split(key, 3)
        x = jax.random.normal(k1, (B, S, D_IN), dtype=jnp.float32)
        ternary_weight = jax.random.randint(k2, (D_OUT, D_IN), 0, 3, dtype=jnp.int32)
        bias = jax.random.normal(k3, (D_OUT,), dtype=jnp.float32)
        act_scale = (jnp.max(jnp.abs(x)) / QB).astype(jnp.float32)
        return {'x': x, 'ternary_weight': ternary_weight, 'bias': bias, 'act_scale': act_scale}
    _L2_ffn_all = _L2_ffn_setup()
    _L2_ffn_in = {k: v for k, v in _L2_ffn_all.items() if k in ('ternary_weight', 'bias', 'act_scale')}
    del _L2_ffn_all

    def _L3_xattn_setup():
        import jax, jax.numpy as jnp
        import numpy as np
        EMBED_DIM = 128
        NUM_HEADS = 16
        HEAD_DIM = EMBED_DIM // NUM_HEADS
        WINDOW = 128
        key = jax.random.key(seed)
        ks = jax.random.split(key, 11)
        B, S, E = (2, 256, EMBED_DIM)
        scale = 1.0 / np.sqrt(E)
        inp = {'q': jax.random.normal(ks[0], (B, S, E), jnp.float32), 'k': jax.random.normal(ks[1], (B, S, E), jnp.float32), 'v': jax.random.normal(ks[2], (B, S, E), jnp.float32), 'Wq': jax.random.normal(ks[3], (E, E), jnp.float32) * scale, 'bq': jnp.zeros((E,), jnp.float32), 'Wk': jax.random.normal(ks[4], (E, E), jnp.float32) * scale, 'bk': jnp.zeros((E,), jnp.float32), 'Wv': jax.random.normal(ks[5], (E, E), jnp.float32) * scale, 'bv': jnp.zeros((E,), jnp.float32), 'Wo': jax.random.normal(ks[6], (E, E), jnp.float32) * scale, 'bo': jnp.zeros((E,), jnp.float32)}
        return inp
    _L3_xattn_all = _L3_xattn_setup()
    _L3_xattn_in = {k: v for k, v in _L3_xattn_all.items() if k in ('Wq', 'bq', 'Wk', 'bk', 'Wv', 'bv', 'Wo', 'bo')}
    del _L3_xattn_all

    def _L3_ffn_setup():
        import jax, jax.numpy as jnp
        import numpy as np

        def _ste(w, w_q):
            return w + jax.lax.stop_gradient(w_q - w)

        def quantize_w8_per(w, axis):
            amax = jnp.clip(jnp.max(jnp.abs(w), axis=axis, keepdims=True), 1e-08, None)
            scale = 127.0 / amax
            w_q = jnp.clip(jnp.round(w * scale), -128.0, 127.0) / scale
            return _ste(w, w_q)

        def quantize_a16(x):
            amax = jnp.clip(jnp.max(jnp.abs(x)), 1e-08, None)
            scale = 32767.0 / amax
            x_q = jnp.clip(jnp.round(x * scale), -32768.0, 32767.0) / scale
            return _ste(x, x_q)
        key = jax.random.key(seed)
        k1, k2, k3 = jax.random.split(key, 3)
        d_model, d_ff = (128, 512)
        x = jax.random.normal(k1, (4, 256, d_model), dtype=jnp.float32)
        W_in = jax.random.normal(k2, (d_model, d_ff), dtype=jnp.float32) / np.sqrt(d_model)
        b_in = jnp.zeros((d_ff,), dtype=jnp.float32)
        W_out = jax.random.normal(k3, (d_ff, d_model), dtype=jnp.float32) / np.sqrt(d_ff)
        b_out = jnp.zeros((d_model,), dtype=jnp.float32)
        return {'x': x, 'W_in': W_in, 'b_in': b_in, 'W_out': W_out, 'b_out': b_out}
    _L3_ffn_all = _L3_ffn_setup()
    _L3_ffn_in = {k: v for k, v in _L3_ffn_all.items() if k in ('W_in', 'b_in', 'W_out', 'b_out')}
    del _L3_ffn_all
    return {'x': x, 'ctx_1024': ctx_1024, '_lenS2': _lenS2, 'mask_BxS2_bk0': mask_BxS2_bk0, 'L0_xattn_igate_w': _L0_xattn_in['igate_w'], 'L0_xattn_igate_b': _L0_xattn_in['igate_b'], 'L0_xattn_fgate_w': _L0_xattn_in['fgate_w'], 'L0_xattn_fgate_b': _L0_xattn_in['fgate_b'], 'L0_xattn_out_w': _L0_xattn_in['out_w'], 'L0_ffn_router_w': _L0_ffn_in['router_w'], 'L0_ffn_w1': _L0_ffn_in['w1'], 'L0_ffn_b1': _L0_ffn_in['b1'], 'L0_ffn_w2': _L0_ffn_in['w2'], 'L0_ffn_b2': _L0_ffn_in['b2'], 'L1_xattn_Wq': _L1_xattn_in['Wq'], 'L1_xattn_Wk': _L1_xattn_in['Wk'], 'L1_xattn_Wv': _L1_xattn_in['Wv'], 'L1_xattn_Wo': _L1_xattn_in['Wo'], 'L1_xattn_q_norm_w': _L1_xattn_in['q_norm_w'], 'L1_xattn_k_norm_w': _L1_xattn_in['k_norm_w'], 'L1_ffn_gate_w': _L1_ffn_in['gate_w'], 'L1_ffn_up_w': _L1_ffn_in['up_w'], 'L1_ffn_up_b': _L1_ffn_in['up_b'], 'L1_ffn_down_w': _L1_ffn_in['down_w'], 'L1_ffn_down_b': _L1_ffn_in['down_b'], 'L1_ffn_sh_up_w': _L1_ffn_in['sh_up_w'], 'L1_ffn_sh_up_b': _L1_ffn_in['sh_up_b'], 'L1_ffn_sh_down_w': _L1_ffn_in['sh_down_w'], 'L1_ffn_sh_down_b': _L1_ffn_in['sh_down_b'], 'L2_xattn_sa_wq': _L2_xattn_in['sa_wq'], 'L2_xattn_sa_wk': _L2_xattn_in['sa_wk'], 'L2_xattn_sa_wv': _L2_xattn_in['sa_wv'], 'L2_xattn_sa_wo': _L2_xattn_in['sa_wo'], 'L2_xattn_sa_bo': _L2_xattn_in['sa_bo'], 'L2_xattn_ca_wq': _L2_xattn_in['ca_wq'], 'L2_xattn_ca_wk': _L2_xattn_in['ca_wk'], 'L2_xattn_ca_wv': _L2_xattn_in['ca_wv'], 'L2_xattn_ca_wo': _L2_xattn_in['ca_wo'], 'L2_xattn_ca_bo': _L2_xattn_in['ca_bo'], 'L2_xattn_ln1_g': _L2_xattn_in['ln1_g'], 'L2_xattn_ln1_b': _L2_xattn_in['ln1_b'], 'L2_xattn_ln2_g': _L2_xattn_in['ln2_g'], 'L2_xattn_ln2_b': _L2_xattn_in['ln2_b'], 'L2_xattn_ln3_g': _L2_xattn_in['ln3_g'], 'L2_xattn_ln3_b': _L2_xattn_in['ln3_b'], 'L2_xattn_fc1_w': _L2_xattn_in['fc1_w'], 'L2_xattn_fc1_b': _L2_xattn_in['fc1_b'], 'L2_xattn_fc2_w': _L2_xattn_in['fc2_w'], 'L2_xattn_fc2_b': _L2_xattn_in['fc2_b'], 'L2_ffn_ternary_weight': _L2_ffn_in['ternary_weight'], 'L2_ffn_bias': _L2_ffn_in['bias'], 'L2_ffn_act_scale': _L2_ffn_in['act_scale'], 'L3_xattn_Wq': _L3_xattn_in['Wq'], 'L3_xattn_bq': _L3_xattn_in['bq'], 'L3_xattn_Wk': _L3_xattn_in['Wk'], 'L3_xattn_bk': _L3_xattn_in['bk'], 'L3_xattn_Wv': _L3_xattn_in['Wv'], 'L3_xattn_bv': _L3_xattn_in['bv'], 'L3_xattn_Wo': _L3_xattn_in['Wo'], 'L3_xattn_bo': _L3_xattn_in['bo'], 'L3_ffn_W_in': _L3_ffn_in['W_in'], 'L3_ffn_b_in': _L3_ffn_in['b_in'], 'L3_ffn_W_out': _L3_ffn_in['W_out'], 'L3_ffn_b_out': _L3_ffn_in['b_out']}

def reference(x, ctx_1024, _lenS2, mask_BxS2_bk0, L0_xattn_igate_w, L0_xattn_igate_b, L0_xattn_fgate_w, L0_xattn_fgate_b, L0_xattn_out_w, L0_ffn_router_w, L0_ffn_w1, L0_ffn_b1, L0_ffn_w2, L0_ffn_b2, L1_xattn_Wq, L1_xattn_Wk, L1_xattn_Wv, L1_xattn_Wo, L1_xattn_q_norm_w, L1_xattn_k_norm_w, L1_ffn_gate_w, L1_ffn_up_w, L1_ffn_up_b, L1_ffn_down_w, L1_ffn_down_b, L1_ffn_sh_up_w, L1_ffn_sh_up_b, L1_ffn_sh_down_w, L1_ffn_sh_down_b, L2_xattn_sa_wq, L2_xattn_sa_wk, L2_xattn_sa_wv, L2_xattn_sa_wo, L2_xattn_sa_bo, L2_xattn_ca_wq, L2_xattn_ca_wk, L2_xattn_ca_wv, L2_xattn_ca_wo, L2_xattn_ca_bo, L2_xattn_ln1_g, L2_xattn_ln1_b, L2_xattn_ln2_g, L2_xattn_ln2_b, L2_xattn_ln3_g, L2_xattn_ln3_b, L2_xattn_fc1_w, L2_xattn_fc1_b, L2_xattn_fc2_w, L2_xattn_fc2_b, L2_ffn_ternary_weight, L2_ffn_bias, L2_ffn_act_scale, L3_xattn_Wq, L3_xattn_bq, L3_xattn_Wk, L3_xattn_bk, L3_xattn_Wv, L3_xattn_bv, L3_xattn_Wo, L3_xattn_bo, L3_ffn_W_in, L3_ffn_b_in, L3_ffn_W_out, L3_ffn_b_out):
    import jax
    import jax.numpy as jnp

    def _L0_xattn_ref(q, k, v, igate_w, igate_b, fgate_w, fgate_b, out_w):
        import jax, jax.numpy as jnp
        import numpy as np
        import math
        EPS = 1e-08
        LN_EPS = 1e-05
        B, S, E, NH = (2, 256, 128, 4)
        DH = E // NH

        def _mlstm_cell(q, k, v, igate_w, igate_b, fgate_w, fgate_b, out_w):
            Bq, Sq, Eq = q.shape
            if_in = jnp.concatenate([q, k, v], axis=-1)
            ig = jnp.einsum('bsf,hf->bsh', if_in, igate_w) + igate_b
            fg = jnp.einsum('bsf,hf->bsh', if_in, fgate_w) + fgate_b
            ig = jnp.transpose(ig, (0, 2, 1))[..., None]
            fg = jnp.transpose(fg, (0, 2, 1))[..., None]
            qh = q.reshape(Bq, Sq, NH, DH).transpose(0, 2, 1, 3)
            kh = k.reshape(Bq, Sq, NH, DH).transpose(0, 2, 1, 3)
            vh = v.reshape(Bq, Sq, NH, DH).transpose(0, 2, 1, 3)
            log_fg = jax.nn.log_sigmoid(fg)
            cs = jnp.cumsum(log_fg, axis=2)
            cs_shift = jnp.concatenate([jnp.zeros_like(cs[:, :, :1]), cs[:, :, :-1]], axis=2)
            logfg_mat = cs - jnp.swapaxes(cs_shift, -2, -1)
            ltr = jnp.tril(jnp.ones((Sq, Sq), dtype=bool))
            logfg_mat = jnp.where(ltr, logfg_mat, -jnp.inf)
            log_D = logfg_mat + jnp.swapaxes(ig, -2, -1)
            max_log_D = jnp.max(log_D, axis=-1, keepdims=True)
            D = jnp.exp(log_D - max_log_D)
            qk = jnp.einsum('bhsd,bhtd->bhst', qh, kh / math.sqrt(DH))
            C = qk * D
            sum_C_abs = jnp.abs(jnp.sum(C, axis=-1, keepdims=True))
            normaliser = jnp.maximum(sum_C_abs, jnp.exp(-max_log_D))
            C_norm = C / (normaliser + EPS)
            h = jnp.einsum('bhst,bhtd->bhsd', C_norm, vh)
            mean = jnp.mean(h, axis=-1, keepdims=True)
            var = jnp.mean((h - mean) ** 2, axis=-1, keepdims=True)
            h_norm = (h - mean) / jnp.sqrt(var + LN_EPS)
            scale = (1.0 + out_w).reshape(1, NH, 1, DH)
            h_norm = h_norm * scale
            return h_norm.transpose(0, 2, 1, 3).reshape(Bq, Sq, Eq)
        return _mlstm_cell(q, k, v, igate_w, igate_b, fgate_w, fgate_b, out_w)

    def _L0_ffn_ref(hidden_states, router_w, w1, b1, w2, b2):
        import jax, jax.numpy as jnp
        import numpy as np
        S, B, H, F, E, K = (256, 2, 128, 256, 8, 2)

        def _moe_forward(hidden_states, router_w, w1, b1, w2, b2):
            s, b, h = hidden_states.shape
            T = s * b
            x = hidden_states.reshape(T, h)
            logits = jnp.einsum('th,eh->te', x, router_w)
            topk_logits, topk_idx = jax.lax.top_k(logits, K)
            probs = jax.nn.softmax(topk_logits, axis=-1)
            combine = jnp.zeros((T, E), dtype=x.dtype)
            combine = combine.at[jnp.arange(T)[:, None], topk_idx].add(probs.astype(x.dtype))
            hmid = jnp.einsum('th,efh->etf', x, w1) + b1[:, None, :]
            hmid = jax.nn.gelu(hmid, approximate=False)
            y = jnp.einsum('etf,ehf->eth', hmid, w2) + b2[:, None, :]
            out = jnp.einsum('eth,te->th', y, combine)
            return out.reshape(s, b, h)
        return _moe_forward(hidden_states, router_w, w1, b1, w2, b2)

    def _L1_xattn_ref(q, kv, x_seqlens, Wq, Wk, Wv, Wo, q_norm_w, k_norm_w):
        import jax, jax.numpy as jnp
        import numpy as np
        DIM, HEADS, HEAD_DIM = (128, 16, 64)
        B, L, S = (4, 256, 256)
        EPS = 1e-05
        NEG_INF = -1000000000.0

        def rms_norm(x, w):
            var = jnp.mean(jnp.square(x), axis=-1, keepdims=True)
            return x * jax.lax.rsqrt(var + EPS) * w
        b, l, _ = q.shape
        s = kv.shape[1]
        qh = (q @ Wq).reshape(b, l, HEADS, HEAD_DIM).transpose(0, 2, 1, 3)
        kh = (kv @ Wk).reshape(b, s, HEADS, HEAD_DIM).transpose(0, 2, 1, 3)
        vh = (kv @ Wv).reshape(b, s, HEADS, HEAD_DIM).transpose(0, 2, 1, 3)
        qh = rms_norm(qh, q_norm_w)
        kh = rms_norm(kh, k_norm_w)
        mask = (jnp.arange(s, dtype=jnp.int32)[None, :] < x_seqlens[:, None])[:, None, None, :]
        scores = jnp.einsum('bhld,bhsd->bhls', qh, kh) * (1.0 / np.sqrt(HEAD_DIM))
        scores = jnp.where(mask, scores, NEG_INF)
        attn = jax.nn.softmax(scores, axis=-1)
        o = jnp.einsum('bhls,bhsd->bhld', attn, vh)
        o = o.transpose(0, 2, 1, 3).reshape(b, l, HEADS * HEAD_DIM)
        return o @ Wo

    def _L1_ffn_ref(x, gate_w, up_w, up_b, down_w, down_b, sh_up_w, sh_up_b, sh_down_w, sh_down_b):
        import jax, jax.numpy as jnp
        import numpy as np
        D_MODEL = 128
        HIDDEN = 128
        NUM_EXPERTS = 8
        TOP_K = 2
        b, s, d = x.shape
        xf = x.reshape(-1, d)
        shared = jax.nn.silu(x @ sh_up_w + sh_up_b) @ sh_down_w + sh_down_b
        logits = xf @ gate_w.T
        scores = jax.nn.softmax(logits, axis=-1)
        topk_w, topk_i = jax.lax.top_k(scores, TOP_K)
        topk_w = topk_w / (topk_w.sum(axis=-1, keepdims=True) + 1e-20)
        comb = (jax.nn.one_hot(topk_i, NUM_EXPERTS, dtype=xf.dtype) * topk_w[..., None]).sum(axis=1)
        h = jnp.einsum('nd,edh->neh', xf, up_w) + up_b
        h = jax.nn.silu(h)
        ye = jnp.einsum('neh,ehd->ned', h, down_w) + down_b
        y = jnp.einsum('ned,ne->nd', ye, comb).reshape(b, s, d)
        return y + shared

    def _L2_xattn_ref(x, enc_output, sa_wq, sa_wk, sa_wv, sa_wo, sa_bo, ca_wq, ca_wk, ca_wv, ca_wo, ca_bo, ln1_g, ln1_b, ln2_g, ln2_b, ln3_g, ln3_b, fc1_w, fc1_b, fc2_w, fc2_b, tgt_mask, src_mask):
        import jax, jax.numpy as jnp
        import numpy as np
        B, S, D = (2, 256, 128)
        H, DH = (16, 64)
        INNER = H * DH
        FF = 512
        SCALE = DH ** (-0.5)
        EPS = 1e-05

        def layernorm(x, g, b):
            m = jnp.mean(x, axis=-1, keepdims=True)
            v = jnp.var(x, axis=-1, keepdims=True)
            return (x - m) * jax.lax.rsqrt(v + EPS) * g + b

        def attention(x, ctx, mask, wq, wk, wv, wo, bo):
            b, n, _ = x.shape
            j = ctx.shape[1]
            q = (x @ wq).reshape(b, n, H, DH).transpose(0, 2, 1, 3)
            k = (ctx @ wk).reshape(b, j, H, DH).transpose(0, 2, 1, 3)
            v = (ctx @ wv).reshape(b, j, H, DH).transpose(0, 2, 1, 3)
            sim = jnp.einsum('bhid,bhjd->bhij', q, k) * SCALE
            if mask is not None:
                neg = -jnp.finfo(sim.dtype).max
                sim = jnp.where(mask[:, None, None, :], neg, sim)
            attn = jax.nn.softmax(sim, axis=-1)
            out = jnp.einsum('bhij,bhjd->bhid', attn, v)
            out = out.transpose(0, 2, 1, 3).reshape(b, n, INNER)
            return out @ wo + bo
        a = attention(x, x, tgt_mask, sa_wq, sa_wk, sa_wv, sa_wo, sa_bo)
        x = layernorm(x + a, ln1_g, ln1_b)
        a = attention(x, enc_output, src_mask, ca_wq, ca_wk, ca_wv, ca_wo, ca_bo)
        x = layernorm(x + a, ln2_g, ln2_b)
        h = jax.nn.gelu(x @ fc1_w + fc1_b, approximate=False)
        ff = h @ fc2_w + fc2_b
        x = layernorm(x + ff, ln3_g, ln3_b)
        return x

    def _L2_ffn_ref(x, ternary_weight, bias, act_scale):
        import jax, jax.numpy as jnp
        import numpy as np
        B, S, D_IN, D_OUT = (16, 512, 128, 128)
        ACT_BITS = 8
        QB = float(2 ** (ACT_BITS - 1) - 1)
        scale = jnp.maximum(act_scale, 1e-05)
        x_int = jnp.clip(jnp.round(x / scale), -QB, QB)
        x_dq = jnp.nan_to_num(x_int * scale, nan=0.0, posinf=10000.0, neginf=-10000.0)
        w = ternary_weight.astype(jnp.float32) - 1.0
        return jnp.einsum('bsi,oi->bso', x_dq, w) + bias

    def _L3_xattn_ref(q, k, v, Wq, bq, Wk, bk, Wv, bv, Wo, bo):
        import jax, jax.numpy as jnp
        import numpy as np
        EMBED_DIM = 128
        NUM_HEADS = 16
        HEAD_DIM = EMBED_DIM // NUM_HEADS
        WINDOW = 128
        B, S, E = q.shape
        H, D = (NUM_HEADS, HEAD_DIM)
        Q = (q @ Wq.T + bq).reshape(B, S, H, D).transpose(0, 2, 1, 3)
        K = (k @ Wk.T + bk).reshape(B, S, H, D).transpose(0, 2, 1, 3)
        V = (v @ Wv.T + bv).reshape(B, S, H, D).transpose(0, 2, 1, 3)
        scores = jnp.einsum('bhqd,bhkd->bhqk', Q, K) / jnp.sqrt(jnp.float32(D))
        idx = jnp.arange(S)
        band = jnp.abs(idx[:, None] - idx[None, :]) <= WINDOW
        scores = jnp.where(band[None, None], scores, -jnp.inf)
        probs = jax.nn.softmax(scores, axis=-1)
        out = jnp.einsum('bhqk,bhkd->bhqd', probs, V)
        out = out.transpose(0, 2, 1, 3).reshape(B, S, E)
        return out @ Wo.T + bo

    def _L3_ffn_ref(x, W_in, b_in, W_out, b_out):
        import jax, jax.numpy as jnp
        import numpy as np

        def _ste(w, w_q):
            return w + jax.lax.stop_gradient(w_q - w)

        def quantize_w8_per(w, axis):
            amax = jnp.clip(jnp.max(jnp.abs(w), axis=axis, keepdims=True), 1e-08, None)
            scale = 127.0 / amax
            w_q = jnp.clip(jnp.round(w * scale), -128.0, 127.0) / scale
            return _ste(w, w_q)

        def quantize_a16(x):
            amax = jnp.clip(jnp.max(jnp.abs(x)), 1e-08, None)
            scale = 32767.0 / amax
            x_q = jnp.clip(jnp.round(x * scale), -32768.0, 32767.0) / scale
            return _ste(x, x_q)
        W_in_sim = quantize_w8_per(W_in, axis=0)
        W_out_sim = quantize_w8_per(W_out, axis=1)
        x_sim = quantize_a16(x)
        hidden = jax.nn.gelu(x_sim @ W_in_sim + b_in, approximate=False)
        hidden_sim = quantize_a16(hidden)
        out = hidden_sim @ W_out_sim + b_out
        return out
    x = x + _L0_xattn_ref(_layernorm(x, axis=-1), ctx_1024, ctx_1024, L0_xattn_igate_w, L0_xattn_igate_b, L0_xattn_fgate_w, L0_xattn_fgate_b, L0_xattn_out_w)
    x = x + _L0_ffn_ref(_layernorm(x, axis=-1), L0_ffn_router_w, L0_ffn_w1, L0_ffn_b1, L0_ffn_w2, L0_ffn_b2)
    x = x + _L1_xattn_ref(_layernorm(x, axis=-1), ctx_1024, _lenS2, L1_xattn_Wq, L1_xattn_Wk, L1_xattn_Wv, L1_xattn_Wo, L1_xattn_q_norm_w, L1_xattn_k_norm_w)
    x = x + _L1_ffn_ref(_layernorm(x, axis=-1), L1_ffn_gate_w, L1_ffn_up_w, L1_ffn_up_b, L1_ffn_down_w, L1_ffn_down_b, L1_ffn_sh_up_w, L1_ffn_sh_up_b, L1_ffn_sh_down_w, L1_ffn_sh_down_b)
    x = x + _L2_xattn_ref(_layernorm(x, axis=-1), ctx_1024, L2_xattn_sa_wq, L2_xattn_sa_wk, L2_xattn_sa_wv, L2_xattn_sa_wo, L2_xattn_sa_bo, L2_xattn_ca_wq, L2_xattn_ca_wk, L2_xattn_ca_wv, L2_xattn_ca_wo, L2_xattn_ca_bo, L2_xattn_ln1_g, L2_xattn_ln1_b, L2_xattn_ln2_g, L2_xattn_ln2_b, L2_xattn_ln3_g, L2_xattn_ln3_b, L2_xattn_fc1_w, L2_xattn_fc1_b, L2_xattn_fc2_w, L2_xattn_fc2_b, mask_BxS2_bk0, mask_BxS2_bk0)
    x = x + _L2_ffn_ref(_layernorm(x, axis=-1), L2_ffn_ternary_weight, L2_ffn_bias, L2_ffn_act_scale)
    x = x + _L3_xattn_ref(_layernorm(x, axis=-1), ctx_1024, ctx_1024, L3_xattn_Wq, L3_xattn_bq, L3_xattn_Wk, L3_xattn_bk, L3_xattn_Wv, L3_xattn_bv, L3_xattn_Wo, L3_xattn_bo)
    x = x + _L3_ffn_ref(_layernorm(x, axis=-1), L3_ffn_W_in, L3_ffn_b_in, L3_ffn_W_out, L3_ffn_b_out)
    return x

_drawn_inputs = setup_inputs


def setup_inputs(seed=0):
    import zlib

    import numpy as np

    out = dict(_drawn_inputs(seed))
    spreads = {'L0_xattn_out_w': (0.0, 0.1),
     'L0_ffn_b1': (0.0, 0.1),
     'L0_ffn_b2': (0.0, 0.1),
     'L1_xattn_q_norm_w': (1.0, 0.2),
     'L1_xattn_k_norm_w': (1.0, 0.2),
     'L1_ffn_up_b': (0.0, 0.699),
     'L1_ffn_down_b': (0.0, 0.1),
     'L1_ffn_sh_up_b': (0.0, 0.563),
     'L1_ffn_sh_down_b': (0.0, 0.1),
     'L2_xattn_sa_bo': (0.0, 0.1),
     'L2_xattn_ca_bo': (0.0, 0.1),
     'L2_xattn_ln1_g': (1.0, 0.2),
     'L2_xattn_ln1_b': (0.0, 0.1),
     'L2_xattn_ln2_g': (1.0, 0.2),
     'L2_xattn_ln2_b': (0.0, 0.1),
     'L2_xattn_ln3_g': (1.0, 0.2),
     'L2_xattn_ln3_b': (0.0, 0.1),
     'L2_xattn_fc1_b': (0.0, 0.279),
     'L2_xattn_fc2_b': (0.0, 0.1),
     'L3_xattn_bq': (0.0, 2.0),
     'L3_xattn_bk': (0.0, 2.0),
     'L3_xattn_bv': (0.0, 0.8),
     'L3_xattn_bo': (0.0, 0.762),
     'L3_ffn_b_in': (0.0, 0.8),
     'L3_ffn_b_out': (0.0, 0.8)}
    factors = {'L0_xattn_igate_b': 64.0,
     'L1_ffn_up_w': 3.933,
     'L1_ffn_down_w': 3.743,
     'L1_ffn_sh_up_w': 3.199,
     'L1_ffn_sh_down_w': 3.029}
    for name, (base, spread) in spreads.items():
        noise = np.random.default_rng([zlib.crc32(name.encode()), seed]).standard_normal(out[name].shape)
        drawn = base * np.exp(spread * noise) if base else spread * noise
        out[name] = jnp.asarray(drawn.astype(out[name].dtype))
    for name, factor in factors.items():
        out[name] = (out[name] * factor).astype(out[name].dtype)
    return out
```

```python
from contextlib import ExitStack

import concourse.bass as bass
from concourse import mybir

F32 = mybir.dt.float32
I32 = mybir.dt.int32
U32 = mybir.dt.uint32
U8 = mybir.dt.uint8
ALU = mybir.AluOpType
ACT = mybir.ActivationFunctionType
AX = mybir.AxisListType.X
ABSMAX = bass.bass_isa.ReduceOp.absmax

P = 128
B, S, D = 32, 64, 128
T = B * S
TILES = T // P
PAIRS = TILES // 2
PT = 2 * P
NEG = 3.0e38
ROUND = 12582912.0
FLT_MAX = 3.4028234663852886e38
BUMP = 64

SECTIONS = [
    ("gates", 768), ("gate_bias", 2),
    ("m0_router", 8), ("m0_up", 2048), ("m0_upb", 16), ("m0_down", 2048),
    ("a1_wq", 1024), ("a1_wk", 1024), ("a1_wv", 1024), ("a1_wo", 1024), ("a1_norm", 2),
    ("m1_router", 8), ("m1_up", 1152), ("m1_upb", 9), ("m1_down", 1152),
    ("sa_wq", 1024), ("sa_wk", 1024), ("sa_wv", 1024), ("sa_wo", 1024),
    ("ca_wq", 1024), ("ca_wk", 1024), ("ca_wv", 1024), ("ca_wo", 1024),
    ("fc1", 512), ("fc1b", 4), ("fc2", 512),
    ("l3_wq", 128), ("l3_wk", 128), ("l3_wv", 128), ("l3_wo", 128), ("l3_qkb", 2),
    ("l3_in", 512), ("l3_inb", 4), ("l3_out", 512),
]
WIDTH = sum(n for _, n in SECTIONS)
ROWS = ["out_w", "sa_bo", "ca_bo", "ln1_g", "ln1_b", "ln2_g", "ln2_b", "ln3_g", "ln3_b", "fc2_b",
        "tern_b", "l3_bv", "l3_bo", "l3_bout"]


class Stage:

    def __init__(self, index, units, before, sems, ring=6):
        self.index, self.units = index, units
        self.names = [n for n, _ in units]
        self.sems = sems
        self.filled0, self.base = (before.filled0 + len(before.units) * PAIRS, {
            e: before.base[e] + before.per[e] * PAIRS for e in "av"}) if before else (0, {"a": BUMP, "v": BUMP})
        self.per = {e: sum(1 for _, k in units if k == e) for e in "av"}
        self.ring = ring

    def bank(self, name):
        return self.names.index(name) % self.ring

    def filled(self, p, name):
        return p * len(self.units) + (self.filled0 + self.names.index(name) + 1)

    def _emptied(self, p, j, back):
        e = self.units[j][1]
        order = sum(1 for _, k in self.units[:j + 1] if k == e)
        return self.sems[e], p * self.per[e] + (self.base[e] + order - back * self.per[e])

    def emptied(self, p, name):
        return self._emptied(p, self.names.index(name), 0)

    def bank_free(self, p, name):
        j = self.names.index(name)
        if j >= self.ring:
            return self._emptied(p, j - self.ring, 0)
        last = max(k for k in range(len(self.units)) if k % self.ring == j % self.ring)
        return self._emptied(p, last, 1)


def build_program(nc, wpack, x_in, ctx_in, ctxT_in, rows_in, moeb_in, lens_in, mask_in, tern_in, scale_in, out,
                  layers=8):
    es = ExitStack()
    with es:
        def sb(name, shape, dt=F32):
            return es.enter_context(nc.sbuf_tensor(name, shape, dt))

        def sem(name):
            return es.enter_context(nc.semaphore(name))

        W = sb("weights", [P, WIDTH])
        wcol, at = {}, 0
        for name, n in SECTIONS:
            wcol[name] = (at, n)
            at += n

        def w(name):
            a, n = wcol[name]
            return W[:, a:a + n]

        x_all = sb("x_all", [P, TILES, D])
        xT_all = sb("xT_all", [P, T])
        ctxT_all = sb("ctxT_all", [P, T])
        tok_all = sb("tok_all", [P, TILES, D])
        keep_len = sb("keep_len", [P, T])
        keep_mask = sb("keep_mask", [P, T])
        rows = sb("rows", [P, len(ROWS), D])
        moeb = sb("moeb", [9, 2, D])
        ternw = sb("ternw", [P, D])
        ident = sb("ident", [P, P])
        stack2 = sb("stack2", [P, S])
        xs = sb("xs", [P, PT])
        cs = sb("cs", [P, PT])
        ks = sb("ks", [P, PT])
        negm = sb("negm", [P, PT])
        xn = sb("xn", [P, 2, D])
        xr = sb("xr", [P, 2, D])
        st = sb("st", [P, 2, 6])
        mv = sb("mv", [P, 2, 2])
        var = sb("var", [P, 2])
        rstd = sb("rstd", [P, 2])
        nhalf = sb("nhalf", [P, 32])
        euler = sb("euler", [P, 16])
        work = sb("work", [P, 12288])
        small = sb("small", [P, 512])
        iota8 = sb("iota8", [P, 16])
        ix = sb("ix", [P, 2, 8], U32)
        row1 = sb("row1", [P, 1])
        row2 = sb("row2", [P, 1])
        row1h = sb("row1h", [P, 4])
        negrow2 = sb("negrow2", [P, 4])
        quarter = sb("quarter", [P, 4])
        parity = sb("parity", [P, 2])
        headmask = sb("headmask", [P, 16])
        causal = sb("causal", [P, S])
        restart = sb("restart", [P, PT])
        restart_neg = sb("restart_neg", [P, PT])
        iseq = sb("iseq", [P, S])
        lensf = sb("lensf", [P, B])
        actscale = sb("actscale", [P, 2])
        amax = sb("amax", [P, 16])
        big = es.enter_context(nc.psum_tensor("banks", [P, 8, 512], F32))

        def bank(i):
            return big[:, i, :]

        ybank = bank(6)[:, 0:PT].rearrange("p (u d) -> p u d", u=2)
        xtbank = bank(7)[:, 0:PT]
        lens_i = work[:, 0:B].bitcast(I32)
        mask_u8 = work[:, 1024:1024 + T // 4].bitcast(U8)
        tern_i = work[:, 64:64 + D].bitcast(I32)

        def row(name, n=2):
            i = ROWS.index(name)
            return rows[:, i:i + 1, :].to_broadcast([P, n, D])

        def pair(ap3, p):
            return ap3[:, bass.ds(2 * p, 2), :]

        def cols(ap2, p):
            return ap2[:, bass.ds(PT * p, PT)]

        weights_in = [sem(f"weights_in{i}") for i in range(5)]
        x_in_done = sem("x_in_done")
        ctx_in_done = sem("ctx_in_done")
        rest_in = sem("rest_in")
        consts_made = sem("consts_made")
        converted = sem("converted")
        banks_filled = sem("banks_filled")
        act_emptied = sem("act_emptied")
        dve_emptied = sem("dve_emptied")
        y_filled = sem("y_filled")
        xn_ready = sem("xn_ready")
        xt_filled = sem("xt_filled")
        xt_stored = sem("xt_stored")
        staged = sem("staged")
        inputs_used = sem("inputs_used")
        var_ready = sem("var_ready")
        rstd_ready = sem("rstd_ready")
        out_ready = sem("out_ready")
        out_stored = sem("out_stored")
        sems = {"a": act_emptied, "v": dve_emptied}

        def attn_units(n):
            u = []
            if n == 1:
                for t in range(2):
                    u += [(f"tok{t}{c}", "a") for c in range(4)]
            else:
                u += [(f"qk{c}", "av"[c % 2]) for c in range(8)]
            return u

        stages = []

        def stage(units):
            s = Stage(len(stages), units, stages[-1] if stages else None, sems)
            stages.append(s)
            return s

        first = stage([("none", "a")])
        first.units = []
        first.per = {"a": 0, "v": 0}
        lstm = stage([("gates", "a"), ("maxD", "a"), ("argD", "v"), ("qk", "v"), ("num", "a")])

        def moe_units(nu, nd, lag):
            u = [("route", "v"), ("up0", "a"), ("up1", "a")]
            ups, downs = list(range(2, nu)), list(range(nd))
            per = nu / nd
            done = 2
            for d in downs:
                need = min(nu, int(per * (d + 1) + 0.99) + lag)
                while done < need:
                    u.append((f"up{done}", "a"))
                    done += 1
                if d == nd - 1:
                    u.append(("combT", "v"))
                u.append((f"down{d}", "v"))
            return u

        moe0 = stage(moe_units(8, 4, 2))
        att1 = stage([(f"tok{t}{c}", "a") for t in range(2) for c in range(4)] + [(f"v{c}", "a") for c in range(4)]
                     + [(f"turn{t}{c}", "a") for t in range(2) for c in range(4)]
                     + [(f"s{t}{h}", "v") for t in range(2) for h in range(2)]
                     + [(f"{k}{t}{h}", "a") for t in range(2) for k in "po" for h in range(2)])
        moe1 = stage(moe_units(5, 5, 1))
        direct = ([(f"qk{c}", "av"[c % 2]) for c in range(8)] + [("s00", "v"), ("s01", "v")]
                  + [(f"v{c}", "a") for c in range(4)] + [("s10", "v"), ("s11", "v")]
                  + [(f"{k}{t}{h}", "a") for t in range(2) for k in "po" for h in range(2)])
        satt = stage(direct)
        catt = stage(direct)
        ffn2 = stage([("up0", "a"), ("up1", "a")])
        tern = stage([])
        att3 = stage([("qk", "a"), ("v", "v"), ("s00", "v"), ("s01", "v"), ("s10", "v"), ("s11", "v"),
                      ("p00", "a"), ("p01", "a"), ("o00", "v"), ("o01", "v"), ("p10", "a"), ("p11", "a"), ("o10", "v"),
                      ("o11", "v"), ("oT", "a")])
        hid3 = stage([("up0", "a"), ("up1", "a")])
        out3 = stage([])

        plan = {0: [], 1: [lstm], 2: [moe0], 3: [att1], 4: [moe1], 5: [satt, catt, ffn2], 6: [tern], 7: [att3],
                8: [hid3, out3]}
        run = [s for k in range(layers + 1) for s in plan[k]]
        weight_group = {lstm: 0, moe0: 1, att1: 2, moe1: 3}

        class Handoff:
            def __init__(self, name, n):
                self.sem, self.n = sem(name), n

            def at(self, p, k):
                return self.sem, p * self.n + k

        def norm_rows(v, src, dst, value):
            for u in range(2):
                v.bn_stats(st[:, u, :], src[:, u, :])
            v.drain()
            for u in range(2):
                v.bn_aggr(mv[:, u, :], st[:, u, :])
            v.drain()
            v.tensor_scalar(var[:], mv[:, :, 1], 1e-5, None, ALU.add).then_inc(var_ready, 1)
            v.wait_ge(rstd_ready, value)
            for u in range(2):
                ins = v.tensor_scalar(dst[:, u, :], src[:, u, :], mv[:, u, 0:1], rstd[:, u:u + 1],
                                      ALU.subtract, ALU.mult)
            return ins

        roots = {}
        count = 0
        for s in [first] + run:
            per = {ffn2: 2, lstm: 1}.get(s, 1)
            if s in (hid3, out3):
                per = 0
            roots[s] = (count, per)
            count += per * PAIRS

        def root(s, p, k):
            return p * roots[s][1] + (roots[s][0] + k)

        def take_root(g, s, p, k):
            g.wait_ge(var_ready, root(s, p, k))
            g.tensor_tensor(rstd[:], var[:], nhalf[:, 0:2], ALU.pow).then_inc(rstd_ready, 1)

        def store_normed(v, s, p):
            pass

        def turn_normed(pe, g):
            pe.wait_ge(xn_ready, g)
            pe.wait_ge(xt_stored, g)
            for u in range(2):
                ins = pe.transpose(xtbank[:, u * P:(u + 1) * P], xn[:, u, :], ident[:])
            ins.then_inc(xt_filled, 1)

        settled = sem("settled")

        def settle(pe):
            pe.sem_inc(settled, 1)

        def store_turned(act, g, p):
            act.wait_ge(xt_filled, g + BUMP)
            act.activation(cols(xT_all, p), xtbank, ACT.Copy).then_inc(xt_stored, 1)

        def g_of(s, p):
            return p + PAIRS * stages_run.index(s)

        stages_run = [first] + run

        def prev_pair(p):
            return p + (PAIRS - 1) if isinstance(p, int) else p + (PAIRS - 1)

        def before(eng, p):
            return eng.snap((p + (PAIRS - 1)) & (PAIRS - 1))

        def first_vector(v):
            v.wait_ge(x_in_done, 16)
            with v.Fori(0, PAIRS) as p:
                v.drain()
                v.tensor_copy(xr[:], pair(x_all, p))
                v.drain()
                v.wait_ge(xt_filled, p + BUMP)
                norm_rows(v, xr, xn, root(first, p, 1)).then_inc(xn_ready, 1)

        lstm_z = work[:, 0:256]
        lstm_e = work[:, 256:512]
        lstm_ig = work[:, 512:768]
        lstm_lf = work[:, 768:1024]
        lstm_cs = work[:, 1024:1280]
        lstm_g = work[:, 1280:1536]
        lstm_G = work[:, 1536:1792]
        lstm_m = work[:, 1792:2048]
        lstm_L = work[:, 2048:2304]
        lstm_R = work[:, 5120:6144].rearrange("p (h t) -> p h t", h=4)
        lstm_q = work[:, 6144:7168].rearrange("p (h t) -> p h t", h=4)
        lstm_D = work[:, 2560:3072]
        lstm_C = work[:, 3072:3584]
        lstm_v = work[:, 3584:3584 + 264].rearrange("p (u h e) -> p u h e", u=2, h=4)
        lstm_h = work[:, 4096:4096 + 264].rearrange("p (u h e) -> p (u h) e", u=2, h=4)
        lstm_n = work[:, 4608:4864].rearrange("p (g e) -> p g e", g=8)
        lstm_n2 = work[:, 4864:5120].rearrange("p (g e) -> p g e", g=8)
        lstm_hv = small[:, 0:8]
        lstm_hr = small[:, 8:16]
        lstm_hm = small[:, 16:24]
        lstm_hs = small[:, 24:32]
        lstm_hq = small[:, 32:40]
        lstm_em = small[:, 40:48]
        h_lstm = {}

        def lstm_tensor(pe):
            s = lstm
            gw = w("gates").rearrange("p (k n) -> p k n", k=6)
            pe.wait_ge(weights_in[0], 16)
            with pe.Fori(0, PAIRS) as p:
                g = g_of(s, p)
                pe.wait_ge(*s.bank_free(p, "gates"))
                pe.wait_ge(staged, g + 1 - PAIRS)
                bk = bank(s.bank("gates"))
                for gate in range(2):
                    for k in range(3):
                        ins = pe.matmul(bk[:, gate * PT:(gate + 1) * PT], gw[:, 3 * gate + k, :],
                                        xs[:] if k == 0 else cs[:], start=(k == 0), stop=(k == 2))
                ins.then_inc(banks_filled, 1)
                turn_normed(pe, g)
                pe.wait_ge(*h_lstm["rows"].at(p, 1))
                pe.wait_ge(*s.bank_free(p, "maxD"))
                for u in range(2):
                    ins = pe.transpose(bank(s.bank("maxD"))[:, u * P:(u + 1) * P], lstm_m[:, u * P:(u + 1) * P],
                                       ident[:])
                ins.then_inc(banks_filled, 1)
                for name, lhs, rhs in (("argD", lstm_L, lstm_R), ("qk", cs, lstm_q)):
                    pe.wait_ge(*s.bank_free(p, name))
                    bk = bank(s.bank(name))
                    for u in range(2):
                        for b in range(2):
                            c = (2 * u + b) * S
                            ins = pe.matmul(bk[b * S:(b + 1) * S, u * 256:(u + 1) * 256], lhs[:, c:c + S],
                                            rhs[:, :, c:c + S], start=True, stop=True)
                    ins.then_inc(banks_filled, 1)
                pe.wait_ge(*s.emptied(p, "qk"))
                pe.wait_ge(*s.bank_free(p, "num"))
                settle(pe)
                bk = bank(s.bank("num"))
                for u in range(2):
                    for h in range(4):
                        for b in range(2):
                            ins = pe.matmul(bk[b * S:(b + 1) * S, (u * 4 + h) * 33:(u * 4 + h + 1) * 33],
                                            lstm_C[b * S:(b + 1) * S, (u * 4 + h) * S:(u * 4 + h + 1) * S],
                                            lstm_v[b * S:(b + 1) * S, u, h, :], start=True, stop=True)
                ins.then_inc(banks_filled, 1)
                pe.drain().then_inc(inputs_used, 1)

        def lstm_scalar(act):
            s = lstm
            act.wait_ge(weights_in[0], 16)
            with act.Fori(0, PAIRS) as p:
                g = g_of(s, p)
                act.wait_ge(banks_filled, s.filled(p, "gates"))
                bk = bank(s.bank("gates"))
                act.activation(lstm_ig, bk[:, 0:PT], ACT.Identity, bias=w("gate_bias")[:, 0:1])
                act.activation(lstm_z, bk[:, PT:2 * PT], ACT.Identity,
                               bias=w("gate_bias")[:, 1:2]).then_inc(act_emptied, 1)
                act.wait_ge(*h_lstm["abs"].at(p, 1))
                act.activation(lstm_e, lstm_e, ACT.Exp, scale=-1.0)
                act.drain()
                act.activation(lstm_e, lstm_e, ACT.Ln, bias=1.0).then_inc(h_lstm["ln"].sem, 1)
                store_turned(act, g, before(act, p))
                act.wait_ge(banks_filled, s.filled(p, "maxD"))
                m8 = bank(s.bank("maxD"))[:, 0:PT].rearrange("p (u h r) -> p u h r", u=2, h=4)
                act.activation(lstm_em.rearrange("p (u h) -> p u h", u=2), m8[:, :, :, 0], ACT.Exp,
                               scale=-1.0).then_inc(act_emptied, 1)
                act.wait_ge(*s.emptied(p, "argD"))
                act.activation(lstm_D, lstm_D, ACT.Exp).then_inc(h_lstm["D"].sem, 1)
                act.wait_ge(banks_filled, s.filled(p, "num"))
                act.activation(lstm_h, bank(s.bank("num"))[:, 0:264].rearrange("p (g e) -> p g e", e=33),
                               ACT.Copy).then_inc(act_emptied, 1)

        def lstm_vector(v):
            s = lstm
            with v.Fori(0, PAIRS) as p:
                v.drain()
                g = g_of(s, p)
                v.wait_ge(*s.emptied(p, "gates"))
                v.scalar_tensor_tensor(out=lstm_e, in0=lstm_z, scalar=-1.0, in1=lstm_z, op0=ALU.mult,
                                       op1=ALU.max).then_inc(h_lstm["abs"].sem, 1)
                v.wait_ge(*h_lstm["ln"].at(p, 1))
                v.scalar_tensor_tensor(out=lstm_lf, in0=lstm_z, scalar=0.0, in1=lstm_e, op0=ALU.min,
                                       op1=ALU.subtract)
                v.drain()
                v.tensor_tensor_scan(lstm_cs, restart[:], lstm_lf, 0.0, ALU.mult, ALU.add)
                v.drain()
                v.tensor_tensor(lstm_g, lstm_lf, lstm_cs, ALU.subtract)
                v.drain()
                v.tensor_tensor(lstm_g, lstm_g, lstm_ig, ALU.add)
                v.drain()
                v.tensor_tensor_scan(lstm_G, restart_neg[:], lstm_g, -NEG, ALU.add, ALU.max)
                v.drain()
                v.tensor_scalar(lstm_L, lstm_g, row1[:], row2[:], ALU.mult, ALU.add)
                v.tensor_tensor(lstm_m, lstm_cs, lstm_G, ALU.add)
                for h in range(4):
                    ins = v.tensor_scalar(lstm_R[:, h, :], lstm_G, negrow2[:, h:h + 1], row1h[:, h:h + 1],
                                          ALU.mult, ALU.add)
                ins.then_inc(h_lstm["rows"].sem, 1)
                v.wait_ge(banks_filled, s.filled(p, "argD"))
                v.tensor_tensor(lstm_D.rearrange("p (g k) -> p g k", g=8),
                                bank(s.bank("argD")).rearrange("p (g k) -> p g k", g=8),
                                causal[:, None, :].to_broadcast([P, 8, S]), ALU.add).then_inc(dve_emptied, 1)
                v.wait_ge(*h_lstm["D"].at(p, 1))
                v.wait_ge(banks_filled, s.filled(p, "qk"))
                v.scalar_tensor_tensor(out=lstm_C, in0=bank(s.bank("qk")), scalar=32.0 ** -0.5, in1=lstm_D,
                                       op0=ALU.mult, op1=ALU.mult).then_inc(dve_emptied, 1)
                v.wait_ge(*s.emptied(p, "num"))
                v.scalar_tensor_tensor(out=lstm_hv, in0=lstm_h[:, :, 32], scalar=-1.0, in1=lstm_h[:, :, 32],
                                       op0=ALU.mult, op1=ALU.max)
                v.drain()
                v.tensor_tensor(lstm_hv, lstm_hv, lstm_em, ALU.max)
                v.drain()
                v.tensor_scalar(lstm_hv, lstm_hv, 1e-8, None, ALU.add)
                v.drain()
                v.reciprocal(lstm_hr, lstm_hv)
                v.drain()
                v.tensor_tensor(lstm_n, lstm_h[:, :, 0:32], lstm_hr[:, :, None].to_broadcast([P, 8, 32]), ALU.mult)
                v.drain()
                v.reduce_sum(lstm_hm, lstm_n, AX)
                v.drain()
                v.tensor_scalar(lstm_hm, lstm_hm, 1.0 / 32, None, ALU.mult)
                v.drain()
                v.tensor_tensor(lstm_n, lstm_n, lstm_hm[:, :, None].to_broadcast([P, 8, 32]), ALU.subtract)
                v.drain()
                v.tensor_tensor(lstm_n2, lstm_n, lstm_n, ALU.mult)
                v.drain()
                v.reduce_sum(lstm_hs, lstm_n2, AX)
                v.drain()
                v.tensor_scalar(lstm_hs, lstm_hs, 1.0 / 32, 1e-5, ALU.mult, ALU.add).then_inc(h_lstm["hvar"].sem, 1)
                v.wait_ge(*h_lstm["hroot"].at(p, 1))
                v.tensor_tensor(lstm_n, lstm_n, lstm_hq[:, :, None].to_broadcast([P, 8, 32]), ALU.mult)
                v.tensor_scalar(lstm_n2.rearrange("p (u h) e -> p u (h e)", u=2), row("out_w"), 1.0, None, ALU.add)
                v.drain()
                v.tensor_tensor(lstm_n, lstm_n, lstm_n2, ALU.mult)
                v.drain()
                v.tensor_tensor(xr[:], lstm_n.rearrange("p (u h) e -> p u (h e)", u=2), pair(x_all, p), ALU.add)
                finish(v, s, p, g)

        def finish(v, s, p, g):
            v.drain()
            v.tensor_copy(pair(x_all, p), xr[:])
            v.wait_ge(xt_filled, g + BUMP)
            norm_rows(v, xr, xn, root(s, p, roots[s][1])).then_inc(xn_ready, 1)

        lg = small[:, 0:16].rearrange("p (u e) -> p u e", u=2)
        mx8 = small[:, 16:32].rearrange("p (u e) -> p u e", u=2)
        ds8 = small[:, 32:48].rearrange("p (u e) -> p u e", u=2)
        es8 = small[:, 48:64].rearrange("p (u e) -> p u e", u=2)
        idxf = small[:, 64:68].rearrange("p (u e) -> p u e", u=2)
        tsum = small[:, 68:70]
        wtop = small[:, 70:74].rearrange("p (u e) -> p u e", u=2)
        comb = small[:, 80:98].rearrange("p (u e) -> p u e", u=2)
        comb2 = small[:, 100:116].rearrange("p (u e) -> p u e", u=2)
        combT = small[:, 128:384]
        hT = work[:, 0:4096].rearrange("p (c t) -> p c t", t=PT)
        prod = work[:, 4096:4096 + 2304]

        def moe(tag, s, pre, experts, chunks, func, layer):
            nch = experts * chunks
            ups = [n for n in s.names if n.startswith("up")]
            downs = [n for n in s.names if n.startswith("down")]
            per_down = 2
            pr = prod[:, 0:2 * experts * D].rearrange("p (u e d) -> p u e d", u=2, e=experts)
            asked = Handoff(f"{tag}_exp_asked", 1)
            given = Handoff(f"{tag}_exp_given", 1)
            comb_ready = Handoff(f"{tag}_comb_ready", 1)
            upw = w(pre + "_up").rearrange("p (c f) -> p c f", f=P)
            dnw = w(pre + "_down").rearrange("p (c f) -> p c f", f=D)

            def tensor(pe):
                pe.wait_ge(weights_in[weight_group[s]], 16)
                with pe.Fori(0, PAIRS) as p:
                    g = g_of(s, p)
                    pe.wait_ge(staged, g + 1 - PAIRS)
                    for n, name in enumerate(s.names):
                        if name == "combT":
                            pe.wait_ge(*comb_ready.at(p, 1))
                        pe.wait_ge(*s.bank_free(p, name))
                        bk = bank(s.bank(name))
                        if name == "route":
                            for u in range(2):
                                ins = pe.matmul(bk[:, 8 * u:8 * u + 8], xs[:, u * P:(u + 1) * P], w(pre + "_router"),
                                                start=True, stop=True)
                        elif name == "combT":
                            for u in range(2):
                                ins = pe.transpose(bk[0:experts, u * P:(u + 1) * P], comb[:, u, 0:experts], ident[:])
                        elif name.startswith("up"):
                            j = int(name[2:])
                            for c in range(2 * j, min(2 * j + 2, nch)):
                                ins = pe.matmul(bk[:, (c % 2) * PT:(c % 2 + 1) * PT], upw[:, c, :], xs[:],
                                                start=True, stop=True)
                        else:
                            j = int(name[4:])
                            last = min((j + 1) * per_down * chunks, nch) - 1
                            settle(pe)
                            pe.wait_ge(*s.emptied(p, f"up{last // 2}"))
                            for u in range(2):
                                for e in range(2 * j, min(2 * j + 2, experts)):
                                    for c in range(chunks):
                                        ins = pe.matmul(bk[:, (2 * u + e % 2) * D:(2 * u + e % 2 + 1) * D],
                                                        hT[:, e * chunks + c, u * P:(u + 1) * P],
                                                        dnw[:, e * chunks + c, :], start=(c == 0),
                                                        stop=(c == chunks - 1))
                        ins.then_inc(banks_filled, 1)
                        if name == "up1":
                            turn_normed(pe, g)
                    pe.drain().then_inc(inputs_used, 1)
                    pe.wait_ge(*s.emptied(p, "combT"))
                    for u in range(2):
                        ins = pe.matmul(ybank[:, u, :], combT[0:experts, u * P:(u + 1) * P],
                                        moeb[0:experts, layer, :], start=True, stop=True)
                    ins.then_inc(y_filled, 1)

            def scalar(act):
                with act.Fori(0, PAIRS) as p:
                    for name in ups:
                        j = int(name[2:])
                        act.wait_ge(banks_filled, s.filled(p, name))
                        for c in range(2 * j, min(2 * j + 2, nch)):
                            ins = act.activation(hT[:, c, :], bank(s.bank(name))[:, (c % 2) * PT:(c % 2 + 1) * PT],
                                                 func, bias=w(pre + "_upb")[:, c:c + 1])
                        ins.then_inc(act_emptied, 1)
                        if j == 1:
                            store_turned(act, g_of(s, p), before(act, p))

            def vector(v):
                if experts == 9:
                    v.memset(comb[:, :, 8:9], 1.0)
                with v.Fori(0, PAIRS) as p:
                    v.drain()
                    v.wait_ge(banks_filled, s.filled(p, "route"))
                    v.tensor_copy(lg, bank(s.bank("route"))[:, 0:16].rearrange("p (u e) -> p u e", u=2)) \
                        .then_inc(dve_emptied, 1)
                    v.drain()
                    for u in range(2):
                        v.max(mx8[:, u, :], lg[:, u, :])
                    v.drain()
                    v.tensor_tensor(ds8, mx8, mx8[:, :, 0:1].to_broadcast([P, 2, 8]), ALU.subtract) \
                        .then_inc(asked.sem, 1)
                    for u in range(2):
                        v.max_index(ix[:, u, :], mx8[:, u, :], lg[:, u, :])
                    v.drain()
                    v.tensor_copy(idxf, ix[:, :, 0:2])
                    v.wait_ge(*given.at(p, 1))
                    if experts == 9:
                        v.reduce_sum(tsum, es8, AX)
                        v.drain()
                        v.reciprocal(tsum, tsum)
                        v.drain()
                        v.tensor_tensor(wtop, es8[:, :, 0:2], tsum[:, :, None].to_broadcast([P, 2, 2]), ALU.mult)
                        v.drain()
                        v.tensor_tensor(tsum, wtop[:, :, 0], wtop[:, :, 1], ALU.add)
                        v.drain()
                        v.tensor_scalar(tsum, tsum, 1e-20, None, ALU.add)
                        top = wtop
                    else:
                        v.tensor_tensor(tsum, es8[:, :, 0], es8[:, :, 1], ALU.add)
                        top = es8[:, :, 0:2]
                    v.drain()
                    v.reciprocal(tsum, tsum)
                    v.drain()
                    v.tensor_tensor(wtop, top, tsum[:, :, None].to_broadcast([P, 2, 2]), ALU.mult)
                    v.drain()
                    for u in range(2):
                        v.tensor_scalar(comb[:, u, 0:8], iota8[:, 0:8], idxf[:, u, 0:1], wtop[:, u, 0:1],
                                        ALU.is_equal, ALU.mult)
                        v.tensor_scalar(comb2[:, u, :], iota8[:, 0:8], idxf[:, u, 1:2], wtop[:, u, 1:2],
                                        ALU.is_equal, ALU.mult)
                    v.drain()
                    v.tensor_tensor(comb[:, :, 0:8], comb[:, :, 0:8], comb2, ALU.add).then_inc(comb_ready.sem, 1)
                    v.drain()
                    for name in s.names[1:]:
                        if name.startswith("up"):
                            continue
                        v.wait_ge(banks_filled, s.filled(p, name))
                        if name == "combT":
                            v.tensor_copy(combT[0:experts, :], bank(s.bank(name))[0:experts, 0:PT]) \
                                .then_inc(dve_emptied, 1)
                            continue
                        j = int(name[4:])
                        n = min(2 * j + 2, experts) - 2 * j
                        bk = bank(s.bank(name)).rearrange("p (u e d) -> p u e d", u=2, e=2)
                        for u in range(2):
                            ins = v.tensor_tensor(pr[:, u, 2 * j:2 * j + n, :], bk[:, u, 0:n, :],
                                                  comb[:, u, 2 * j:2 * j + n, None].to_broadcast([P, n, D]), ALU.mult)
                        ins.then_inc(dve_emptied, 1)
                    v.drain()
                    for u in range(2):
                        v.reduce_sum(xr[:, u, :], pr[:, u, :, :].rearrange("p e d -> p d e"), AX)
                    v.drain()
                    v.tensor_tensor(xr[:], xr[:], pair(x_all, p), ALU.add)
                    v.drain()
                    v.wait_ge(y_filled, p + yb(s))
                    v.tensor_tensor(xr[:], ybank, xr[:], ALU.add)
                    if layer == 1:
                        finish(v, s, p, g_of(s, p))
                        v.drain()
                        v.tensor_copy(pair(tok_all, p), xn[:])
                    else:
                        finish(v, s, p, g_of(s, p))

            def pool(g, p):
                g.wait_ge(*asked.at(p, 1))
                g.tensor_tensor(es8, euler[:].rearrange("p (u e) -> p u e", u=2), ds8, ALU.pow).then_inc(given.sem, 1)

            return tensor, scalar, vector, pool

        ystages = [s for s in run if s is not lstm and s is not hid3]

        def yb(s):
            return ystages.index(s) * PAIRS + 1

        qT = work[:, 0:2048].rearrange("p (c t) -> p c t", t=PT)
        kT = work[:, 2048:4096].rearrange("p (c t) -> p c t", t=PT)
        vv = work[:, 4096:6144].rearrange("p (u n) -> p u n", u=2)
        sm = work[:, 6144:8192].rearrange("p (u n) -> p u n", u=2)
        pT = work[:, 8192:10240].rearrange("p (u c t) -> p u c t", u=2, c=8)
        oT = work[:, 10240:12288].rearrange("p (u c t) -> p u c t", u=2, c=8)
        mxs = small[:, 0:32].rearrange("p (u g) -> p u g", u=2)
        rs = small[:, 32:64].rearrange("p (u g) -> p u g", u=2)
        ssq = small[:, 64:128].rearrange("p (u g) -> p u g", u=2)
        rsq = small[:, 128:192].rearrange("p (u g) -> p u g", u=2)

        def soft_in(v, s, p, u, masked, h):
            for half in range(2):
                name = f"s{u}{half}"
                v.wait_ge(banks_filled, s.filled(p, name))
                bk = bank(s.bank(name)).rearrange("p (g k) -> p g k", k=S)
                dst = sm[:, u, 512 * half:512 * half + 512].rearrange("p (g k) -> p g k", k=S)
                mx = mxs[:, u, 8 * half:8 * half + 8]
                if masked:
                    v.tensor_tensor(dst.rearrange("p (c b) k -> p c (b k)", b=2),
                                    bank(s.bank(name)).rearrange("p (c k) -> p c k", k=P),
                                    negm[:, None, u * P:(u + 1) * P].to_broadcast([P, 4, P]), ALU.add) \
                        .then_inc(dve_emptied, 1)
                    v.drain()
                    src = dst
                else:
                    src = bk
                v.reduce_max(mx, src, AX)
                v.drain()
                ins = v.tensor_tensor(dst, src, mx[:, :, None].to_broadcast([P, 8, S]), ALU.subtract)
                if masked:
                    ins.then_inc(h["arg"].sem, 1)
                else:
                    ins.then_inc(dve_emptied, 1)

        def soft_exp(act, s, p, u, half, scale, h, masked):
            if masked:
                act.wait_ge(*h["arg"].at(p, 2 * u + half + 1))
            else:
                act.wait_ge(*s.emptied(p, f"s{u}{half}"))
            part = sm[:, u, 512 * half:512 * half + 512]
            act.activation(part, part, ACT.Exp, scale=scale).then_inc(h["exp"].sem, 1)

        def soft_out(v, p, u, h):
            for half in range(2):
                part = sm[:, u, 512 * half:512 * half + 512].rearrange("p (g k) -> p g k", k=S)
                r = rs[:, u, 8 * half:8 * half + 8]
                v.wait_ge(*h["exp"].at(p, 2 * u + half + 1))
                v.reduce_sum(r, part, AX)
                v.drain()
                v.reciprocal(r, r)
                v.drain()
                v.tensor_tensor(part, part, r[:, :, None].to_broadcast([P, 8, S]), ALU.mult).then_inc(h["prob"].sem, 1)

        def probs_turned(pe, s, p, u, h):
            for half in range(2):
                name = f"p{u}{half}"
                pe.wait_ge(*h["prob"].at(p, 2 * u + half + 1))
                pe.wait_ge(*s.bank_free(p, name))
                for c in range(4):
                    ins = pe.transpose(bank(s.bank(name))[:, c * P:(c + 1) * P],
                                       sm[:, u, 512 * half + c * P:512 * half + (c + 1) * P], ident[:])
                ins.then_inc(banks_filled, 1)

        def store_probs(act, s, p, u):
            for half in range(2):
                act.wait_ge(banks_filled, s.filled(p, f"p{u}{half}"))
                act.activation(pT[:, u, 4 * half:4 * half + 4, :].rearrange("p c t -> p (c t)"),
                               bank(s.bank(f"p{u}{half}")), ACT.Copy).then_inc(act_emptied, 1)

        def attention(tag, s, wq, wk, wv, wo, normed, group, end):
            h = {k: Handoff(f"{tag}_{k}", 4) for k in ("arg", "exp", "prob")}
            if normed:
                h["sq"] = Handoff(f"{tag}_squares", 2)
                h["var"] = Handoff(f"{tag}_variances", 2)
                h["root"] = Handoff(f"{tag}_roots", 2)
                h["scaled"] = Handoff(f"{tag}_scaled", 2)
            wq, wk, wv = (w(n).rearrange("p (c f) -> p c f", f=P) for n in (wq, wk, wv))
            wo = w(wo).rearrange("p (c f) -> p c f", f=D)
            scale = 64.0 ** -0.5
            tok = {(0, u): sm[:, u, :] for u in range(2)}
            tok.update({(1, u): pT[:, u, :, :].rearrange("p c t -> p (c t)") for u in range(2)})
            squares = {(k, u): oT[:, u, :, :].rearrange("p c t -> p (c t)")[:, 0:1024] for u in range(2) for k in range(2)}

            def scores(pe, p, u):
                for half in range(2):
                    name = f"s{u}{half}"
                    pe.wait_ge(*s.bank_free(p, name))
                    settle(pe)
                    bk = bank(s.bank(name))
                    for c in range(4):
                        hp = 4 * half + c
                        for b in range(2):
                            for par in range(2):
                                r0, t0 = par * S, (2 * u + b) * S
                                ins = pe.matmul(bk[r0:r0 + S, (2 * c + b) * S:(2 * c + b + 1) * S],
                                                qT[r0:r0 + S, hp, t0:t0 + S], kT[r0:r0 + S, hp, t0:t0 + S],
                                                start=True, stop=True)
                    ins.then_inc(banks_filled, 1)

            def values(pe, p):
                for c in range(4):
                    u, n = c // 2, c % 2
                    pe.wait_ge(*s.bank_free(p, f"v{c}"))
                    pe.matmul(bank(s.bank(f"v{c}")), vsrc[:, u * P:(u + 1) * P],
                              wv[:, 4 * n:4 * n + 4, :].rearrange("p c f -> p (c f)"), start=True, stop=True) \
                        .then_inc(banks_filled, 1)
                pe.drain().then_inc(inputs_used, 1)

            vsrc = xs if tag == "sa" else cs

            def mix(pe, p, u):
                probs_turned(pe, s, p, u, h)
                for b in range(2):
                    name = f"o{u}{b}"
                    pe.wait_ge(*s.bank_free(p, name))
                    settle(pe)
                    pe.wait_ge(*s.emptied(p, f"p{u}1"))
                    settle(pe)
                    bk = bank(s.bank(name))
                    for hp in range(8):
                        for par in range(2):
                            ins = pe.matmul(bk[par * S:(par + 1) * S, hp * S:(hp + 1) * S],
                                            vv[b * S:(b + 1) * S, u, (2 * hp + par) * S:(2 * hp + par + 1) * S],
                                            pT[b * S:(b + 1) * S, u, hp, par * S:(par + 1) * S],
                                            start=True, stop=True)
                    ins.then_inc(banks_filled, 1)

            def tensor(pe):
                pe.wait_ge(weights_in[group], 16)
                with pe.Fori(0, PAIRS) as p:
                    g = g_of(s, p)
                    pe.wait_ge(staged, g + 1 - PAIRS)
                    if normed:
                        for u in range(2):
                            for c in range(4):
                                name = f"tok{u}{c}"
                                src, wt = (xs, wq) if c < 2 else (ks, wk)
                                pe.wait_ge(*s.bank_free(p, name))
                                pe.matmul(bank(s.bank(name)), src[:, u * P:(u + 1) * P],
                                          wt[:, 4 * (c % 2):4 * (c % 2) + 4, :].rearrange("p c f -> p (c f)"),
                                          start=True, stop=True).then_inc(banks_filled, 1)
                        turn_normed(pe, g)
                        values(pe, p)
                        for u in range(2):
                            pe.wait_ge(*h["scaled"].at(p, u + 1))
                            for c in range(4):
                                name = f"turn{u}{c}"
                                pe.wait_ge(*s.bank_free(p, name))
                                for i in range(4):
                                    a = (4 * (c % 2) + i) * P
                                    ins = pe.transpose(bank(s.bank(name))[:, i * P:(i + 1) * P],
                                                       tok[(c // 2, u)][:, a:a + P], ident[:])
                                ins.then_inc(banks_filled, 1)
                        pe.wait_ge(*s.emptied(p, "turn13"))
                        settle(pe)
                        scores(pe, p, 0)
                        scores(pe, p, 1)
                    else:
                        for c in range(8):
                            pe.wait_ge(*s.bank_free(p, f"qk{c}"))
                            wt, src = (wq, xs) if c < 4 else (wk, ks)
                            for i in range(2):
                                ins = pe.matmul(bank(s.bank(f"qk{c}"))[:, i * PT:(i + 1) * PT],
                                                wt[:, 2 * (c % 4) + i, :], src[:], start=True, stop=True)
                            ins.then_inc(banks_filled, 1)
                        turn_normed(pe, g)
                        pe.wait_ge(*s.emptied(p, "qk6"))
                        pe.wait_ge(*s.emptied(p, "qk7"))
                        settle(pe)
                        scores(pe, p, 0)
                        values(pe, p)
                        scores(pe, p, 1)
                    mix(pe, p, 0)
                    mix(pe, p, 1)
                    for u in range(2):
                        pe.wait_ge(*s.emptied(p, f"o{u}1"))
                        for c in range(8):
                            ins = pe.matmul(ybank[:, u, :], oT[:, u, c, :], wo[:, c, :], start=(c == 0), stop=(c == 7))
                    ins.then_inc(y_filled, 1)

            def scalar(act):
                with act.Fori(0, PAIRS) as p:
                    g = g_of(s, p)
                    if normed:
                        for u in range(2):
                            for c in range(4):
                                name = f"tok{u}{c}"
                                act.wait_ge(banks_filled, s.filled(p, name))
                                act.activation(tok[(c // 2, u)][:, 512 * (c % 2):512 * (c % 2) + 512],
                                               bank(s.bank(name)), ACT.Copy).then_inc(act_emptied, 1)
                        store_turned(act, g, before(act, p))
                    else:
                        for c in range(0, 8, 2):
                            act.wait_ge(banks_filled, s.filled(p, f"qk{c}"))
                            dst = (qT if c < 4 else kT)[:, 2 * (c % 4):2 * (c % 4) + 2, :]
                            act.activation(dst.rearrange("p c t -> p (c t)"), bank(s.bank(f"qk{c}")), ACT.Copy) \
                                .then_inc(act_emptied, 1)
                        store_turned(act, g, before(act, p))

                    def value(c):
                        act.wait_ge(banks_filled, s.filled(p, f"v{c}"))
                        act.activation(vv[:, c // 2, 512 * (c % 2):512 * (c % 2) + 512], bank(s.bank(f"v{c}")),
                                       ACT.Copy).then_inc(act_emptied, 1)

                    def mixed(u):
                        for b in range(2):
                            act.wait_ge(banks_filled, s.filled(p, f"o{u}{b}"))
                            act.activation(oT[:, u, :, b * S:(b + 1) * S],
                                           bank(s.bank(f"o{u}{b}")).rearrange("p (c q) -> p c q", q=S),
                                           ACT.Copy).then_inc(act_emptied, 1)

                    if normed:
                        for c in range(4):
                            value(c)
                        for u in range(2):
                            for c in range(4):
                                name = f"turn{u}{c}"
                                act.wait_ge(banks_filled, s.filled(p, name))
                                dst = (qT if c < 2 else kT)[:, 4 * (c % 2):4 * (c % 2) + 4, u * P:(u + 1) * P]
                                act.activation(dst, bank(s.bank(name)).rearrange("p (c t) -> p c t", t=P), ACT.Copy,
                                               scale=w("a1_norm")[:, c // 2:c // 2 + 1]).then_inc(act_emptied, 1)
                        soft_exp(act, s, p, 0, 0, scale, h, True)
                        soft_exp(act, s, p, 0, 1, scale, h, True)
                    else:
                        value(0)
                        value(1)
                        soft_exp(act, s, p, 0, 0, scale, h, True)
                        value(2)
                        soft_exp(act, s, p, 0, 1, scale, h, True)
                        value(3)
                    store_probs(act, s, p, 0)
                    soft_exp(act, s, p, 1, 0, scale, h, True)
                    soft_exp(act, s, p, 1, 1, scale, h, True)
                    mixed(0)
                    store_probs(act, s, p, 1)
                    mixed(1)

            def vector(v):
                with v.Fori(0, PAIRS) as p:
                    v.drain()
                    if normed:
                        for u in range(2):
                            v.wait_ge(*h["sq"].at(p, u + 1))
                            for k in range(2):
                                v.reduce_sum(ssq[:, u, 16 * k:16 * k + 16],
                                             squares2(u, k).rearrange("p (g e) -> p g e", e=64), AX)
                            v.drain()
                            v.tensor_scalar(ssq[:, u, :], ssq[:, u, :], 1.0 / 64, 1e-5, ALU.mult, ALU.add) \
                                .then_inc(h["var"].sem, 1)
                            v.wait_ge(*h["root"].at(p, u + 1))
                            for k in range(2):
                                t3 = tok[(k, u)].rearrange("p (g e) -> p g e", e=64)
                                ins = v.tensor_tensor(t3, t3, rsq[:, u, 16 * k:16 * k + 16, None].to_broadcast(
                                    [P, 16, 64]), ALU.mult)
                            ins.then_inc(h["scaled"].sem, 1)
                        soft_in(v, s, p, 0, True, h)
                        soft_in(v, s, p, 1, True, h)
                        v.drain().then_inc(mask_used, 1)
                        soft_out(v, p, 0, h)
                        soft_out(v, p, 1, h)
                    else:
                        for c in range(1, 8, 2):
                            v.wait_ge(banks_filled, s.filled(p, f"qk{c}"))
                            dst = (qT if c < 4 else kT)[:, 2 * (c % 4):2 * (c % 4) + 2, :]
                            v.tensor_copy(dst.rearrange("p c t -> p (c t)"), bank(s.bank(f"qk{c}"))) \
                                .then_inc(dve_emptied, 1)
                        soft_in(v, s, p, 0, True, h)
                        soft_out(v, p, 0, h)
                        soft_in(v, s, p, 1, True, h)
                        v.drain().then_inc(mask_used, 1)
                        soft_out(v, p, 1, h)
                    v.wait_ge(y_filled, p + yb(s))
                    end(v, s, p)

            def squares2(u, k):
                return oT[:, k, :, :].rearrange("p c t -> p (c t)")

            def pool(g, p):
                if normed:
                    for u in range(2):
                        g.wait_ge(*s.emptied(p, f"tok{u}3"))
                        for k in range(2):
                            if k == 0 and u == 1:
                                g.wait_ge(*h["scaled"].at(p, 1))
                            ins = g.tensor_tensor(squares2(u, k), tok[(k, u)], tok[(k, u)], ALU.mult)
                        ins.then_inc(h["sq"].sem, 1)
                        g.wait_ge(*h["var"].at(p, u + 1))
                        g.tensor_tensor(rsq[:, u, :], ssq[:, u, :], nhalf[:], ALU.pow).then_inc(h["root"].sem, 1)

            return tensor, scalar, vector, pool

        def end_residual(v, s, p):
            v.tensor_tensor(xr[:], ybank, pair(x_all, p), ALU.add)
            finish(v, s, p, g_of(s, p))

        def end_decoder(gain, shift, bias):
            def end(v, s, p):
                v.tensor_tensor(xr[:], ybank, pair(tok_all, p), ALU.add)
                v.drain()
                v.tensor_tensor(xr[:], xr[:], row(bias), ALU.add)
                v.drain()
                v.wait_ge(xt_filled, g_of(s, p) + BUMP)
                norm_rows(v, xr, xn, root(s, p, 1))
                v.drain()
                v.tensor_tensor(xn[:], xn[:], row(gain), ALU.mult)
                v.drain()
                v.tensor_tensor(xn[:], xn[:], row(shift), ALU.add)
                v.drain()
                v.tensor_copy(pair(tok_all, p), xn[:]).then_inc(xn_ready, 1)
            return end

        def ffn_tensor(pe):
            s = ffn2
            with pe.Fori(0, PAIRS) as p:
                g = g_of(s, p)
                pe.wait_ge(staged, g + 1 - PAIRS)
                up_product(pe, s, p, w("fc1"), xs)
                pe.drain().then_inc(inputs_used, 1)
                turn_normed(pe, g)
                pe.wait_ge(*s.emptied(p, "up1"))
                down_product(pe, w("fc2"), hT)

        def up_product(pe, s, p, weights, src):
            wv = weights.rearrange("p (c f) -> p c f", f=P)
            for j in range(2):
                pe.wait_ge(*s.bank_free(p, f"up{j}"))
                for i in range(2):
                    ins = pe.matmul(bank(s.bank(f"up{j}"))[:, i * PT:(i + 1) * PT], wv[:, 2 * j + i, :], src[:],
                                    start=True, stop=True)
                ins.then_inc(banks_filled, 1)

        def down_product(pe, weights, hidden):
            wv = weights.rearrange("p (c f) -> p c f", f=D)
            for u in range(2):
                for c in range(4):
                    ins = pe.matmul(ybank[:, u, :], hidden[:, c, u * P:(u + 1) * P], wv[:, c, :], start=(c == 0),
                                    stop=(c == 3))
            ins.then_inc(y_filled, 1)

        def ffn_scalar(act):
            s = ffn2
            with act.Fori(0, PAIRS) as p:
                for j in range(2):
                    act.wait_ge(banks_filled, s.filled(p, f"up{j}"))
                    for i in range(2):
                        ins = act.activation(hT[:, 2 * j + i, :], bank(s.bank(f"up{j}"))[:, i * PT:(i + 1) * PT],
                                             ACT.Gelu, bias=w("fc1b")[:, 2 * j + i:2 * j + i + 1])
                    ins.then_inc(act_emptied, 1)
                store_turned(act, g_of(s, p), before(act, p))

        def ffn_vector(v):
            s = ffn2
            with v.Fori(0, PAIRS) as p:
                v.drain()
                v.wait_ge(y_filled, p + yb(s))
                v.tensor_tensor(xr[:], ybank, pair(tok_all, p), ALU.add)
                v.drain()
                v.tensor_tensor(xr[:], xr[:], row("fc2_b"), ALU.add)
                v.drain()
                norm_rows(v, xr, xr, root(s, p, 1))
                v.drain()
                v.tensor_tensor(xr[:], xr[:], row("ln3_g"), ALU.mult)
                v.drain()
                v.tensor_tensor(xr[:], xr[:], row("ln3_b"), ALU.add)
                v.drain()
                v.tensor_tensor(xr[:], xr[:], pair(x_all, p), ALU.add)
                finish(v, s, p, g_of(s, p))

        tq = work[:, 0:PT]
        tz = work[:, PT:2 * PT]
        tm = work[:, 2 * PT:3 * PT]
        tc = work[:, 3 * PT:4 * PT]
        td = work[:, 4 * PT:5 * PT]
        tern_ready = Handoff("tern_ready", 1)

        def tern_tensor(pe):
            s = tern
            with pe.Fori(0, PAIRS) as p:
                g = g_of(s, p)
                turn_normed(pe, g)
                pe.wait_ge(*tern_ready.at(p, 1))
                for u in range(2):
                    ins = pe.matmul(ybank[:, u, :], tz[:, u * P:(u + 1) * P], ternw[:], start=True, stop=True)
                ins.then_inc(y_filled, 1)

        def tern_scalar(act):
            with act.Fori(0, PAIRS) as p:
                store_turned(act, g_of(tern, p), before(act, p))

        def tern_vector(v):
            s = tern
            v.memset(tc, 1.0e4)
            v.memset(td, -1.0e4)
            with v.Fori(0, PAIRS) as p:
                v.drain()
                v.wait_ge(staged, g_of(s, p) + 1 - PAIRS)
                v.tensor_scalar(tq, xs[:], actscale[:, 1:2], ROUND, ALU.mult, ALU.add)
                v.drain()
                v.tensor_scalar(tq, tq, ROUND, -127.0, ALU.subtract, ALU.max).then_inc(inputs_used, 1)
                v.drain()
                v.tensor_scalar(tq, tq, 127.0, actscale[:, 0:1], ALU.min, ALU.mult)
                v.drain()
                v.memset(tz, 0.0)
                v.tensor_tensor(tm, tq, tq, ALU.is_equal)
                v.drain()
                v.copy_predicated(tz, tm.bitcast(U32), tq)
                v.drain()
                v.tensor_scalar(tm, tq, FLT_MAX, None, ALU.is_gt)
                v.drain()
                v.copy_predicated(tz, tm.bitcast(U32), tc)
                v.drain()
                v.tensor_scalar(tm, tq, -FLT_MAX, None, ALU.is_lt)
                v.drain()
                v.copy_predicated(tz, tm.bitcast(U32), td).then_inc(tern_ready.sem, 1)
                v.wait_ge(y_filled, p + yb(s))
                v.tensor_tensor(xr[:], ybank, pair(x_all, p), ALU.add)
                v.drain()
                v.tensor_tensor(xr[:], xr[:], row("tern_b"), ALU.add)
                finish(v, s, p, g_of(s, p))

        q3 = work[:, 0:256]
        k3 = work[:, 256:512]
        v3 = work[:, 512:768].rearrange("p (u d) -> p u d", u=2)
        o3 = work[:, 1024:1536].rearrange("p (u b n) -> p u b n", u=2, b=2)
        o3T = work[:, 1536:1792]
        qx = work[:, 2048:6144].rearrange("p (u b h q) -> p u b h q", u=2, b=2, h=16)
        h3 = {k: Handoff(f"l3_{k}", n) for k, n in (("exp", 4), ("prob", 4), ("spread", 2))}

        def att3_tensor(pe):
            s = att3
            with pe.Fori(0, PAIRS) as p:
                g = g_of(s, p)
                pe.wait_ge(staged, g + 1 - PAIRS)
                pe.wait_ge(*s.bank_free(p, "qk"))
                bk = bank(s.bank("qk"))
                pe.matmul(bk[:, 0:PT], w("l3_wq"), xs[:], start=True, stop=True)
                pe.matmul(bk[:, PT:2 * PT], w("l3_wk"), cs[:], start=True, stop=True).then_inc(banks_filled, 1)
                pe.wait_ge(*s.bank_free(p, "v"))
                for u in range(2):
                    ins = pe.matmul(bank(s.bank("v"))[:, u * D:(u + 1) * D], cs[:, u * P:(u + 1) * P], w("l3_wv"),
                                    start=True, stop=True)
                ins.then_inc(banks_filled, 1)
                pe.drain().then_inc(inputs_used, 1)
                turn_normed(pe, g)
                for u in range(2):
                    pe.wait_ge(*h3["spread"].at(p, u + 1))
                    for half in range(2):
                        pe.wait_ge(*s.bank_free(p, f"s{u}{half}"))
                        bk = bank(s.bank(f"s{u}{half}"))
                        for c in range(4):
                            hp = 4 * half + c
                            for b in range(2):
                                t0 = (2 * u + b) * S
                                ins = pe.matmul(bk[:, (2 * c + b) * S:(2 * c + b + 1) * S],
                                                qx[:, u, b, 2 * hp:2 * hp + 2, :].rearrange("p h q -> p (h q)"),
                                                k3[:, t0:t0 + S], start=True, stop=True)
                        ins.then_inc(banks_filled, 1)
                for u in range(2):
                    probs_turned(pe, s, p, u, h3)
                    pe.wait_ge(*s.emptied(p, f"p{u}1"))
                    settle(pe)
                    for b in range(2):
                        pe.wait_ge(*s.bank_free(p, f"o{u}{b}"))
                        for hp in range(8):
                            ins = pe.matmul(bank(s.bank(f"o{u}{b}"))[:, hp * 16:hp * 16 + 16],
                                            pT[b * S:(b + 1) * S, u, hp, :],
                                            v3[b * S:(b + 1) * S, u, hp * 16:hp * 16 + 16], start=True, stop=True)
                        ins.then_inc(banks_filled, 1)
                pe.wait_ge(*s.emptied(p, "o11"))
                settle(pe)
                pe.wait_ge(*s.bank_free(p, "oT"))
                for u in range(2):
                    for b in range(2):
                        t0 = (2 * u + b) * S
                        ins = pe.matmul(bank(s.bank("oT"))[:, t0:t0 + S], o3[:, u, b, :], stack2[:], start=True,
                                        stop=True)
                ins.then_inc(banks_filled, 1)
                pe.wait_ge(*s.emptied(p, "oT"))
                for u in range(2):
                    ins = pe.matmul(ybank[:, u, :], o3T[:, u * P:(u + 1) * P], w("l3_wo"), start=True, stop=True)
                ins.then_inc(y_filled, 1)

        def att3_scalar(act):
            s = att3
            with act.Fori(0, PAIRS) as p:
                act.wait_ge(banks_filled, s.filled(p, "qk"))
                bk = bank(s.bank("qk"))
                act.activation(q3, bk[:, 0:PT], ACT.Identity, bias=w("l3_qkb")[:, 0:1])
                act.activation(k3, bk[:, PT:2 * PT], ACT.Identity, bias=w("l3_qkb")[:, 1:2]).then_inc(act_emptied, 1)
                store_turned(act, g_of(s, p), before(act, p))
                for u in range(2):
                    for half in range(2):
                        soft_exp(act, s, p, u, half, 8.0 ** -0.5, h3, False)
                store_probs(act, s, p, 0)
                store_probs(act, s, p, 1)
                act.wait_ge(banks_filled, s.filled(p, "oT"))
                act.activation(o3T, bank(s.bank("oT"))[:, 0:PT], ACT.Copy).then_inc(act_emptied, 1)

        def att3_vector(v):
            s = att3
            with v.Fori(0, PAIRS) as p:
                v.drain()
                v.wait_ge(banks_filled, s.filled(p, "v"))
                v.tensor_tensor(v3, bank(s.bank("v"))[:, 0:PT].rearrange("p (u d) -> p u d", u=2), row("l3_bv"),
                                ALU.add).then_inc(dve_emptied, 1)
                v.wait_ge(*s.emptied(p, "qk"))
                for u in range(2):
                    for b in range(2):
                        t0 = (2 * u + b) * S
                        ins = v.tensor_tensor(qx[:, u, b, :, :], q3[:, None, t0:t0 + S].to_broadcast([P, 16, S]),
                                              headmask[:, :, None].to_broadcast([P, 16, S]), ALU.mult)
                    ins.then_inc(h3["spread"].sem, 1)
                soft_in(v, s, p, 0, False, h3)
                soft_in(v, s, p, 1, False, h3)
                soft_out(v, p, 0, h3)
                soft_out(v, p, 1, h3)
                for u in range(2):
                    for b in range(2):
                        v.wait_ge(banks_filled, s.filled(p, f"o{u}{b}"))
                        v.tensor_tensor(o3[:, u, b, :].rearrange("p (c a e) -> p c a e", c=8, a=2),
                                        bank(s.bank(f"o{u}{b}"))[:, 0:P].rearrange("p (c a e) -> p c a e", c=8, a=2),
                                        parity[:, None, :, None].to_broadcast([P, 8, 2, 8]),
                                        ALU.mult).then_inc(dve_emptied, 1)
                v.wait_ge(y_filled, p + yb(s))
                v.tensor_tensor(xr[:], ybank, pair(x_all, p), ALU.add)
                v.drain()
                v.tensor_tensor(xr[:], xr[:], row("l3_bo"), ALU.add)
                finish(v, s, p, g_of(s, p))

        hid = work[:, 0:4 * T].rearrange("p (c t) -> p c t", c=4)
        hq = work[:, 4 * T:4 * T + 4 * PT].rearrange("p (c t) -> p c t", c=4)
        wsc = work[:, 4 * T + 4 * PT:4 * T + 4 * PT + 1536]
        q_ready = Handoff("q_ready", 1) if layers == 8 else None
        hq_ready = Handoff("hq_ready", 1) if layers == 8 else None
        amax_asked = sem("amax_asked")
        amax_given = sem("amax_given")
        LAST = PAIRS * (len(run) - 1)

        def quant16(v, ap, src, sc, inv):
            v.tensor_scalar(ap, src, sc, ROUND, ALU.mult, ALU.add)
            v.drain()
            v.tensor_scalar(ap, ap, ROUND, -32768.0, ALU.subtract, ALU.max)
            v.drain()
            return v.tensor_scalar(ap, ap, 32767.0, inv, ALU.min, ALU.mult)

        def hid3_tensor(pe):
            s = hid3
            turn_normed(pe, LAST)
            with pe.Fori(0, PAIRS) as p:
                pe.wait_ge(*q_ready.at(p, 1))
                up_product(pe, s, p, w("l3_in"), xs)

        def hid3_scalar(act):
            s = hid3
            store_turned(act, LAST, PAIRS - 1)
            with act.Fori(0, PAIRS) as p:
                for j in range(2):
                    act.wait_ge(banks_filled, s.filled(p, f"up{j}"))
                    for i in range(2):
                        ins = act.activation(hid[:, 2 * j + i, bass.ds(PT * p, PT)],
                                             bank(s.bank(f"up{j}"))[:, i * PT:(i + 1) * PT],
                                             ACT.Gelu, bias=w("l3_inb")[:, 2 * j + i:2 * j + i + 1])
                    ins.then_inc(act_emptied, 1)

        def scales(v, m, sc, inv, top):
            v.tensor_scalar(m, m, 1e-8, None, ALU.max)
            v.drain()
            v.reciprocal(sc, m)
            v.tensor_scalar(inv, m, 1.0 / top, None, ALU.mult)
            v.drain()
            v.tensor_scalar(sc, sc, top, None, ALU.mult)
            v.drain()

        def hid3_vector(v):
            s = hid3
            v.wait_ge(weights_in[4], 16)
            wo4 = w("l3_out").rearrange("p (c f) -> p c f", f=D)
            v.tensor_reduce(amax[:, 4:8], wo4, AX, ALU.max, apply_absolute_value=True)
            v.drain()
            scales(v, amax[:, 4:8], amax[:, 8:12], amax[:, 12:16], 127.0)
            for c in range(4):
                v.tensor_scalar(wo4[:, c, :], wo4[:, c, :], amax[:, 8 + c:9 + c], ROUND, ALU.mult, ALU.add)
            v.drain()
            v.tensor_scalar(w("l3_out"), w("l3_out"), ROUND, -128.0, ALU.subtract, ALU.max)
            v.drain()
            for c in range(4):
                v.tensor_scalar(wo4[:, c, :], wo4[:, c, :], 127.0, amax[:, 12 + c:13 + c], ALU.min, ALU.mult)
            v.drain()
            v.wait_ge(amax_given, 1)
            m, sc, inv = (wsc[:, 512 * i:512 * i + 512] for i in range(3))
            scales(v, m, sc, inv, 127.0)
            v.tensor_tensor(w("l3_in"), w("l3_in"), sc, ALU.mult)
            v.drain()
            v.tensor_scalar(w("l3_in"), w("l3_in"), ROUND, None, ALU.add)
            v.drain()
            v.tensor_scalar(w("l3_in"), w("l3_in"), ROUND, -128.0, ALU.subtract, ALU.max)
            v.drain()
            v.tensor_scalar(w("l3_in"), w("l3_in"), 127.0, None, ALU.min)
            v.drain()
            v.tensor_tensor(w("l3_in"), w("l3_in"), inv, ALU.mult)
            v.wait_ge(xt_stored, LAST + 1)
            v.tensor_reduce(amax[:, 0:1], xT_all[:], AX, ALU.max, apply_absolute_value=True).then_inc(amax_asked, 1)
            v.wait_ge(amax_given, 2)
            scales(v, amax[:, 1:2], amax[:, 2:3], amax[:, 3:4], 32767.0)
            with v.Fori(0, PAIRS) as p:
                v.drain()
                v.wait_ge(banks_filled, s.filled(p, "up1") - 2)
                quant16(v, xs[:], cols(xT_all, p), amax[:, 2:3], amax[:, 3:4]).then_inc(q_ready.sem, 1)
                v.wait_ge(*s.emptied(p, "up1"))
                v.tensor_reduce(small[:, bass.ds(p, 1)], hid[:, :, bass.ds(PT * p, PT)], mybir.AxisListType.XY,
                                ALU.max, apply_absolute_value=True)
            v.drain()
            v.tensor_reduce(amax[:, 0:1], small[:, 0:PAIRS], AX, ALU.max).then_inc(amax_asked, 1)
            v.wait_ge(amax_given, 3)
            scales(v, amax[:, 1:2], amax[:, 2:3], amax[:, 3:4], 32767.0)

        def hid3_pool(g):
            g.wait_ge(weights_in[4], 16)
            g.partition_all_reduce(wsc[:, 0:512], w("l3_in"), P, ABSMAX).then_inc(amax_given, 1)
            for k in range(2):
                g.wait_ge(amax_asked, k + 1)
                g.partition_all_reduce(amax[:, 1:2], amax[:, 0:1], P, ABSMAX).then_inc(amax_given, 1)

        def out3_tensor(pe):
            with pe.Fori(0, PAIRS) as p:
                pe.wait_ge(*hq_ready.at(p, 1))
                down_product(pe, w("l3_out"), hq)

        def out3_vector(v):
            s = out3
            with v.Fori(0, PAIRS) as p:
                v.drain()
                quant16(v, hq, hid[:, :, bass.ds(PT * p, PT)], amax[:, 2:3], amax[:, 3:4]).then_inc(hq_ready.sem, 1)
                v.wait_ge(y_filled, p + yb(s))
                v.tensor_tensor(xr[:], ybank, pair(x_all, p), ALU.add)
                v.drain()
                v.tensor_tensor(pair(x_all, p), xr[:], row("l3_bout"), ALU.add).then_inc(out_ready, 1)

        prog = {}
        if lstm in run:
            for k, n in (("rows", 1), ("abs", 1), ("ln", 1), ("D", 1), ("hvar", 1), ("hroot", 1)):
                h_lstm[k] = Handoff("lstm_" + k, n)

            def lstm_pool(g, p):
                g.wait_ge(*h_lstm["hvar"].at(p, 1))
                g.tensor_tensor(lstm_hq, lstm_hs, nhalf[:, 0:8], ALU.pow).then_inc(h_lstm["hroot"].sem, 1)
            prog[lstm] = (lstm_tensor, lstm_scalar, lstm_vector, lstm_pool)
        if moe0 in run:
            prog[moe0] = moe("m0", moe0, "m0", 8, 2, ACT.Gelu, 0)
        if att1 in run:
            prog[att1] = attention("a1", att1, "a1_wq", "a1_wk", "a1_wv", "a1_wo", True, 2, end_residual)
        if moe1 in run:
            prog[moe1] = moe("m1", moe1, "m1", 9, 1, ACT.Silu, 1)
        if satt in run:
            prog[satt] = attention("sa", satt, "sa_wq", "sa_wk", "sa_wv", "sa_wo", False, 4,
                                   end_decoder("ln1_g", "ln1_b", "sa_bo"))
            prog[catt] = attention("ca", catt, "ca_wq", "ca_wk", "ca_wv", "ca_wo", False, 4,
                                   end_decoder("ln2_g", "ln2_b", "ca_bo"))
            prog[ffn2] = (ffn_tensor, ffn_scalar, ffn_vector, None)
        if tern in run:
            prog[tern] = (tern_tensor, tern_scalar, tern_vector, None)
        if att3 in run:
            prog[att3] = (att3_tensor, att3_scalar, att3_vector, None)
        if hid3 in run:
            prog[hid3] = (hid3_tensor, hid3_scalar, hid3_vector, None)
            prog[out3] = (out3_tensor, lambda act: None, out3_vector, None)

        def stage_inputs(g, s, p):
            k = g_of(s, p)
            g.wait_ge(xt_stored, k + 2 - PAIRS)
            g.wait_ge(inputs_used, k + 1 - PAIRS)
            own = s in (satt,)
            keep = keep_len if s is att1 else keep_mask
            masked = s in (att1, satt, catt)
            g.tensor_copy(xs[:], cols(xT_all, p))
            if s in (lstm, att1, catt, att3):
                g.tensor_copy(cs[:], cols(ctxT_all, p))
            if masked:
                src = xT_all if own else ctxT_all
                g.tensor_tensor(ks[:], cols(src, p), cols(keep, p), ALU.mult)
            if s is lstm:
                g.tensor_tensor(lstm_q, cols(xT_all, p)[:, None, :].to_broadcast([P, 4, PT]),
                                quarter[:, :, None].to_broadcast([P, 4, PT]), ALU.mult)
                g.tensor_copy(lstm_v[:, :, :, 0:32], pair(tok_all, p).rearrange("p u (h e) -> p u h e", h=4))
            if masked:
                g.wait_ge(mask_used, masks.index(s) * PAIRS + p + 1)
                fill = FLT_MAX if s in (satt, catt) else 8.0e9
                settle(g)
                g.tensor_copy(negm[:], cols(keep, p))
                g.drain()
                g.tensor_scalar(negm[:], negm[:], -1.0, fill, ALU.add, ALU.mult)
            g.drain().then_inc(staged, 1)

        def take_last(g, pending):
            s, early = pending
            if early:
                early(g, PAIRS - 1)
            for k in range(roots[s][1]):
                take_root(g, s, PAIRS - 1, k + 1)

        masks = [s for s in (att1, satt, catt)]
        mask_used = sem("mask_used")

        block = es.enter_context(nc.Block())

        @block.sync
        def _(sp):
            sp.dma_start(x_all[:], x_in.rearrange("(t p) d -> p t d", p=P)).then_inc(x_in_done, 16)
            bounds = ["gates", "m0_router", "a1_wq", "m1_router", "sa_wq", None]
            for i in range(5):
                a = wcol[bounds[i]][0]
                z = wcol[bounds[i + 1]][0] if bounds[i + 1] else WIDTH
                if i == 1:
                    sp.dma_start(ctxT_all[:], ctxT_in).then_inc(ctx_in_done, 16)
                    sp.dma_start(tok_all[:], ctx_in.rearrange("(t p) d -> p t d", p=P)).then_inc(ctx_in_done, 16)
                    sp.dma_start(rows[:], rows_in.partition_broadcast(P)).then_inc(rest_in, 16)
                    sp.dma_start(moeb[:], moeb_in).then_inc(rest_in, 16)
                    sp.dma_start(lens_i, lens_in.partition_broadcast(P)).then_inc(rest_in, 16)
                    sp.dma_start(mask_u8, mask_in.partition_broadcast(P)).then_inc(rest_in, 16)
                    sp.dma_start(tern_i, tern_in).then_inc(rest_in, 16)
                    sp.dma_start(actscale[:, 0:1], scale_in.partition_broadcast(P)).then_inc(rest_in, 16)
                sp.dma_start(W[:, a:z], wpack[:, a:z]).then_inc(weights_in[i], 16)
            if layers < 8:
                sp.wait_ge(xn_ready, PAIRS * len(stages_run))
                sp.dma_start(out.rearrange("(t p) d -> p t d", p=P), x_all[:]).then_inc(out_stored, 16)
                sp.wait_ge(out_stored, 16)
            else:
                with sp.Fori(0, PAIRS) as p:
                    sp.wait_ge(out_ready, p + 1)
                    sp.dma_start(out[bass.ds(PT * p, PT), :].rearrange("(u p) d -> p u d", p=P),
                                 pair(x_all, p)).then_inc(out_stored, 16)
                sp.wait_ge(out_stored, 16 * PAIRS)

        @block.gpsimd
        def _(g):
            g.memset(ident[:], 0.0)
            g.memset(nhalf[:], -0.5)
            g.memset(euler[:], 2.718281828459045)
            g.memset(headmask[:], 1.0)
            g.memset(causal[:], 0.0)
            g.iota(ix[:].rearrange("p u e -> p (u e)").bitcast(I32), [[1, 16]], base=0, channel_multiplier=0)
            g.drain()
            g.affine_select(out=ident[:], in_=ident[:], compare_op=ALU.not_equal, fill=1.0, base=0,
                            pattern=[[-1, P]], channel_multiplier=1)
            g.affine_select(out=headmask[:], in_=headmask[:], compare_op=ALU.is_ge, fill=0.0, base=0,
                            pattern=[[-8, 16]], channel_multiplier=1)
            g.drain()
            for b in range(2):
                g.affine_select(out=causal[b * S:(b + 1) * S, :], in_=causal[b * S:(b + 1) * S, :],
                                compare_op=ALU.is_ge, fill=-NEG, base=0, pattern=[[1, S]], channel_multiplier=-1)
                g.drain()
            g.tensor_copy(iota8[:], ix[:].rearrange("p u e -> p (u e)").bitcast(I32))
            g.iota(xs[:, 0:S].bitcast(I32), [[1, S]], base=0, channel_multiplier=0)
            g.drain()
            g.affine_select(out=headmask[:], in_=headmask[:], compare_op=ALU.is_ge, fill=0.0, base=7,
                            pattern=[[8, 16]], channel_multiplier=-1)
            g.tensor_copy(iseq[:], xs[:, 0:S].bitcast(I32))
            g.memset(lstm_v[:, :, :, 32:33], 1.0)
            g.drain()
            g.drain().then_inc(consts_made, 1)
            g.drain().then_inc(inputs_used, 1)
            g.drain().then_inc(mask_used, 1)
            g.wait_ge(ctx_in_done, 32)
            g.wait_ge(converted, 1)
            with g.Fori(0, PAIRS - 1) as p:
                take_root(g, first, p, 1)
            pending = (first, None)
            for s in run + [None]:
                if s in (hid3, out3):
                    if s is hid3:
                        take_last(g, pending)
                        hid3_pool(g)
                        pending = None
                    continue
                if s is None:
                    if pending:
                        take_last(g, pending)
                    continue
                if pending[1]:
                    pending[1](g, PAIRS - 1)
                stage_inputs(g, s, 0)
                take_last(g, (pending[0], None))
                early = prog[s][3]
                with g.Fori(0, PAIRS - 1) as p:
                    if early:
                        early(g, p)
                    stage_inputs(g, s, p + 1)
                    for k in range(roots[s][1]):
                        take_root(g, s, p, k + 1)
                pending = (s, early)

        @block.vector
        def _(v):
            v.memset(parity[:], 0.0)
            v.memset(restart[:], 1.0)
            v.memset(restart_neg[:], 0.0)
            v.drain()
            v.memset(parity[0:S, 0:1], 1.0)
            v.memset(parity[S:P, 1:2], 1.0)
            v.memset(quarter[:], 0.0)
            v.drain()
            for h in range(4):
                v.memset(quarter[32 * h:32 * h + 32, h:h + 1], 1.0)
            v.memset(restart[:, 0:PT:S], 0.0)
            v.memset(restart_neg[:, 0:PT:S], -NEG)
            v.wait_ge(consts_made, 1)
            v.reduce_sum(row1[:], ident[:, 0:P:32], AX)
            v.reduce_sum(row2[:], ident[:, 1:P:32], AX)
            v.tensor_tensor(stack2[:], ident[:, 0:S], ident[:, S:P], ALU.add)
            v.tensor_copy(row1h[:], ident[:, 0:P:32])
            v.tensor_scalar(negrow2[:], ident[:, 1:P:32], -1.0, None, ALU.mult)
            v.wait_ge(rest_in, 96)
            v.tensor_copy(lensf[:], lens_i)
            v.tensor_scalar(actscale[:, 0:1], actscale[:, 0:1], 1e-5, None, ALU.max)
            v.tensor_copy(ternw[:], tern_i)
            v.drain()
            v.reciprocal(actscale[:, 1:2], actscale[:, 0:1])
            v.tensor_scalar(ternw[:], ternw[:], -1.0, None, ALU.add)
            v.tensor_tensor(keep_len[:].rearrange("p (b k) -> p b k", k=S), iseq[:, None, :].to_broadcast([P, B, S]),
                            lensf[:, :, None].to_broadcast([P, B, S]), ALU.is_lt)
            v.tensor_scalar(keep_mask[:], mask_u8, -1.0, 1.0, ALU.mult, ALU.add)
            v.drain()
            v.drain().then_inc(converted, 1)
            v.drain().then_inc(xt_filled, BUMP)
            v.drain().then_inc(dve_emptied, BUMP)
            first_vector(v)
            for s in run:
                prog[s][2](v)

        @block.scalar
        def _(act):
            act.drain().then_inc(xt_stored, 1)
            act.drain().then_inc(act_emptied, BUMP)
            with act.Fori(0, PAIRS - 1) as p:
                store_turned(act, p + 1, p)
            for s in run:
                prog[s][1](act)

        @block.tensor
        def _(pe):
            pe.wait_ge(consts_made, 1)
            with pe.Fori(0, PAIRS - 1) as p:
                turn_normed(pe, p + 1)
            for s in run:
                pe.wait_ge(act_emptied, s.base["a"])
                pe.wait_ge(dve_emptied, s.base["v"])
                prog[s][0](pe)


def pack(i):
    import numpy as np

    def chunks(a, n):
        return np.asarray(a).reshape(n, P, -1).transpose(1, 0, 2).reshape(P, -1)

    a = {k: np.asarray(v) for k, v in i.items()}
    ig, fg = a["L0_xattn_igate_w"], a["L0_xattn_fgate_w"]
    parts = {
        "gates": np.concatenate([np.repeat(g[:, 128 * k:128 * k + 128].T, 32, axis=1) for g in (ig, fg)
                                 for k in range(3)], axis=1),
        "gate_bias": np.stack([np.repeat(a["L0_xattn_igate_b"], 32), np.repeat(a["L0_xattn_fgate_b"], 32)], axis=1),
        "m0_router": a["L0_ffn_router_w"].T,
        "m0_up": a["L0_ffn_w1"].transpose(2, 0, 1).reshape(P, -1),
        "m0_upb": a["L0_ffn_b1"].reshape(16, P).T,
        "m0_down": chunks(a["L0_ffn_w2"].transpose(0, 2, 1).reshape(2048, P), 16),
        "a1_wq": a["L1_xattn_Wq"], "a1_wk": a["L1_xattn_Wk"], "a1_wv": a["L1_xattn_Wv"],
        "a1_wo": chunks(a["L1_xattn_Wo"], 8),
        "a1_norm": np.stack([np.tile(a["L1_xattn_q_norm_w"], 2), np.tile(a["L1_xattn_k_norm_w"], 2)], axis=1),
        "m1_router": a["L1_ffn_gate_w"].T,
        "m1_up": np.concatenate([chunks(a["L1_ffn_up_w"].reshape(1024, P), 8), a["L1_ffn_sh_up_w"]], axis=1),
        "m1_upb": np.concatenate([a["L1_ffn_up_b"], a["L1_ffn_sh_up_b"][None]]).T,
        "m1_down": np.concatenate([chunks(a["L1_ffn_down_w"].reshape(1024, P), 8), a["L1_ffn_sh_down_w"]], axis=1),
        "sa_wq": a["L2_xattn_sa_wq"], "sa_wk": a["L2_xattn_sa_wk"], "sa_wv": a["L2_xattn_sa_wv"],
        "sa_wo": chunks(a["L2_xattn_sa_wo"], 8),
        "ca_wq": a["L2_xattn_ca_wq"], "ca_wk": a["L2_xattn_ca_wk"], "ca_wv": a["L2_xattn_ca_wv"],
        "ca_wo": chunks(a["L2_xattn_ca_wo"], 8),
        "fc1": a["L2_xattn_fc1_w"], "fc1b": a["L2_xattn_fc1_b"].reshape(4, P).T, "fc2": chunks(a["L2_xattn_fc2_w"], 4),
        "l3_wq": a["L3_xattn_Wq"].T, "l3_wk": a["L3_xattn_Wk"].T, "l3_wv": a["L3_xattn_Wv"].T,
        "l3_wo": a["L3_xattn_Wo"].T, "l3_qkb": np.stack([a["L3_xattn_bq"], a["L3_xattn_bk"]], axis=1),
        "l3_in": a["L3_ffn_W_in"], "l3_inb": a["L3_ffn_b_in"].reshape(4, P).T, "l3_out": chunks(a["L3_ffn_W_out"], 4),
    }
    rows = {"out_w": "L0_xattn_out_w", "sa_bo": "L2_xattn_sa_bo", "ca_bo": "L2_xattn_ca_bo", "fc2_b": "L2_xattn_fc2_b",
            "tern_b": "L2_ffn_bias", "l3_bv": "L3_xattn_bv", "l3_bo": "L3_xattn_bo", "l3_bout": "L3_ffn_b_out"}
    for k in "123":
        rows[f"ln{k}_g"], rows[f"ln{k}_b"] = f"L2_xattn_ln{k}_g", f"L2_xattn_ln{k}_b"
    moeb = np.zeros((9, 2, D), np.float32)
    moeb[0:8, 0] = a["L0_ffn_b2"]
    moeb[0:8, 1] = a["L1_ffn_down_b"]
    moeb[8, 1] = a["L1_ffn_sh_down_b"]
    ctx = a["ctx_1024"].reshape(T, D)
    return {
        "wpack": np.concatenate([parts[n] for n, _ in SECTIONS], axis=1),
        "x_in": a["x"].reshape(T, D), "ctx_in": ctx, "ctxT_in": ctx.T,
        "rows_in": np.stack([a[rows[n]] for n in ROWS]), "moeb_in": moeb,
        "lens_in": a["_lenS2"], "mask_in": a["mask_BxS2_bk0"].reshape(T),
        "tern_in": a["L2_ffn_ternary_weight"].T, "scale_in": a["L2_ffn_act_scale"].reshape(1),
    }


LAYERS = 8


def kernel(**inputs):
    import numpy as np
    import concourse.bacc as bacc
    from concourse.bass_utils import run_bass_kernel_spmd

    nc = bacc.Bacc("TRN2", target_bir_lowering=False, num_devices=1)
    arrays = {k: np.ascontiguousarray(v) for k, v in pack(inputs).items()}
    aps = [nc.dram_tensor(k, v.shape, mybir.dt.from_np(v.dtype), kind="ExternalInput").ap() for k, v in arrays.items()]
    out = nc.dram_tensor("out", (T, D), F32, kind="ExternalOutput").ap()
    build_program(nc, *aps, out, layers=LAYERS)
    r = run_bass_kernel_spmd(nc, [arrays], core_ids=[0])
    return r.results[0]["out"].reshape(B, S, D)
```

```python
from contextlib import ExitStack

import concourse.bass as bass
from concourse import mybir

F32 = mybir.dt.float32
I32 = mybir.dt.int32
U32 = mybir.dt.uint32
U8 = mybir.dt.uint8
ALU = mybir.AluOpType
ACT = mybir.ActivationFunctionType
AX = mybir.AxisListType.X
ABSMAX = bass.bass_isa.ReduceOp.absmax

P = 128
B, S, D = 32, 64, 128
T = B * S
TILES = T // P
PAIRS = TILES // 2
PT = 2 * P
NEG = 3.0e38
ROUND = 12582912.0
FLT_MAX = 3.4028234663852886e38
BUMP = 64

SECTIONS = [
    ("gates", 768), ("gate_bias", 2),
    ("m0_router", 8), ("m0_up", 2048), ("m0_upb", 16), ("m0_down", 2048),
    ("a1_wq", 1024), ("a1_wk", 1024), ("a1_wv", 1024), ("a1_wo", 1024), ("a1_norm", 2),
    ("m1_router", 8), ("m1_up", 1152), ("m1_upb", 9), ("m1_down", 1152),
    ("sa_wq", 1024), ("sa_wk", 1024), ("sa_wv", 1024), ("sa_wo", 1024),
    ("ca_wq", 1024), ("ca_wk", 1024), ("ca_wv", 1024), ("ca_wo", 1024),
    ("fc1", 512), ("fc1b", 4), ("fc2", 512),
    ("l3_wq", 128), ("l3_wk", 128), ("l3_wv", 128), ("l3_wo", 128), ("l3_qkb", 2),
    ("l3_in", 512), ("l3_inb", 4), ("l3_out", 512),
]
WIDTH = sum(n for _, n in SECTIONS)
ROWS = ["out_w", "sa_bo", "ca_bo", "ln1_g", "ln1_b", "ln2_g", "ln2_b", "ln3_g", "ln3_b", "fc2_b",
        "tern_b", "l3_bv", "l3_bo", "l3_bout"]


class Stage:

    def __init__(self, index, units, before, sems, reps=PAIRS, ring=6):
        self.index, self.units, self.reps = index, units, reps
        self.names = [n for n, _ in units]
        self.sems = sems
        self.filled0, self.base = (before.filled0 + len(before.units) * before.reps, {
            e: before.base[e] + before.per[e] * before.reps for e in "av"}) if before else (0, {"a": BUMP, "v": BUMP})
        self.per = {e: sum(1 for _, k in units if k == e) for e in "av"}
        self.ring = ring

    def bank(self, name):
        return self.names.index(name) % self.ring

    def filled(self, p, name):
        return p * len(self.units) + (self.filled0 + self.names.index(name) + 1)

    def _emptied(self, p, j, back):
        e = self.units[j][1]
        order = sum(1 for _, k in self.units[:j + 1] if k == e)
        return self.sems[e], p * self.per[e] + (self.base[e] + order - back * self.per[e])

    def emptied(self, p, name):
        return self._emptied(p, self.names.index(name), 0)

    def emptied_before(self, p, name):
        return self._emptied(p, self.names.index(name), 1)

    def bank_free(self, p, name):
        j = self.names.index(name)
        if j >= self.ring:
            return self._emptied(p, j - self.ring, 0)
        last = max(k for k in range(len(self.units)) if k % self.ring == j % self.ring)
        return self._emptied(p, last, 1)


def build_program(nc, wpack, x_in, ctx_in, ctxT_in, rows_in, moeb_in, lens_in, mask_in, tern_in, scale_in, out,
                  layers=8):
    es = ExitStack()
    with es:
        def sb(name, shape, dt=F32):
            return es.enter_context(nc.sbuf_tensor(name, shape, dt))

        def sem(name):
            return es.enter_context(nc.semaphore(name))

        W = sb("weights", [P, WIDTH])
        wcol, at = {}, 0
        for name, n in SECTIONS:
            wcol[name] = (at, n)
            at += n

        def w(name):
            a, n = wcol[name]
            return W[:, a:a + n]

        x_all = sb("x_all", [P, TILES, D])
        xT_all = sb("xT_all", [P, T])
        ctxT_all = sb("ctxT_all", [P, T])
        tok_all = sb("tok_all", [P, TILES, D])
        neg_len = sb("neg_len", [P, T])
        neg_mask = sb("neg_mask", [P, T])
        rows = sb("rows", [P, len(ROWS), D])
        moeb = sb("moeb", [9, 2, D])
        ternw = sb("ternw", [P, D])
        ident = sb("ident", [P, P])
        xs = sb("xs", [P, PT])
        cs = sb("cs", [P, PT])
        xn = sb("xn", [P, 2, D])
        xr = sb("xr", [P, 2, D])
        st = sb("st", [P, 2, 6])
        mv = sb("mv", [P, 2, 2])
        var = sb("var", [P, 2])
        rstd = sb("rstd", [P, 2])
        nhalf = sb("nhalf", [P, 32])
        euler = sb("euler", [P, 16])
        work = sb("work", [P, 12288])
        small = sb("small", [P, 512])
        iota8 = sb("iota8", [P, 16])
        ix = sb("ix", [P, 2, 8], U32)
        row1 = sb("row1", [P, 1])
        row2 = sb("row2", [P, 1])
        row1h = sb("row1h", [P, 4])
        negrow2 = sb("negrow2", [P, 4])
        quarter = sb("quarter", [P, 4])
        parity = sb("parity", [P, 2])
        headmask = sb("headmask", [P, 16])
        causal = sb("causal", [P, S])
        restart = sb("restart", [P, PT])
        restart_neg = sb("restart_neg", [P, PT])
        iseq = sb("iseq", [P, S])
        lensf = sb("lensf", [P, B])
        actscale = sb("actscale", [P, 2])
        amax = sb("amax", [P, 16])
        big = es.enter_context(nc.psum_tensor("banks", [P, 8, 512], F32))

        def bank(i):
            return big[:, i, :]

        ybank = bank(6)[:, 0:PT].rearrange("p (u d) -> p u d", u=2)
        xtbank = bank(7)[:, 0:PT]
        lens_i = work[:, 0:B].bitcast(I32)
        mask_u8 = work[:, 1024:1024 + T // 4].bitcast(U8)
        tern_i = work[:, 64:64 + D].bitcast(I32)

        def row(name, n=2):
            i = ROWS.index(name)
            return rows[:, i:i + 1, :].to_broadcast([P, n, D])

        def pair(ap3, p):
            return ap3[:, bass.ds(2 * p, 2), :]

        def cols(ap2, p):
            return ap2[:, bass.ds(PT * p, PT)]

        weights_in = [sem(f"weights_in{i}") for i in range(5)]
        x_in_done = sem("x_in_done")
        ctx_in_done = sem("ctx_in_done")
        rest_in = sem("rest_in")
        consts_made = sem("consts_made")
        converted = sem("converted")
        banks_filled = sem("banks_filled")
        act_emptied = sem("act_emptied")
        dve_emptied = sem("dve_emptied")
        y_filled = sem("y_filled")
        xn_ready = sem("xn_ready")
        xt_filled = sem("xt_filled")
        xt_stored = sem("xt_stored")
        staged = sem("staged")
        inputs_used = sem("inputs_used")
        var_ready = sem("var_ready")
        rstd_ready = sem("rstd_ready")
        out_ready = sem("out_ready")
        out_stored = sem("out_stored")
        sems = {"a": act_emptied, "v": dve_emptied}

        stages = []

        def stage(units, reps=PAIRS):
            s = Stage(len(stages), units, stages[-1] if stages else None, sems, reps)
            stages.append(s)
            return s

        def pipelined(these, mixing, inputs, late, tail=[]):
            s = stage([])
            s.pro = stage(inputs + late, 1)
            s.body = stage(these + inputs + mixing + late + tail, PAIRS - 1)
            s.epi = stage(these + mixing + tail, 1)
            return s

        first = stage([("none", "a")])
        first.units = []
        first.per = {"a": 0, "v": 0}
        lstm = stage([("gates", "a"), ("maxD", "a"), ("argD", "v"), ("qk", "v"), ("num", "a")])

        def moe_units(nu, nd, lag):
            u = [("route", "v"), ("up0", "a"), ("up1", "a")]
            ups, downs = list(range(2, nu)), list(range(nd))
            per = nu / nd
            done = 2
            for d in downs:
                need = min(nu, int(per * (d + 1) + 0.99) + lag)
                while done < need:
                    u.append((f"up{done}", "a"))
                    done += 1
                if d == nd - 1:
                    u.append(("combT", "v"))
                u.append((f"down{d}", "v"))
            return u

        moe0 = stage(moe_units(8, 4, 2))
        scores4 = [(f"s{u}{half}", "v") for u in range(2) for half in range(2)]
        mixing8 = [(f"{k}{u}{n}", "a") for k in "po" for u in range(2) for n in range(2)]
        values4 = [(f"v{c}", "a") for c in range(4)]
        att1 = pipelined(scores4, mixing8, [(f"tok{u}{c}", "a") for u in range(2) for c in range(4)],
                         values4 + [(f"turn{u}{c}", "av"[c % 2]) for u in range(2) for c in range(4)])
        moe1 = stage(moe_units(5, 5, 1))
        satt = pipelined(scores4, mixing8, [(f"qk{c}", "a") for c in range(8)], values4)
        catt = pipelined(scores4, mixing8, [(f"qk{c}", "a") for c in range(8)], values4)
        ffn2 = stage([("up0", "a"), ("up1", "a")])
        tern = stage([])
        att3 = pipelined(scores4, [("p00", "a"), ("p01", "a"), ("p10", "a"), ("p11", "a"), ("o", "a")],
                         [("qk", "a")], [("v", "v")], [("oT", "a")])
        hid3 = stage([("up0", "a"), ("up1", "a")])
        out3 = stage([])

        plan = {0: [], 1: [lstm], 2: [moe0], 3: [att1], 4: [moe1], 5: [satt, catt, ffn2], 6: [tern], 7: [att3],
                8: [hid3, out3]}
        run = [s for k in range(layers + 1) for s in plan[k]]
        weight_group = {lstm: 0, moe0: 1, att1: 2, moe1: 3}

        class Handoff:
            def __init__(self, name, n):
                self.sem, self.n = sem(name), n

            def at(self, p, k):
                return self.sem, p * self.n + k

        def norm_stats(v, src):
            for u in range(2):
                v.bn_stats(st[:, u, :], src[:, u, :])
            v.drain()
            for u in range(2):
                v.bn_aggr(mv[:, u, :], st[:, u, :])
            v.drain()
            v.tensor_scalar(var[:], mv[:, :, 1], 1e-5, None, ALU.add).then_inc(var_ready, 1)

        def norm_apply(v, src, dst, value):
            v.wait_ge(rstd_ready, value)
            for u in range(2):
                ins = v.tensor_scalar(dst[:, u, :], src[:, u, :], mv[:, u, 0:1], rstd[:, u:u + 1],
                                      ALU.subtract, ALU.mult)
            return ins

        def norm_rows(v, src, dst, value):
            norm_stats(v, src)
            return norm_apply(v, src, dst, value)

        roots = {}
        count = 0
        for s in [first] + run:
            per = {ffn2: 2, lstm: 1}.get(s, 1)
            if s in (hid3, out3):
                per = 0
            roots[s] = (count, per)
            count += per * PAIRS

        def root(s, p, k):
            return p * roots[s][1] + (roots[s][0] + k)

        def take_root(g, s, p, k):
            g.wait_ge(var_ready, root(s, p, k))
            g.tensor_tensor(rstd[:], var[:], nhalf[:, 0:2], ALU.pow).then_inc(rstd_ready, 1)

        def store_normed(v, s, p):
            pass

        def turn_normed(pe, g):
            pe.wait_ge(xn_ready, g)
            pe.wait_ge(xt_stored, g)
            for u in range(2):
                ins = pe.transpose(xtbank[:, u * P:(u + 1) * P], xn[:, u, :], ident[:])
            ins.then_inc(xt_filled, 1)

        settled = sem("settled")

        def settle(pe):
            pe.sem_inc(settled, 1)

        def store_turned(act, g, p):
            act.wait_ge(xt_filled, g + BUMP)
            act.activation(cols(xT_all, p), xtbank, ACT.Copy).then_inc(xt_stored, 1)

        def g_of(s, p):
            return p + PAIRS * stages_run.index(s)

        stages_run = [first] + run

        def prev_pair(p):
            return p + (PAIRS - 1) if isinstance(p, int) else p + (PAIRS - 1)

        def before(eng, p):
            return eng.snap((p + (PAIRS - 1)) & (PAIRS - 1))

        def first_vector(v):
            v.wait_ge(x_in_done, 16)
            with v.Fori(0, PAIRS) as p:
                v.drain()
                v.tensor_copy(xr[:], pair(x_all, p))
                v.drain()
                v.wait_ge(xt_filled, p + BUMP)
                norm_rows(v, xr, xn, root(first, p, 1)).then_inc(xn_ready, 1)

        lstm_z = work[:, 0:256]
        lstm_e = work[:, 256:512]
        lstm_ig = work[:, 512:768]
        lstm_lf = work[:, 768:1024]
        lstm_cs = work[:, 1024:1280]
        lstm_g = work[:, 1280:1536]
        lstm_G = work[:, 1536:1792]
        lstm_m = work[:, 1792:2048]
        lstm_L = work[:, 2048:2304]
        lstm_R = work[:, 5120:6144].rearrange("p (h t) -> p h t", h=4)
        lstm_q = work[:, 6144:7168].rearrange("p (h t) -> p h t", h=4)
        lstm_D = work[:, 2560:3072]
        lstm_C = work[:, 3072:3584]
        lstm_v = work[:, 3584:3584 + 264].rearrange("p (u h e) -> p u h e", u=2, h=4)
        lstm_h = work[:, 4096:4096 + 264].rearrange("p (u h e) -> p (u h) e", u=2, h=4)
        lstm_n = work[:, 4608:4864].rearrange("p (g e) -> p g e", g=8)
        lstm_n2 = work[:, 4864:5120].rearrange("p (g e) -> p g e", g=8)
        lstm_hv = small[:, 0:8]
        lstm_hr = small[:, 8:16]
        lstm_hm = small[:, 16:24]
        lstm_hs = small[:, 24:32]
        lstm_hq = small[:, 32:40]
        lstm_em = small[:, 40:48]
        h_lstm = {}

        def lstm_tensor(pe):
            s = lstm
            gw = w("gates").rearrange("p (k n) -> p k n", k=6)
            pe.wait_ge(weights_in[0], 16)
            with pe.Fori(0, PAIRS) as p:
                g = g_of(s, p)
                pe.wait_ge(*s.bank_free(p, "gates"))
                pe.wait_ge(staged, g + 1 - PAIRS)
                bk = bank(s.bank("gates"))
                for gate in range(2):
                    for k in range(3):
                        ins = pe.matmul(bk[:, gate * PT:(gate + 1) * PT], gw[:, 3 * gate + k, :],
                                        xs[:] if k == 0 else cs[:], start=(k == 0), stop=(k == 2))
                ins.then_inc(banks_filled, 1)
                turn_normed(pe, g)
                pe.wait_ge(*h_lstm["rows"].at(p, 1))
                pe.wait_ge(*s.bank_free(p, "maxD"))
                for u in range(2):
                    ins = pe.transpose(bank(s.bank("maxD"))[:, u * P:(u + 1) * P], lstm_m[:, u * P:(u + 1) * P],
                                       ident[:])
                ins.then_inc(banks_filled, 1)
                for name, lhs, rhs in (("argD", lstm_L, lstm_R), ("qk", cs, lstm_q)):
                    pe.wait_ge(*s.bank_free(p, name))
                    bk = bank(s.bank(name))
                    for u in range(2):
                        for b in range(2):
                            c = (2 * u + b) * S
                            ins = pe.matmul(bk[b * S:(b + 1) * S, u * 256:(u + 1) * 256], lhs[:, c:c + S],
                                            rhs[:, :, c:c + S], start=True, stop=True)
                    ins.then_inc(banks_filled, 1)
                pe.wait_ge(*s.emptied(p, "qk"))
                pe.wait_ge(*s.bank_free(p, "num"))
                settle(pe)
                bk = bank(s.bank("num"))
                for u in range(2):
                    for h in range(4):
                        for b in range(2):
                            ins = pe.matmul(bk[b * S:(b + 1) * S, (u * 4 + h) * 33:(u * 4 + h + 1) * 33],
                                            lstm_C[b * S:(b + 1) * S, (u * 4 + h) * S:(u * 4 + h + 1) * S],
                                            lstm_v[b * S:(b + 1) * S, u, h, :], start=True, stop=True)
                ins.then_inc(banks_filled, 1)
                pe.drain().then_inc(inputs_used, 1)

        def lstm_scalar(act):
            s = lstm
            act.wait_ge(weights_in[0], 16)
            with act.Fori(0, PAIRS) as p:
                g = g_of(s, p)
                act.wait_ge(banks_filled, s.filled(p, "gates"))
                bk = bank(s.bank("gates"))
                act.activation(lstm_ig, bk[:, 0:PT], ACT.Identity, bias=w("gate_bias")[:, 0:1])
                act.activation(lstm_z, bk[:, PT:2 * PT], ACT.Identity,
                               bias=w("gate_bias")[:, 1:2]).then_inc(act_emptied, 1)
                act.wait_ge(*h_lstm["abs"].at(p, 1))
                act.activation(lstm_e, lstm_e, ACT.Exp, scale=-1.0)
                act.drain()
                act.activation(lstm_e, lstm_e, ACT.Ln, bias=1.0).then_inc(h_lstm["ln"].sem, 1)
                store_turned(act, g, before(act, p))
                act.wait_ge(banks_filled, s.filled(p, "maxD"))
                m8 = bank(s.bank("maxD"))[:, 0:PT].rearrange("p (u h r) -> p u h r", u=2, h=4)
                act.activation(lstm_em.rearrange("p (u h) -> p u h", u=2), m8[:, :, :, 0], ACT.Exp,
                               scale=-1.0).then_inc(act_emptied, 1)
                act.wait_ge(*s.emptied(p, "argD"))
                act.activation(lstm_D, lstm_D, ACT.Exp).then_inc(h_lstm["D"].sem, 1)
                act.wait_ge(banks_filled, s.filled(p, "num"))
                act.activation(lstm_h, bank(s.bank("num"))[:, 0:264].rearrange("p (g e) -> p g e", e=33),
                               ACT.Copy).then_inc(act_emptied, 1)

        def lstm_vector(v):
            s = lstm
            with v.Fori(0, PAIRS) as p:
                v.drain()
                g = g_of(s, p)
                v.wait_ge(*s.emptied(p, "gates"))
                v.scalar_tensor_tensor(out=lstm_e, in0=lstm_z, scalar=-1.0, in1=lstm_z, op0=ALU.mult,
                                       op1=ALU.max).then_inc(h_lstm["abs"].sem, 1)
                v.wait_ge(*h_lstm["ln"].at(p, 1))
                v.scalar_tensor_tensor(out=lstm_lf, in0=lstm_z, scalar=0.0, in1=lstm_e, op0=ALU.min,
                                       op1=ALU.subtract)
                v.drain()
                v.tensor_tensor_scan(lstm_cs, restart[:], lstm_lf, 0.0, ALU.mult, ALU.add)
                v.drain()
                v.tensor_tensor(lstm_g, lstm_lf, lstm_cs, ALU.subtract)
                v.drain()
                v.tensor_tensor(lstm_g, lstm_g, lstm_ig, ALU.add)
                v.drain()
                v.tensor_tensor_scan(lstm_G, restart_neg[:], lstm_g, -NEG, ALU.add, ALU.max)
                v.drain()
                v.tensor_scalar(lstm_L, lstm_g, row1[:], row2[:], ALU.mult, ALU.add)
                v.tensor_tensor(lstm_m, lstm_cs, lstm_G, ALU.add)
                for h in range(4):
                    ins = v.tensor_scalar(lstm_R[:, h, :], lstm_G, negrow2[:, h:h + 1], row1h[:, h:h + 1],
                                          ALU.mult, ALU.add)
                ins.then_inc(h_lstm["rows"].sem, 1)
                v.wait_ge(banks_filled, s.filled(p, "argD"))
                v.tensor_tensor(lstm_D.rearrange("p (g k) -> p g k", g=8),
                                bank(s.bank("argD")).rearrange("p (g k) -> p g k", g=8),
                                causal[:, None, :].to_broadcast([P, 8, S]), ALU.add).then_inc(dve_emptied, 1)
                v.wait_ge(*h_lstm["D"].at(p, 1))
                v.wait_ge(banks_filled, s.filled(p, "qk"))
                v.scalar_tensor_tensor(out=lstm_C, in0=bank(s.bank("qk")), scalar=32.0 ** -0.5, in1=lstm_D,
                                       op0=ALU.mult, op1=ALU.mult).then_inc(dve_emptied, 1)
                v.wait_ge(*s.emptied(p, "num"))
                v.scalar_tensor_tensor(out=lstm_hv, in0=lstm_h[:, :, 32], scalar=-1.0, in1=lstm_h[:, :, 32],
                                       op0=ALU.mult, op1=ALU.max)
                v.drain()
                v.tensor_tensor(lstm_hv, lstm_hv, lstm_em, ALU.max)
                v.drain()
                v.tensor_scalar(lstm_hv, lstm_hv, 1e-8, None, ALU.add)
                v.drain()
                v.reciprocal(lstm_hr, lstm_hv)
                v.drain()
                v.tensor_tensor(lstm_n, lstm_h[:, :, 0:32], lstm_hr[:, :, None].to_broadcast([P, 8, 32]), ALU.mult)
                v.drain()
                v.reduce_sum(lstm_hm, lstm_n, AX)
                v.drain()
                v.tensor_scalar(lstm_hm, lstm_hm, 1.0 / 32, None, ALU.mult)
                v.drain()
                v.tensor_tensor(lstm_n, lstm_n, lstm_hm[:, :, None].to_broadcast([P, 8, 32]), ALU.subtract)
                v.drain()
                v.tensor_tensor(lstm_n2, lstm_n, lstm_n, ALU.mult)
                v.drain()
                v.reduce_sum(lstm_hs, lstm_n2, AX)
                v.drain()
                v.tensor_scalar(lstm_hs, lstm_hs, 1.0 / 32, 1e-5, ALU.mult, ALU.add).then_inc(h_lstm["hvar"].sem, 1)
                v.wait_ge(*h_lstm["hroot"].at(p, 1))
                v.tensor_tensor(lstm_n, lstm_n, lstm_hq[:, :, None].to_broadcast([P, 8, 32]), ALU.mult)
                v.tensor_scalar(lstm_n2.rearrange("p (u h) e -> p u (h e)", u=2), row("out_w"), 1.0, None, ALU.add)
                v.drain()
                v.tensor_tensor(lstm_n, lstm_n, lstm_n2, ALU.mult)
                v.drain()
                v.tensor_tensor(xr[:], lstm_n.rearrange("p (u h) e -> p u (h e)", u=2), pair(x_all, p), ALU.add)
                finish(v, s, p, g)

        def finish(v, s, p, g):
            v.drain()
            v.tensor_copy(pair(x_all, p), xr[:])
            v.wait_ge(xt_filled, g + BUMP)
            norm_rows(v, xr, xn, root(s, p, roots[s][1])).then_inc(xn_ready, 1)

        lg = small[:, 0:16].rearrange("p (u e) -> p u e", u=2)
        mx8 = small[:, 16:32].rearrange("p (u e) -> p u e", u=2)
        ds8 = small[:, 32:48].rearrange("p (u e) -> p u e", u=2)
        es8 = small[:, 48:64].rearrange("p (u e) -> p u e", u=2)
        idxf = small[:, 64:68].rearrange("p (u e) -> p u e", u=2)
        tsum = small[:, 68:70]
        wtop = small[:, 70:74].rearrange("p (u e) -> p u e", u=2)
        comb = small[:, 80:98].rearrange("p (u e) -> p u e", u=2)
        comb2 = small[:, 100:116].rearrange("p (u e) -> p u e", u=2)
        combT = small[:, 128:384]
        hT = work[:, 0:4096].rearrange("p (c t) -> p c t", t=PT)
        prod = work[:, 4096:4096 + 2304]

        def moe(tag, s, pre, experts, chunks, func, layer):
            nch = experts * chunks
            ups = [n for n in s.names if n.startswith("up")]
            downs = [n for n in s.names if n.startswith("down")]
            per_down = 2
            pr = prod[:, 0:2 * experts * D].rearrange("p (u e d) -> p u e d", u=2, e=experts)
            asked = Handoff(f"{tag}_exp_asked", 1)
            given = Handoff(f"{tag}_exp_given", 1)
            comb_ready = Handoff(f"{tag}_comb_ready", 1)
            upw = w(pre + "_up").rearrange("p (c f) -> p c f", f=P)
            dnw = w(pre + "_down").rearrange("p (c f) -> p c f", f=D)

            def tensor(pe):
                pe.wait_ge(weights_in[weight_group[s]], 16)
                with pe.Fori(0, PAIRS) as p:
                    g = g_of(s, p)
                    pe.wait_ge(staged, g + 1 - PAIRS)
                    for n, name in enumerate(s.names):
                        if name == "combT":
                            pe.wait_ge(*comb_ready.at(p, 1))
                        pe.wait_ge(*s.bank_free(p, name))
                        bk = bank(s.bank(name))
                        if name == "route":
                            for u in range(2):
                                ins = pe.matmul(bk[:, 8 * u:8 * u + 8], xs[:, u * P:(u + 1) * P], w(pre + "_router"),
                                                start=True, stop=True)
                        elif name == "combT":
                            for u in range(2):
                                ins = pe.transpose(bk[0:experts, u * P:(u + 1) * P], comb[:, u, 0:experts], ident[:])
                        elif name.startswith("up"):
                            j = int(name[2:])
                            for c in range(2 * j, min(2 * j + 2, nch)):
                                ins = pe.matmul(bk[:, (c % 2) * PT:(c % 2 + 1) * PT], upw[:, c, :], xs[:],
                                                start=True, stop=True)
                        else:
                            j = int(name[4:])
                            last = min((j + 1) * per_down * chunks, nch) - 1
                            settle(pe)
                            pe.wait_ge(*s.emptied(p, f"up{last // 2}"))
                            for u in range(2):
                                for e in range(2 * j, min(2 * j + 2, experts)):
                                    for c in range(chunks):
                                        ins = pe.matmul(bk[:, (2 * u + e % 2) * D:(2 * u + e % 2 + 1) * D],
                                                        hT[:, e * chunks + c, u * P:(u + 1) * P],
                                                        dnw[:, e * chunks + c, :], start=(c == 0),
                                                        stop=(c == chunks - 1))
                        ins.then_inc(banks_filled, 1)
                        if name == "up1":
                            turn_normed(pe, g)
                    pe.drain().then_inc(inputs_used, 1)
                    pe.wait_ge(*s.emptied(p, "combT"))
                    for u in range(2):
                        ins = pe.matmul(ybank[:, u, :], combT[0:experts, u * P:(u + 1) * P],
                                        moeb[0:experts, layer, :], start=True, stop=True)
                    ins.then_inc(y_filled, 1)

            def scalar(act):
                with act.Fori(0, PAIRS) as p:
                    for name in ups:
                        j = int(name[2:])
                        act.wait_ge(banks_filled, s.filled(p, name))
                        for c in range(2 * j, min(2 * j + 2, nch)):
                            ins = act.activation(hT[:, c, :], bank(s.bank(name))[:, (c % 2) * PT:(c % 2 + 1) * PT],
                                                 func, bias=w(pre + "_upb")[:, c:c + 1])
                        ins.then_inc(act_emptied, 1)
                        if j == 1:
                            store_turned(act, g_of(s, p), before(act, p))

            def vector(v):
                if experts == 9:
                    v.memset(comb[:, :, 8:9], 1.0)
                with v.Fori(0, PAIRS) as p:
                    v.drain()
                    v.wait_ge(banks_filled, s.filled(p, "route"))
                    v.tensor_copy(lg, bank(s.bank("route"))[:, 0:16].rearrange("p (u e) -> p u e", u=2)) \
                        .then_inc(dve_emptied, 1)
                    v.drain()
                    for u in range(2):
                        v.max(mx8[:, u, :], lg[:, u, :])
                    v.drain()
                    v.tensor_tensor(ds8, mx8, mx8[:, :, 0:1].to_broadcast([P, 2, 8]), ALU.subtract) \
                        .then_inc(asked.sem, 1)
                    for u in range(2):
                        v.max_index(ix[:, u, :], mx8[:, u, :], lg[:, u, :])
                    v.drain()
                    v.tensor_copy(idxf, ix[:, :, 0:2])
                    v.wait_ge(*given.at(p, 1))
                    if experts == 9:
                        v.reduce_sum(tsum, es8, AX)
                        v.drain()
                        v.reciprocal(tsum, tsum)
                        v.drain()
                        v.tensor_tensor(wtop, es8[:, :, 0:2], tsum[:, :, None].to_broadcast([P, 2, 2]), ALU.mult)
                        v.drain()
                        v.tensor_tensor(tsum, wtop[:, :, 0], wtop[:, :, 1], ALU.add)
                        v.drain()
                        v.tensor_scalar(tsum, tsum, 1e-20, None, ALU.add)
                        top = wtop
                    else:
                        v.tensor_tensor(tsum, es8[:, :, 0], es8[:, :, 1], ALU.add)
                        top = es8[:, :, 0:2]
                    v.drain()
                    v.reciprocal(tsum, tsum)
                    v.drain()
                    v.tensor_tensor(wtop, top, tsum[:, :, None].to_broadcast([P, 2, 2]), ALU.mult)
                    v.drain()
                    for u in range(2):
                        v.tensor_scalar(comb[:, u, 0:8], iota8[:, 0:8], idxf[:, u, 0:1], wtop[:, u, 0:1],
                                        ALU.is_equal, ALU.mult)
                        v.tensor_scalar(comb2[:, u, :], iota8[:, 0:8], idxf[:, u, 1:2], wtop[:, u, 1:2],
                                        ALU.is_equal, ALU.mult)
                    v.drain()
                    v.tensor_tensor(comb[:, :, 0:8], comb[:, :, 0:8], comb2, ALU.add).then_inc(comb_ready.sem, 1)
                    v.drain()
                    for name in s.names[1:]:
                        if name.startswith("up"):
                            continue
                        v.wait_ge(banks_filled, s.filled(p, name))
                        if name == "combT":
                            v.tensor_copy(combT[0:experts, :], bank(s.bank(name))[0:experts, 0:PT]) \
                                .then_inc(dve_emptied, 1)
                            continue
                        j = int(name[4:])
                        n = min(2 * j + 2, experts) - 2 * j
                        bk = bank(s.bank(name)).rearrange("p (u e d) -> p u e d", u=2, e=2)
                        for u in range(2):
                            ins = v.tensor_tensor(pr[:, u, 2 * j:2 * j + n, :], bk[:, u, 0:n, :],
                                                  comb[:, u, 2 * j:2 * j + n, None].to_broadcast([P, n, D]), ALU.mult)
                        ins.then_inc(dve_emptied, 1)
                    v.drain()
                    for u in range(2):
                        v.reduce_sum(xr[:, u, :], pr[:, u, :, :].rearrange("p e d -> p d e"), AX)
                    v.drain()
                    v.tensor_tensor(xr[:], xr[:], pair(x_all, p), ALU.add)
                    v.drain()
                    v.wait_ge(y_filled, p + yb(s))
                    v.tensor_tensor(xr[:], ybank, xr[:], ALU.add)
                    if layer == 1:
                        finish(v, s, p, g_of(s, p))
                        v.drain()
                        v.tensor_copy(pair(tok_all, p), xn[:])
                    else:
                        finish(v, s, p, g_of(s, p))

            def pool(g, p):
                g.wait_ge(*asked.at(p, 1))
                g.tensor_tensor(es8, euler[:].rearrange("p (u e) -> p u e", u=2), ds8, ALU.pow).then_inc(given.sem, 1)

            return tensor, scalar, vector, pool

        ystages = [s for s in run if s is not lstm and s is not hid3]

        def yb(s):
            return ystages.index(s) * PAIRS + 1

        qT = work[:, 0:2048].rearrange("p (c t) -> p c t", t=PT)
        kT = work[:, 2048:4096].rearrange("p (c t) -> p c t", t=PT)
        vv = work[:, 4096:6144].rearrange("p (u n) -> p u n", u=2)
        sm = work[:, 6144:8192].rearrange("p (u n) -> p u n", u=2)
        pT = work[:, 8192:10240].rearrange("p (u c t) -> p u c t", u=2, c=8)
        oT = work[:, 10240:12288].rearrange("p (u c t) -> p u c t", u=2, c=8)
        mxs = small[:, 0:32].rearrange("p (u g) -> p u g", u=2)
        rs = small[:, 32:64].rearrange("p (u g) -> p u g", u=2)
        ssq = small[:, 64:128]
        rsq = small[:, 128:192]

        def soft_in(v, s, i, p, u, neg, h):
            every = sm[:, u, :].rearrange("p (g k) -> p g k", k=S)
            if neg is not None:
                for half in range(2):
                    v.wait_ge(banks_filled, s.filled(i, f"s{u}{half}"))
                    v.tensor_tensor(sm[:, u, 512 * half:512 * half + 512].rearrange("p (c k) -> p c k", k=P),
                                    bank(s.bank(f"s{u}{half}")).rearrange("p (c k) -> p c k", k=P),
                                    cols(neg, p)[:, None, u * P:(u + 1) * P].to_broadcast([P, 4, P]), ALU.add) \
                        .then_inc(dve_emptied, 1)
                v.drain()
                v.reduce_max(mxs[:, u, :], every, AX)
                v.drain()
                v.tensor_tensor(every, every, mxs[:, u, :, None].to_broadcast([P, 16, S]), ALU.subtract) \
                    .then_inc(h["arg"].sem, 1)
                return
            for half in range(2):
                v.wait_ge(banks_filled, s.filled(i, f"s{u}{half}"))
                v.reduce_max(mxs[:, u, 8 * half:8 * half + 8],
                             bank(s.bank(f"s{u}{half}")).rearrange("p (g k) -> p g k", k=S), AX)
            v.drain()
            for half in range(2):
                v.tensor_tensor(every[:, 8 * half:8 * half + 8, :],
                                bank(s.bank(f"s{u}{half}")).rearrange("p (g k) -> p g k", k=S),
                                mxs[:, u, 8 * half:8 * half + 8, None].to_broadcast([P, 8, S]), ALU.subtract) \
                    .then_inc(dve_emptied, 1)
            v.drain().then_inc(h["arg"].sem, 1)

        def soft_exp(act, p, u, scale, h):
            act.wait_ge(*h["arg"].at(p, u + 1))
            act.activation(sm[:, u, :], sm[:, u, :], ACT.Exp, scale=scale).then_inc(h["exp"].sem, 1)

        def soft_out(v, p, u, h):
            every = sm[:, u, :].rearrange("p (g k) -> p g k", k=S)
            v.wait_ge(*h["exp"].at(p, u + 1))
            v.reduce_sum(rs[:, u, :], every, AX)
            v.drain()
            v.reciprocal(rs[:, u, :], rs[:, u, :])
            v.drain()
            v.tensor_tensor(every, every, rs[:, u, :, None].to_broadcast([P, 16, S]), ALU.mult) \
                .then_inc(h["prob"].sem, 1)

        def probs_turned(pe, s, i, p, u, h):
            pe.wait_ge(*h["prob"].at(p, u + 1))
            for half in range(2):
                name = f"p{u}{half}"
                pe.wait_ge(*s.bank_free(i, name))
                for c in range(4):
                    ins = pe.transpose(bank(s.bank(name))[:, c * P:(c + 1) * P],
                                       sm[:, u, 512 * half + c * P:512 * half + (c + 1) * P], ident[:])
                ins.then_inc(banks_filled, 1)

        def store_probs(act, s, i, u):
            for half in range(2):
                act.wait_ge(banks_filled, s.filled(i, f"p{u}{half}"))
                act.activation(pT[:, u, 4 * half:4 * half + 4, :].rearrange("p c t -> p (c t)"),
                               bank(s.bank(f"p{u}{half}")), ACT.Copy).then_inc(act_emptied, 1)

        def steps(eng, s, part):
            for ring, this, nxt in ((s.pro, False, True), (s.body, True, True), (s.epi, True, False)):
                if eng is nc.tensor:
                    eng.wait_ge(act_emptied, ring.base["a"])
                    eng.wait_ge(dve_emptied, ring.base["v"])
                if ring is s.body:
                    part(ring, 0, 0, this, nxt, last=False)
                    with eng.Fori(1, PAIRS - 1) as p:
                        part(ring, p, p, this, nxt)
                else:
                    part(ring, 0, PAIRS - 1 if this else -1, this, nxt)

        def attention(tag, s, wq, wk, wv, wo, normed, group, neg, end):
            h = {k: Handoff(f"{tag}_{k}", 2) for k in ("arg", "exp", "prob")}
            if normed:
                h["var"] = Handoff(f"{tag}_variances", 1)
                h["root"] = Handoff(f"{tag}_roots", 1)
                h["scaled"] = Handoff(f"{tag}_scaled", 2)
            wq, wk, wv = (w(n).rearrange("p (c f) -> p c f", f=P) for n in (wq, wk, wv))
            wo = w(wo).rearrange("p (c f) -> p c f", f=D)
            scale = 64.0 ** -0.5
            vsrc = xs if tag == "sa" else cs
            tokw = W[:, wcol["m0_up"][0]:wcol["m0_up"][0] + 2048], W[:, wcol["m0_down"][0]:wcol["m0_down"][0] + 2048]

            def tok(u, k):
                return tokw[k][:, 1024 * u:1024 * u + 1024]

            def squares(u, k):
                return work[:, 2048 * k + 1024 * u:2048 * k + 1024 * u + 1024]

            def scores(pe, s, i, u):
                for half in range(2):
                    name = f"s{u}{half}"
                    pe.wait_ge(*s.bank_free(i, name))
                    settle(pe)
                    bk = bank(s.bank(name))
                    for c in range(4):
                        hp = 4 * half + c
                        for b in range(2):
                            for par in range(2):
                                r0, t0 = par * S, (2 * u + b) * S
                                ins = pe.matmul(bk[r0:r0 + S, (2 * c + b) * S:(2 * c + b + 1) * S],
                                                qT[r0:r0 + S, hp, t0:t0 + S], kT[r0:r0 + S, hp, t0:t0 + S],
                                                start=True, stop=True)
                    ins.then_inc(banks_filled, 1)

            def project(pe, s, i):
                if normed:
                    for u in range(2):
                        for c in range(4):
                            src, wt = (xs, wq) if c < 2 else (cs, wk)
                            pe.wait_ge(*s.bank_free(i, f"tok{u}{c}"))
                            pe.matmul(bank(s.bank(f"tok{u}{c}")), src[:, u * P:(u + 1) * P],
                                      wt[:, 4 * (c % 2):4 * (c % 2) + 4, :].rearrange("p c f -> p (c f)"),
                                      start=True, stop=True).then_inc(banks_filled, 1)
                    return
                for c in range(8):
                    wt, src = (wq, xs) if c < 4 else (wk, vsrc)
                    pe.wait_ge(*s.bank_free(i, f"qk{c}"))
                    for j in range(2):
                        ins = pe.matmul(bank(s.bank(f"qk{c}"))[:, j * PT:(j + 1) * PT],
                                        wt[:, 2 * (c % 4) + j, :], src[:], start=True, stop=True)
                    ins.then_inc(banks_filled, 1)

            def values(pe, s, i):
                for c in range(4):
                    u, n = c // 2, c % 2
                    pe.wait_ge(*s.bank_free(i, f"v{c}"))
                    pe.matmul(bank(s.bank(f"v{c}")), vsrc[:, u * P:(u + 1) * P],
                              wv[:, 4 * n:4 * n + 4, :].rearrange("p c f -> p (c f)"), start=True, stop=True) \
                        .then_inc(banks_filled, 1)
                pe.drain().then_inc(inputs_used, 1)

            def turn_qk(pe, s, i, p):
                for u in range(2):
                    pe.wait_ge(*h["scaled"].at(p, u + 1))
                    for c in range(4):
                        pe.wait_ge(*s.bank_free(i, f"turn{u}{c}"))
                        for j in range(4):
                            a = (4 * (c % 2) + j) * P
                            ins = pe.transpose(bank(s.bank(f"turn{u}{c}"))[:, j * P:(j + 1) * P],
                                               tok(u, c // 2)[:, a:a + P], ident[:])
                        ins.then_inc(banks_filled, 1)

            def mix(pe, s, i, u):
                pe.wait_ge(*s.emptied(i, f"p{u}1"))
                settle(pe)
                for b in range(2):
                    name = f"o{u}{b}"
                    pe.wait_ge(*s.bank_free(i, name))
                    settle(pe)
                    bk = bank(s.bank(name))
                    for hp in range(8):
                        for par in range(2):
                            ins = pe.matmul(bk[par * S:(par + 1) * S, hp * S:(hp + 1) * S],
                                            vv[b * S:(b + 1) * S, u, (2 * hp + par) * S:(2 * hp + par + 1) * S],
                                            pT[b * S:(b + 1) * S, u, hp, par * S:(par + 1) * S],
                                            start=True, stop=True)
                    ins.then_inc(banks_filled, 1)

            def tensor(pe):
                def result(ring, i):
                    for u in range(2):
                        if i is not None:
                            pe.wait_ge(*ring.emptied(i, f"o{u}1"))
                        for c in range(8):
                            ins = pe.matmul(ybank[:, u, :], oT[:, u, c, :], wo[:, c, :], start=(c == 0),
                                            stop=(c == 7))
                    ins.then_inc(y_filled, 1)

                def part(ring, i, p, this, nxt, last=True):
                    if this:
                        if ring is s.body:
                            pe.wait_ge(*ring.emptied_before(i, "turn12" if normed else "qk7"))
                            if normed:
                                pe.wait_ge(*ring.emptied_before(i, "turn13"))
                        settle(pe)
                        scores(pe, ring, i, 0)
                        scores(pe, ring, i, 1)
                    if nxt:
                        pe.wait_ge(staged, g_of(s, p) + 2 - PAIRS)
                        project(pe, ring, i)
                    if this:
                        probs_turned(pe, ring, i, p, 0, h)
                        probs_turned(pe, ring, i, p, 1, h)
                        if last:
                            if ring is s.body:
                                pe.wait_ge(*ring.emptied_before(i, "o11"))
                            result(ring, None)
                        mix(pe, ring, i, 0)
                        mix(pe, ring, i, 1)
                    if nxt:
                        values(pe, ring, i)
                    if nxt and normed:
                        turn_qk(pe, ring, i, p + 1)
                    if this:
                        turn_normed(pe, g_of(s, p))
                    if not nxt:
                        result(ring, i)
                pe.wait_ge(weights_in[group], 16)
                steps(pe, s, part)

            def scalar(act):
                def part(ring, i, p, this, nxt, last=True):
                    def projected(name):
                        if not nxt:
                            return
                        c = int(name[-1])
                        act.wait_ge(banks_filled, ring.filled(i, name))
                        if normed:
                            u, k, half = int(name[3]), c // 2, 512 * (c % 2)
                            act.activation(tok(u, k)[:, half:half + 512], bank(ring.bank(name)), ACT.Copy)
                            act.activation(squares(u, k)[:, half:half + 512], bank(ring.bank(name)), ACT.Square) \
                                .then_inc(act_emptied, 1)
                        else:
                            dst = (qT if c < 4 else kT)[:, 2 * (c % 4):2 * (c % 4) + 2, :]
                            act.activation(dst.rearrange("p c t -> p (c t)"), bank(ring.bank(name)), ACT.Copy) \
                                .then_inc(act_emptied, 1)

                    names = [n for n in s.pro.names if n.startswith("tok" if normed else "qk")]
                    for name in names[0:1]:
                        projected(name)
                    if this:
                        soft_exp(act, p, 0, scale, h)
                    for name in names[1:4]:
                        projected(name)
                    if this:
                        soft_exp(act, p, 1, scale, h)
                    for name in names[4:]:
                        projected(name)
                    if this:
                        store_probs(act, ring, i, 0)
                        store_probs(act, ring, i, 1)
                        for u in range(2):
                            for b in range(2):
                                act.wait_ge(banks_filled, ring.filled(i, f"o{u}{b}"))
                                act.activation(oT[:, u, :, b * S:(b + 1) * S],
                                               bank(ring.bank(f"o{u}{b}")).rearrange("p (c q) -> p c q", q=S),
                                               ACT.Copy).then_inc(act_emptied, 1)
                    if nxt:
                        if normed:
                            act.wait_ge(*h["var"].at(p + 1, 1))
                            act.activation(rsq, ssq, ACT.Ln)
                            act.drain()
                            act.activation(rsq, rsq, ACT.Exp, scale=-0.5).then_inc(h["root"].sem, 1)
                        if ring is s.pro and tag == "sa":
                            act.wait_ge(xn_ready, g_of(s, 0))
                        for c in range(4):
                            act.wait_ge(banks_filled, ring.filled(i, f"v{c}"))
                            act.activation(vv[:, c // 2, 512 * (c % 2):512 * (c % 2) + 512], bank(ring.bank(f"v{c}")),
                                           ACT.Copy).then_inc(act_emptied, 1)
                    if nxt and normed:
                        for u in range(2):
                            for c in (0, 2):
                                name = f"turn{u}{c}"
                                act.wait_ge(banks_filled, ring.filled(i, name))
                                dst = (qT if c < 2 else kT)[:, 0:4, u * P:(u + 1) * P]
                                act.activation(dst, bank(ring.bank(name)).rearrange("p (c t) -> p c t", t=P),
                                               ACT.Copy, scale=w("a1_norm")[:, c // 2:c // 2 + 1]) \
                                    .then_inc(act_emptied, 1)
                    if this:
                        store_turned(act, g_of(s, p), before(act, p))
                steps(act, s, part)

            def vector(v):
                def mean_squares(ring, i, p):
                    for u in range(2):
                        v.wait_ge(*ring.emptied(i, f"tok{u}3"))
                        for k in range(2):
                            v.reduce_sum(ssq[:, 32 * u + 16 * k:32 * u + 16 * k + 16],
                                         squares(u, k).rearrange("p (g e) -> p g e", e=64), AX)
                    v.drain()
                    v.tensor_scalar(ssq, ssq, 1.0 / 64, 1e-5, ALU.mult, ALU.add).then_inc(h["var"].sem, 1)

                def divide(p):
                    v.wait_ge(*h["root"].at(p, 1))
                    for u in range(2):
                        for k in range(2):
                            t3 = tok(u, k).rearrange("p (g e) -> p g e", e=64)
                            ins = v.tensor_tensor(t3, t3, rsq[:, 32 * u + 16 * k:32 * u + 16 * k + 16, None]
                                                  .to_broadcast([P, 16, 64]), ALU.mult)
                        ins.then_inc(h["scaled"].sem, 1)

                def turned(ring, i):
                    for u in range(2):
                        for c in (1, 3):
                            name = f"turn{u}{c}"
                            v.wait_ge(banks_filled, ring.filled(i, name))
                            dst = (qT if c < 2 else kT)[:, 4:8, u * P:(u + 1) * P]
                            v.tensor_scalar(dst, bank(ring.bank(name)).rearrange("p (c t) -> p c t", t=P),
                                            w("a1_norm")[:, c // 2:c // 2 + 1], None, ALU.mult) \
                                .then_inc(dve_emptied, 1)

                def step(ring, i, p, this, nxt, last=True):
                    v.drain()
                    if this:
                        soft_in(v, ring, i, p, 0, neg, h)
                        soft_in(v, ring, i, p, 1, neg, h)
                        soft_out(v, p, 0, h)
                        soft_out(v, p, 1, h)
                    if normed and nxt:
                        mean_squares(ring, i, p + 1)
                    if this and last:
                        end[0](v, s, p - 1)
                    if normed and nxt:
                        divide(p + 1)
                    if this and last:
                        end[1](v, s, p - 1)
                    if normed and nxt:
                        turned(ring, i)

                step(s.pro, 0, -1, False, True)
                step(s.body, 0, 0, True, True, last=False)
                with v.Fori(1, PAIRS - 1) as p:
                    step(s.body, p, p, True, True)
                step(s.epi, 0, PAIRS - 1, True, False)
                v.drain()
                end[0](v, s, PAIRS - 1)
                end[1](v, s, PAIRS - 1)

            return tensor, scalar, vector, None

        def end_residual(bias=None):
            def first_part(v, s, p):
                v.wait_ge(y_filled, p + yb(s))
                v.tensor_tensor(xr[:], ybank, pair(x_all, p), ALU.add)
                v.drain()
                if bias:
                    v.tensor_tensor(xr[:], xr[:], row(bias), ALU.add)
                    v.drain()
                v.tensor_copy(pair(x_all, p), xr[:])
                norm_stats(v, xr)

            def second_part(v, s, p):
                v.wait_ge(xt_filled, g_of(s, p) + BUMP)
                norm_apply(v, xr, xn, root(s, p, 1)).then_inc(xn_ready, 1)
            return first_part, second_part

        def end_decoder(gain, shift, bias):
            def first_part(v, s, p):
                v.wait_ge(y_filled, p + yb(s))
                v.tensor_tensor(xr[:], ybank, pair(tok_all, p), ALU.add)
                v.drain()
                v.tensor_tensor(xr[:], xr[:], row(bias), ALU.add)
                v.drain()
                norm_stats(v, xr)

            def second_part(v, s, p):
                v.wait_ge(xt_filled, g_of(s, p) + BUMP)
                norm_apply(v, xr, xn, root(s, p, 1))
                v.drain()
                v.tensor_tensor(xn[:], xn[:], row(gain), ALU.mult)
                v.drain()
                v.tensor_tensor(xn[:], xn[:], row(shift), ALU.add)
                v.drain()
                v.tensor_copy(pair(tok_all, p), xn[:]).then_inc(xn_ready, 1)
            return first_part, second_part

        def ffn_tensor(pe):
            s = ffn2
            with pe.Fori(0, PAIRS) as p:
                g = g_of(s, p)
                pe.wait_ge(staged, g + 1 - PAIRS)
                up_product(pe, s, p, w("fc1"), xs)
                pe.drain().then_inc(inputs_used, 1)
                turn_normed(pe, g)
                pe.wait_ge(*s.emptied(p, "up1"))
                down_product(pe, w("fc2"), hT)

        def up_product(pe, s, p, weights, src):
            wv = weights.rearrange("p (c f) -> p c f", f=P)
            for j in range(2):
                pe.wait_ge(*s.bank_free(p, f"up{j}"))
                for i in range(2):
                    ins = pe.matmul(bank(s.bank(f"up{j}"))[:, i * PT:(i + 1) * PT], wv[:, 2 * j + i, :], src[:],
                                    start=True, stop=True)
                ins.then_inc(banks_filled, 1)

        def down_product(pe, weights, hidden):
            wv = weights.rearrange("p (c f) -> p c f", f=D)
            for u in range(2):
                for c in range(4):
                    ins = pe.matmul(ybank[:, u, :], hidden[:, c, u * P:(u + 1) * P], wv[:, c, :], start=(c == 0),
                                    stop=(c == 3))
            ins.then_inc(y_filled, 1)

        def ffn_scalar(act):
            s = ffn2
            with act.Fori(0, PAIRS) as p:
                for j in range(2):
                    act.wait_ge(banks_filled, s.filled(p, f"up{j}"))
                    for i in range(2):
                        ins = act.activation(hT[:, 2 * j + i, :], bank(s.bank(f"up{j}"))[:, i * PT:(i + 1) * PT],
                                             ACT.Gelu, bias=w("fc1b")[:, 2 * j + i:2 * j + i + 1])
                    ins.then_inc(act_emptied, 1)
                store_turned(act, g_of(s, p), before(act, p))

        def ffn_vector(v):
            s = ffn2
            with v.Fori(0, PAIRS) as p:
                v.drain()
                v.wait_ge(y_filled, p + yb(s))
                v.tensor_tensor(xr[:], ybank, pair(tok_all, p), ALU.add)
                v.drain()
                v.tensor_tensor(xr[:], xr[:], row("fc2_b"), ALU.add)
                v.drain()
                norm_rows(v, xr, xr, root(s, p, 1))
                v.drain()
                v.tensor_tensor(xr[:], xr[:], row("ln3_g"), ALU.mult)
                v.drain()
                v.tensor_tensor(xr[:], xr[:], row("ln3_b"), ALU.add)
                v.drain()
                v.tensor_tensor(xr[:], xr[:], pair(x_all, p), ALU.add)
                finish(v, s, p, g_of(s, p))

        tq = work[:, 0:PT]
        tz = work[:, PT:2 * PT]
        tm = work[:, 2 * PT:3 * PT]
        tc = work[:, 3 * PT:4 * PT]
        td = work[:, 4 * PT:5 * PT]
        tern_ready = Handoff("tern_ready", 1)

        def tern_tensor(pe):
            s = tern
            with pe.Fori(0, PAIRS) as p:
                g = g_of(s, p)
                turn_normed(pe, g)
                pe.wait_ge(*tern_ready.at(p, 1))
                for u in range(2):
                    ins = pe.matmul(ybank[:, u, :], tz[:, u * P:(u + 1) * P], ternw[:], start=True, stop=True)
                ins.then_inc(y_filled, 1)

        def tern_scalar(act):
            with act.Fori(0, PAIRS) as p:
                store_turned(act, g_of(tern, p), before(act, p))

        def tern_vector(v):
            s = tern
            v.memset(tc, 1.0e4)
            v.memset(td, -1.0e4)
            with v.Fori(0, PAIRS) as p:
                v.drain()
                v.wait_ge(staged, g_of(s, p) + 1 - PAIRS)
                v.tensor_scalar(tq, xs[:], actscale[:, 1:2], ROUND, ALU.mult, ALU.add)
                v.drain()
                v.tensor_scalar(tq, tq, ROUND, -127.0, ALU.subtract, ALU.max).then_inc(inputs_used, 1)
                v.drain()
                v.tensor_scalar(tq, tq, 127.0, actscale[:, 0:1], ALU.min, ALU.mult)
                v.drain()
                v.memset(tz, 0.0)
                v.tensor_tensor(tm, tq, tq, ALU.is_equal)
                v.drain()
                v.copy_predicated(tz, tm.bitcast(U32), tq)
                v.drain()
                v.tensor_scalar(tm, tq, FLT_MAX, None, ALU.is_gt)
                v.drain()
                v.copy_predicated(tz, tm.bitcast(U32), tc)
                v.drain()
                v.tensor_scalar(tm, tq, -FLT_MAX, None, ALU.is_lt)
                v.drain()
                v.copy_predicated(tz, tm.bitcast(U32), td).then_inc(tern_ready.sem, 1)
                v.wait_ge(y_filled, p + yb(s))
                v.tensor_tensor(xr[:], ybank, pair(x_all, p), ALU.add)
                v.drain()
                v.tensor_tensor(xr[:], xr[:], row("tern_b"), ALU.add)
                finish(v, s, p, g_of(s, p))

        q3 = work[:, 0:256]
        k3 = work[:, 256:512]
        v3 = work[:, 512:1024]
        vx = work[:, 1024:1536].rearrange("p (u b n) -> p u b n", u=2, b=2)
        o3 = work[:, 1536:1792].rearrange("p (u d) -> p u d", u=2)
        o3T = work[:, 1792:2048]
        kx = work[:, 2048:6144].rearrange("p (u b h k) -> p u b h k", u=2, b=2, h=16)
        h3 = {k: Handoff(f"l3_{k}", 2) for k in ("arg", "exp", "prob")}
        h3["values"] = Handoff("l3_values", 1)
        h3["spread"] = Handoff("l3_spread", 2)
        end3 = end_residual("l3_bo")

        def att3_tensor(pe):
            s = att3

            def part(ring, i, p, this, nxt, last=True):
                if this:
                    for u in range(2):
                        pe.wait_ge(*h3["spread"].at(p, u + 1))
                        for half in range(2):
                            pe.wait_ge(*ring.bank_free(i, f"s{u}{half}"))
                            settle(pe)
                            for b in range(2):
                                t0 = (2 * u + b) * S
                                ins = pe.matmul(bank(ring.bank(f"s{u}{half}"))[b * S:(b + 1) * S, :],
                                                q3[:, t0:t0 + S],
                                                kx[:, u, b, 8 * half:8 * half + 8, :].rearrange("p h k -> p (h k)"),
                                                start=True, stop=True)
                            ins.then_inc(banks_filled, 1)
                if nxt:
                    pe.wait_ge(staged, g_of(s, p) + 2 - PAIRS)
                    pe.wait_ge(*ring.bank_free(i, "qk"))
                    bk = bank(ring.bank("qk"))
                    pe.matmul(bk[:, 0:PT], w("l3_wq"), xs[:], start=True, stop=True)
                    pe.matmul(bk[:, PT:2 * PT], w("l3_wk"), cs[:], start=True, stop=True).then_inc(banks_filled, 1)
                if this:
                    probs_turned(pe, ring, i, p, 0, h3)
                    probs_turned(pe, ring, i, p, 1, h3)
                    pe.wait_ge(*ring.bank_free(i, "o"))
                    settle(pe)
                    pe.wait_ge(*h3["values"].at(p, 1))
                    settle(pe)
                    for u in range(2):
                        pe.wait_ge(*ring.emptied(i, f"p{u}1"))
                        settle(pe)
                        for b in range(2):
                            for hp in range(8):
                                a = u * D + hp * 16
                                ins = pe.matmul(bank(ring.bank("o"))[b * S:(b + 1) * S, a:a + 16],
                                                pT[:, u, hp, b * S:(b + 1) * S], vx[:, u, b, hp * 16:hp * 16 + 16],
                                                start=True, stop=True)
                    ins.then_inc(banks_filled, 1)
                if nxt:
                    pe.wait_ge(*ring.bank_free(i, "v"))
                    settle(pe)
                    for c in range(4):
                        for half in range(2):
                            ins = pe.matmul(bank(ring.bank("v"))[half * S:(half + 1) * S, c * D:(c + 1) * D],
                                            cs[:, c * S:(c + 1) * S], w("l3_wv"), start=True, stop=True)
                    ins.then_inc(banks_filled, 1)
                    pe.drain().then_inc(inputs_used, 1)
                if this:
                    pe.wait_ge(*ring.emptied(i, "o"))
                    settle(pe)
                    pe.wait_ge(*ring.bank_free(i, "oT"))
                    for u in range(2):
                        ins = pe.transpose(bank(ring.bank("oT"))[:, u * P:(u + 1) * P], o3[:, u, :], ident[:])
                    ins.then_inc(banks_filled, 1)
                    turn_normed(pe, g_of(s, p))
                    pe.wait_ge(*ring.emptied(i, "oT"))
                    for u in range(2):
                        ins = pe.matmul(ybank[:, u, :], o3T[:, u * P:(u + 1) * P], w("l3_wo"), start=True, stop=True)
                    ins.then_inc(y_filled, 1)
            steps(pe, s, part)

        def att3_scalar(act):
            s = att3

            def part(ring, i, p, this, nxt, last=True):
                if nxt:
                    act.wait_ge(banks_filled, ring.filled(i, "qk"))
                    bk = bank(ring.bank("qk"))
                    act.activation(q3, bk[:, 0:PT], ACT.Identity, bias=w("l3_qkb")[:, 0:1])
                    act.activation(k3, bk[:, PT:2 * PT], ACT.Identity, bias=w("l3_qkb")[:, 1:2]) \
                        .then_inc(act_emptied, 1)
                if this:
                    soft_exp(act, p, 0, 8.0 ** -0.5, h3)
                    soft_exp(act, p, 1, 8.0 ** -0.5, h3)
                    store_probs(act, ring, i, 0)
                    store_probs(act, ring, i, 1)
                    act.wait_ge(banks_filled, ring.filled(i, "o"))
                    act.activation(o3.rearrange("p u d -> p (u d)"), bank(ring.bank("o"))[:, 0:PT], ACT.Copy) \
                        .then_inc(act_emptied, 1)
                    act.wait_ge(banks_filled, ring.filled(i, "oT"))
                    act.activation(o3T, bank(ring.bank("oT"))[:, 0:PT], ACT.Copy).then_inc(act_emptied, 1)
                    store_turned(act, g_of(s, p), before(act, p))
            steps(act, s, part)

        def att3_pool(g, ring, i, p):
            g.wait_ge(*ring.emptied(i, "qk"))
            for u in range(2):
                for b in range(2):
                    t0 = (2 * u + b) * S
                    ins = g.tensor_tensor(kx[:, u, b, :, :], k3[:, None, t0:t0 + S].to_broadcast([P, 16, S]),
                                          headmask[:, :, None].to_broadcast([P, 16, S]), ALU.mult)
                ins.then_inc(h3["spread"].sem, 1)

        def att3_vector(v):
            s = att3

            def step(ring, i, p, this, nxt, last=True):
                v.drain()
                if this:
                    soft_in(v, ring, i, p, 0, None, h3)
                    if last:
                        end3[0](v, s, p - 1)
                    soft_in(v, ring, i, p, 1, None, h3)
                    soft_out(v, p, 0, h3)
                    soft_out(v, p, 1, h3)
                    if last:
                        end3[1](v, s, p - 1)
                if nxt:
                    v.wait_ge(banks_filled, ring.filled(i, "v"))
                    v.tensor_tensor(v3.rearrange("p (c d) -> p c d", d=D),
                                    bank(ring.bank("v")).rearrange("p (c d) -> p c d", d=D), row("l3_bv", 4),
                                    ALU.add).then_inc(dve_emptied, 1)
                    v.drain()
                    v.tensor_tensor(vx.rearrange("p u b (c a e) -> p (u b c) a e", c=8, a=2),
                                    v3.rearrange("p (g a e) -> p g a e", a=2, e=8),
                                    parity[:, None, :, None].to_broadcast([P, 32, 2, 8]), ALU.mult)
                    v.drain().then_inc(h3["values"].sem, 1)

            step(s.pro, 0, -1, False, True)
            step(s.body, 0, 0, True, True, last=False)
            with v.Fori(1, PAIRS - 1) as p:
                step(s.body, p, p, True, True)
            step(s.epi, 0, PAIRS - 1, True, False)
            v.drain()
            end3[0](v, s, PAIRS - 1)
            end3[1](v, s, PAIRS - 1)

        hid = work[:, 0:4 * T].rearrange("p (c t) -> p c t", c=4)
        hq = work[:, 4 * T:4 * T + 4 * PT].rearrange("p (c t) -> p c t", c=4)
        wsc = work[:, 4 * T + 4 * PT:4 * T + 4 * PT + 1536]
        q_ready = Handoff("q_ready", 1) if layers == 8 else None
        hq_ready = Handoff("hq_ready", 1) if layers == 8 else None
        amax_asked = sem("amax_asked")
        amax_given = sem("amax_given")
        LAST = PAIRS * (len(run) - 1)

        def quant16(v, ap, src, sc, inv):
            v.tensor_scalar(ap, src, sc, ROUND, ALU.mult, ALU.add)
            v.drain()
            v.tensor_scalar(ap, ap, ROUND, -32768.0, ALU.subtract, ALU.max)
            v.drain()
            return v.tensor_scalar(ap, ap, 32767.0, inv, ALU.min, ALU.mult)

        def hid3_tensor(pe):
            s = hid3
            turn_normed(pe, LAST)
            with pe.Fori(0, PAIRS) as p:
                pe.wait_ge(*q_ready.at(p, 1))
                up_product(pe, s, p, w("l3_in"), xs)

        def hid3_scalar(act):
            s = hid3
            store_turned(act, LAST, PAIRS - 1)
            with act.Fori(0, PAIRS) as p:
                for j in range(2):
                    act.wait_ge(banks_filled, s.filled(p, f"up{j}"))
                    for i in range(2):
                        ins = act.activation(hid[:, 2 * j + i, bass.ds(PT * p, PT)],
                                             bank(s.bank(f"up{j}"))[:, i * PT:(i + 1) * PT],
                                             ACT.Gelu, bias=w("l3_inb")[:, 2 * j + i:2 * j + i + 1])
                    ins.then_inc(act_emptied, 1)

        def scales(v, m, sc, inv, top):
            v.tensor_scalar(m, m, 1e-8, None, ALU.max)
            v.drain()
            v.reciprocal(sc, m)
            v.tensor_scalar(inv, m, 1.0 / top, None, ALU.mult)
            v.drain()
            v.tensor_scalar(sc, sc, top, None, ALU.mult)
            v.drain()

        def hid3_vector(v):
            s = hid3
            v.wait_ge(weights_in[4], 16)
            wo4 = w("l3_out").rearrange("p (c f) -> p c f", f=D)
            v.tensor_reduce(amax[:, 4:8], wo4, AX, ALU.max, apply_absolute_value=True)
            v.drain()
            scales(v, amax[:, 4:8], amax[:, 8:12], amax[:, 12:16], 127.0)
            for c in range(4):
                v.tensor_scalar(wo4[:, c, :], wo4[:, c, :], amax[:, 8 + c:9 + c], ROUND, ALU.mult, ALU.add)
            v.drain()
            v.tensor_scalar(w("l3_out"), w("l3_out"), ROUND, -128.0, ALU.subtract, ALU.max)
            v.drain()
            for c in range(4):
                v.tensor_scalar(wo4[:, c, :], wo4[:, c, :], 127.0, amax[:, 12 + c:13 + c], ALU.min, ALU.mult)
            v.drain()
            v.wait_ge(amax_given, 1)
            m, sc, inv = (wsc[:, 512 * i:512 * i + 512] for i in range(3))
            scales(v, m, sc, inv, 127.0)
            v.tensor_tensor(w("l3_in"), w("l3_in"), sc, ALU.mult)
            v.drain()
            v.tensor_scalar(w("l3_in"), w("l3_in"), ROUND, None, ALU.add)
            v.drain()
            v.tensor_scalar(w("l3_in"), w("l3_in"), ROUND, -128.0, ALU.subtract, ALU.max)
            v.drain()
            v.tensor_scalar(w("l3_in"), w("l3_in"), 127.0, None, ALU.min)
            v.drain()
            v.tensor_tensor(w("l3_in"), w("l3_in"), inv, ALU.mult)
            v.wait_ge(xt_stored, LAST + 1)
            v.tensor_reduce(amax[:, 0:1], xT_all[:], AX, ALU.max, apply_absolute_value=True).then_inc(amax_asked, 1)
            v.wait_ge(amax_given, 2)
            scales(v, amax[:, 1:2], amax[:, 2:3], amax[:, 3:4], 32767.0)
            with v.Fori(0, PAIRS) as p:
                v.drain()
                v.wait_ge(banks_filled, s.filled(p, "up1") - 2)
                quant16(v, xs[:], cols(xT_all, p), amax[:, 2:3], amax[:, 3:4]).then_inc(q_ready.sem, 1)
                v.wait_ge(*s.emptied(p, "up1"))
                v.tensor_reduce(small[:, bass.ds(p, 1)], hid[:, :, bass.ds(PT * p, PT)], mybir.AxisListType.XY,
                                ALU.max, apply_absolute_value=True)
            v.drain()
            v.tensor_reduce(amax[:, 0:1], small[:, 0:PAIRS], AX, ALU.max).then_inc(amax_asked, 1)
            v.wait_ge(amax_given, 3)
            scales(v, amax[:, 1:2], amax[:, 2:3], amax[:, 3:4], 32767.0)

        def hid3_pool(g):
            g.wait_ge(weights_in[4], 16)
            g.partition_all_reduce(wsc[:, 0:512], w("l3_in"), P, ABSMAX).then_inc(amax_given, 1)
            for k in range(2):
                g.wait_ge(amax_asked, k + 1)
                g.partition_all_reduce(amax[:, 1:2], amax[:, 0:1], P, ABSMAX).then_inc(amax_given, 1)

        def out3_tensor(pe):
            with pe.Fori(0, PAIRS) as p:
                pe.wait_ge(*hq_ready.at(p, 1))
                down_product(pe, w("l3_out"), hq)

        def out3_vector(v):
            s = out3
            with v.Fori(0, PAIRS) as p:
                v.drain()
                quant16(v, hq, hid[:, :, bass.ds(PT * p, PT)], amax[:, 2:3], amax[:, 3:4]).then_inc(hq_ready.sem, 1)
                v.wait_ge(y_filled, p + yb(s))
                v.tensor_tensor(xr[:], ybank, pair(x_all, p), ALU.add)
                v.drain()
                v.tensor_tensor(pair(x_all, p), xr[:], row("l3_bout"), ALU.add).then_inc(out_ready, 1)

        prog = {}
        if lstm in run:
            for k, n in (("rows", 1), ("abs", 1), ("ln", 1), ("D", 1), ("hvar", 1), ("hroot", 1)):
                h_lstm[k] = Handoff("lstm_" + k, n)

            def lstm_pool(g, p):
                g.wait_ge(*h_lstm["hvar"].at(p, 1))
                g.tensor_tensor(lstm_hq, lstm_hs, nhalf[:, 0:8], ALU.pow).then_inc(h_lstm["hroot"].sem, 1)
            prog[lstm] = (lstm_tensor, lstm_scalar, lstm_vector, lstm_pool)
        if moe0 in run:
            prog[moe0] = moe("m0", moe0, "m0", 8, 2, ACT.Gelu, 0)
        if att1 in run:
            prog[att1] = attention("a1", att1, "a1_wq", "a1_wk", "a1_wv", "a1_wo", True, 2, neg_len, end_residual())
        if moe1 in run:
            prog[moe1] = moe("m1", moe1, "m1", 9, 1, ACT.Silu, 1)
        if satt in run:
            prog[satt] = attention("sa", satt, "sa_wq", "sa_wk", "sa_wv", "sa_wo", False, 4, neg_mask,
                                   end_decoder("ln1_g", "ln1_b", "sa_bo"))
            prog[catt] = attention("ca", catt, "ca_wq", "ca_wk", "ca_wv", "ca_wo", False, 4, neg_mask,
                                   end_decoder("ln2_g", "ln2_b", "ca_bo"))
            prog[ffn2] = (ffn_tensor, ffn_scalar, ffn_vector, None)
        if tern in run:
            prog[tern] = (tern_tensor, tern_scalar, tern_vector, None)
        if att3 in run:
            prog[att3] = (att3_tensor, att3_scalar, att3_vector, None)
        if hid3 in run:
            prog[hid3] = (hid3_tensor, hid3_scalar, hid3_vector, None)
            prog[out3] = (out3_tensor, lambda act: None, out3_vector, None)

        def stage_inputs(g, s, p):
            k = g_of(s, p)
            g.wait_ge(xt_stored, k + 2 - PAIRS)
            g.wait_ge(inputs_used, k + 1 - PAIRS)
            g.tensor_copy(xs[:], cols(xT_all, p))
            if s in (lstm, att1, catt, att3):
                g.tensor_copy(cs[:], cols(ctxT_all, p))
            if s is lstm:
                g.tensor_tensor(lstm_q, cols(xT_all, p)[:, None, :].to_broadcast([P, 4, PT]),
                                quarter[:, :, None].to_broadcast([P, 4, PT]), ALU.mult)
                g.tensor_copy(lstm_v[:, :, :, 0:32], pair(tok_all, p).rearrange("p u (h e) -> p u h e", h=4))
            g.drain().then_inc(staged, 1)

        def take_last(g, pending):
            s, early = pending
            if early:
                early(g, PAIRS - 1)
            for k in range(roots[s][1]):
                take_root(g, s, PAIRS - 1, k + 1)

        block = es.enter_context(nc.Block())

        @block.sync
        def _(sp):
            sp.dma_start(x_all[:], x_in.rearrange("(t p) d -> p t d", p=P)).then_inc(x_in_done, 16)
            bounds = ["gates", "m0_router", "a1_wq", "m1_router", "sa_wq", None]
            for i in range(5):
                a = wcol[bounds[i]][0]
                z = wcol[bounds[i + 1]][0] if bounds[i + 1] else WIDTH
                if i == 1:
                    sp.dma_start(ctxT_all[:], ctxT_in).then_inc(ctx_in_done, 16)
                    sp.dma_start(tok_all[:], ctx_in.rearrange("(t p) d -> p t d", p=P)).then_inc(ctx_in_done, 16)
                    sp.dma_start(rows[:], rows_in.partition_broadcast(P)).then_inc(rest_in, 16)
                    sp.dma_start(moeb[:], moeb_in).then_inc(rest_in, 16)
                    sp.dma_start(lens_i, lens_in.partition_broadcast(P)).then_inc(rest_in, 16)
                    sp.dma_start(mask_u8, mask_in.partition_broadcast(P)).then_inc(rest_in, 16)
                    sp.dma_start(tern_i, tern_in).then_inc(rest_in, 16)
                    sp.dma_start(actscale[:, 0:1], scale_in.partition_broadcast(P)).then_inc(rest_in, 16)
                sp.dma_start(W[:, a:z], wpack[:, a:z]).then_inc(weights_in[i], 16)
            if layers < 8:
                sp.wait_ge(xn_ready, PAIRS * len(stages_run))
                sp.dma_start(out.rearrange("(t p) d -> p t d", p=P), x_all[:]).then_inc(out_stored, 16)
                sp.wait_ge(out_stored, 16)
            else:
                with sp.Fori(0, PAIRS) as p:
                    sp.wait_ge(out_ready, p + 1)
                    sp.dma_start(out[bass.ds(PT * p, PT), :].rearrange("(u p) d -> p u d", p=P),
                                 pair(x_all, p)).then_inc(out_stored, 16)
                sp.wait_ge(out_stored, 16 * PAIRS)

        @block.gpsimd
        def _(g):
            g.memset(ident[:], 0.0)
            g.memset(nhalf[:], -0.5)
            g.memset(euler[:], 2.718281828459045)
            g.memset(headmask[:], 1.0)
            g.memset(causal[:], 0.0)
            g.iota(ix[:].rearrange("p u e -> p (u e)").bitcast(I32), [[1, 16]], base=0, channel_multiplier=0)
            g.drain()
            g.affine_select(out=ident[:], in_=ident[:], compare_op=ALU.not_equal, fill=1.0, base=0,
                            pattern=[[-1, P]], channel_multiplier=1)
            g.affine_select(out=headmask[:], in_=headmask[:], compare_op=ALU.is_ge, fill=0.0, base=0,
                            pattern=[[-8, 16]], channel_multiplier=1)
            g.drain()
            for b in range(2):
                g.affine_select(out=causal[b * S:(b + 1) * S, :], in_=causal[b * S:(b + 1) * S, :],
                                compare_op=ALU.is_ge, fill=-NEG, base=0, pattern=[[1, S]], channel_multiplier=-1)
                g.drain()
            g.tensor_copy(iota8[:], ix[:].rearrange("p u e -> p (u e)").bitcast(I32))
            g.iota(xs[:, 0:S].bitcast(I32), [[1, S]], base=0, channel_multiplier=0)
            g.drain()
            g.affine_select(out=headmask[:], in_=headmask[:], compare_op=ALU.is_ge, fill=0.0, base=7,
                            pattern=[[8, 16]], channel_multiplier=-1)
            g.tensor_copy(iseq[:], xs[:, 0:S].bitcast(I32))
            g.memset(lstm_v[:, :, :, 32:33], 1.0)
            g.drain()
            g.drain().then_inc(consts_made, 1)
            g.drain().then_inc(inputs_used, 1)
            g.wait_ge(ctx_in_done, 32)
            g.wait_ge(converted, 1)
            with g.Fori(0, PAIRS - 1) as p:
                take_root(g, first, p, 1)
            pending = (first, None)
            for s in run + [None]:
                if s in (hid3, out3):
                    if s is hid3:
                        take_last(g, pending)
                        hid3_pool(g)
                        pending = None
                    continue
                if s is None:
                    if pending:
                        take_last(g, pending)
                    continue
                if pending[1]:
                    pending[1](g, PAIRS - 1)
                stage_inputs(g, s, 0)
                take_last(g, (pending[0], None))
                if s in (att1, satt, catt, att3):
                    if s is att3:
                        att3_pool(g, s.pro, 0, 0)
                    stage_inputs(g, s, 1)
                    if s is att3:
                        att3_pool(g, s.body, 0, 1)
                    with g.Fori(1, PAIRS - 1) as p:
                        stage_inputs(g, s, p + 1)
                        take_root(g, s, p - 1, 1)
                        if s is att3:
                            att3_pool(g, s.body, p, p + 1)
                    take_root(g, s, PAIRS - 2, 1)
                    pending = (s, None)
                    continue
                early = prog[s][3]
                with g.Fori(0, PAIRS - 1) as p:
                    if early:
                        early(g, p)
                    stage_inputs(g, s, p + 1)
                    for k in range(roots[s][1]):
                        take_root(g, s, p, k + 1)
                pending = (s, early)

        @block.vector
        def _(v):
            v.memset(parity[:], 0.0)
            v.memset(restart[:], 1.0)
            v.memset(restart_neg[:], 0.0)
            v.drain()
            v.memset(parity[0:S, 0:1], 1.0)
            v.memset(parity[S:P, 1:2], 1.0)
            v.memset(quarter[:], 0.0)
            v.drain()
            for h in range(4):
                v.memset(quarter[32 * h:32 * h + 32, h:h + 1], 1.0)
            v.memset(restart[:, 0:PT:S], 0.0)
            v.memset(restart_neg[:, 0:PT:S], -NEG)
            v.wait_ge(consts_made, 1)
            v.reduce_sum(row1[:], ident[:, 0:P:32], AX)
            v.reduce_sum(row2[:], ident[:, 1:P:32], AX)
            v.tensor_copy(row1h[:], ident[:, 0:P:32])
            v.tensor_scalar(negrow2[:], ident[:, 1:P:32], -1.0, None, ALU.mult)
            v.wait_ge(rest_in, 96)
            v.tensor_copy(lensf[:], lens_i)
            v.tensor_scalar(actscale[:, 0:1], actscale[:, 0:1], 1e-5, None, ALU.max)
            v.tensor_copy(ternw[:], tern_i)
            v.drain()
            v.reciprocal(actscale[:, 1:2], actscale[:, 0:1])
            v.tensor_scalar(ternw[:], ternw[:], -1.0, None, ALU.add)
            v.tensor_tensor(neg_len[:].rearrange("p (b k) -> p b k", k=S), iseq[:, None, :].to_broadcast([P, B, S]),
                            lensf[:, :, None].to_broadcast([P, B, S]), ALU.is_ge)
            v.tensor_scalar(neg_mask[:], mask_u8, -NEG, None, ALU.mult)
            v.drain()
            v.tensor_scalar(neg_len[:], neg_len[:], -NEG, None, ALU.mult)
            v.drain().then_inc(converted, 1)
            v.drain().then_inc(xt_filled, BUMP)
            v.drain().then_inc(dve_emptied, BUMP)
            first_vector(v)
            for s in run:
                prog[s][2](v)

        @block.scalar
        def _(act):
            act.drain().then_inc(xt_stored, 1)
            act.drain().then_inc(act_emptied, BUMP)
            with act.Fori(0, PAIRS - 1) as p:
                store_turned(act, p + 1, p)
            for s in run:
                prog[s][1](act)

        @block.tensor
        def _(pe):
            pe.wait_ge(consts_made, 1)
            with pe.Fori(0, PAIRS - 1) as p:
                turn_normed(pe, p + 1)
            for s in run:
                pe.wait_ge(act_emptied, s.base["a"])
                pe.wait_ge(dve_emptied, s.base["v"])
                prog[s][0](pe)


def pack(i):
    import numpy as np

    def chunks(a, n):
        return np.asarray(a).reshape(n, P, -1).transpose(1, 0, 2).reshape(P, -1)

    a = {k: np.asarray(v) for k, v in i.items()}
    ig, fg = a["L0_xattn_igate_w"], a["L0_xattn_fgate_w"]
    parts = {
        "gates": np.concatenate([np.repeat(g[:, 128 * k:128 * k + 128].T, 32, axis=1) for g in (ig, fg)
                                 for k in range(3)], axis=1),
        "gate_bias": np.stack([np.repeat(a["L0_xattn_igate_b"], 32), np.repeat(a["L0_xattn_fgate_b"], 32)], axis=1),
        "m0_router": a["L0_ffn_router_w"].T,
        "m0_up": a["L0_ffn_w1"].transpose(2, 0, 1).reshape(P, -1),
        "m0_upb": a["L0_ffn_b1"].reshape(16, P).T,
        "m0_down": chunks(a["L0_ffn_w2"].transpose(0, 2, 1).reshape(2048, P), 16),
        "a1_wq": a["L1_xattn_Wq"], "a1_wk": a["L1_xattn_Wk"], "a1_wv": a["L1_xattn_Wv"],
        "a1_wo": chunks(a["L1_xattn_Wo"], 8),
        "a1_norm": np.stack([np.tile(a["L1_xattn_q_norm_w"], 2), np.tile(a["L1_xattn_k_norm_w"], 2)], axis=1),
        "m1_router": a["L1_ffn_gate_w"].T,
        "m1_up": np.concatenate([chunks(a["L1_ffn_up_w"].reshape(1024, P), 8), a["L1_ffn_sh_up_w"]], axis=1),
        "m1_upb": np.concatenate([a["L1_ffn_up_b"], a["L1_ffn_sh_up_b"][None]]).T,
        "m1_down": np.concatenate([chunks(a["L1_ffn_down_w"].reshape(1024, P), 8), a["L1_ffn_sh_down_w"]], axis=1),
        "sa_wq": a["L2_xattn_sa_wq"], "sa_wk": a["L2_xattn_sa_wk"], "sa_wv": a["L2_xattn_sa_wv"],
        "sa_wo": chunks(a["L2_xattn_sa_wo"], 8),
        "ca_wq": a["L2_xattn_ca_wq"], "ca_wk": a["L2_xattn_ca_wk"], "ca_wv": a["L2_xattn_ca_wv"],
        "ca_wo": chunks(a["L2_xattn_ca_wo"], 8),
        "fc1": a["L2_xattn_fc1_w"], "fc1b": a["L2_xattn_fc1_b"].reshape(4, P).T, "fc2": chunks(a["L2_xattn_fc2_w"], 4),
        "l3_wq": a["L3_xattn_Wq"].T, "l3_wk": a["L3_xattn_Wk"].T, "l3_wv": a["L3_xattn_Wv"].T,
        "l3_wo": a["L3_xattn_Wo"].T, "l3_qkb": np.stack([a["L3_xattn_bq"], a["L3_xattn_bk"]], axis=1),
        "l3_in": a["L3_ffn_W_in"], "l3_inb": a["L3_ffn_b_in"].reshape(4, P).T, "l3_out": chunks(a["L3_ffn_W_out"], 4),
    }
    rows = {"out_w": "L0_xattn_out_w", "sa_bo": "L2_xattn_sa_bo", "ca_bo": "L2_xattn_ca_bo", "fc2_b": "L2_xattn_fc2_b",
            "tern_b": "L2_ffn_bias", "l3_bv": "L3_xattn_bv", "l3_bo": "L3_xattn_bo", "l3_bout": "L3_ffn_b_out"}
    for k in "123":
        rows[f"ln{k}_g"], rows[f"ln{k}_b"] = f"L2_xattn_ln{k}_g", f"L2_xattn_ln{k}_b"
    moeb = np.zeros((9, 2, D), np.float32)
    moeb[0:8, 0] = a["L0_ffn_b2"]
    moeb[0:8, 1] = a["L1_ffn_down_b"]
    moeb[8, 1] = a["L1_ffn_sh_down_b"]
    ctx = a["ctx_1024"].reshape(T, D)
    return {
        "wpack": np.concatenate([parts[n] for n, _ in SECTIONS], axis=1),
        "x_in": a["x"].reshape(T, D), "ctx_in": ctx, "ctxT_in": ctx.T,
        "rows_in": np.stack([a[rows[n]] for n in ROWS]), "moeb_in": moeb,
        "lens_in": a["_lenS2"], "mask_in": a["mask_BxS2_bk0"].reshape(T),
        "tern_in": a["L2_ffn_ternary_weight"].T, "scale_in": a["L2_ffn_act_scale"].reshape(1),
    }


LAYERS = 8


def kernel(**inputs):
    import numpy as np
    import concourse.bacc as bacc
    from concourse.bass_utils import run_bass_kernel_spmd

    nc = bacc.Bacc("TRN2", target_bir_lowering=False, num_devices=1)
    arrays = {k: np.ascontiguousarray(v) for k, v in pack(inputs).items()}
    aps = [nc.dram_tensor(k, v.shape, mybir.dt.from_np(v.dtype), kind="ExternalInput").ap() for k, v in arrays.items()]
    out = nc.dram_tensor("out", (T, D), F32, kind="ExternalOutput").ap()
    build_program(nc, *aps, out, layers=LAYERS)
    r = run_bass_kernel_spmd(nc, [arrays], core_ids=[0])
    return r.results[0]["out"].reshape(B, S, D)
```

```python
from contextlib import ExitStack

import concourse.bass as bass
from concourse import mybir

F32 = mybir.dt.float32
I32 = mybir.dt.int32
U32 = mybir.dt.uint32
U8 = mybir.dt.uint8
ALU = mybir.AluOpType
ACT = mybir.ActivationFunctionType
AX = mybir.AxisListType.X
ABSMAX = bass.bass_isa.ReduceOp.absmax

P = 128
B, S, D = 32, 64, 128
T = B * S
TILES = T // P
PAIRS = TILES // 2
PT = 2 * P
NEG = 3.0e38
ROUND = 12582912.0
FLT_MAX = 3.4028234663852886e38
BUMP = 64

SECTIONS = [
    ("gates", 768), ("gate_bias", 2),
    ("m0_router", 8), ("m0_up", 2048), ("m0_upb", 16), ("m0_down", 2048),
    ("a1_wq", 1024), ("a1_wk", 1024), ("a1_wv", 1024), ("a1_wo", 1024), ("a1_norm", 2),
    ("m1_router", 8), ("m1_up", 1152), ("m1_upb", 9), ("m1_down", 1152),
    ("sa_wq", 1024), ("sa_wk", 1024), ("sa_wv", 1024), ("sa_wo", 1024),
    ("ca_wq", 1024), ("ca_wk", 1024), ("ca_wv", 1024), ("ca_wo", 1024),
    ("fc1", 512), ("fc1b", 4), ("fc2", 512),
    ("l3_wq", 128), ("l3_wk", 128), ("l3_wv", 128), ("l3_wo", 128), ("l3_qkb", 2),
    ("l3_in", 512), ("l3_inb", 4), ("l3_out", 512),
]
WIDTH = sum(n for _, n in SECTIONS)
ROWS = ["out_w", "sa_bo", "ca_bo", "ln1_g", "ln1_b", "ln2_g", "ln2_b", "ln3_g", "ln3_b", "fc2_b",
        "tern_b", "l3_bv", "l3_bo", "l3_bout"]


class Stage:

    def __init__(self, index, units, before, sems, reps=PAIRS, ring=6):
        self.index, self.units, self.reps = index, units, reps
        self.names = [n for n, _ in units]
        self.sems = sems
        self.filled0, self.base = (before.filled0 + len(before.units) * before.reps, {
            e: before.base[e] + before.per[e] * before.reps for e in "av"}) if before else (0, {"a": BUMP, "v": BUMP})
        self.per = {e: sum(1 for _, k in units if k == e) for e in "av"}
        self.ring = ring

    def bank(self, name):
        return self.names.index(name) % self.ring

    def filled(self, p, name):
        return p * len(self.units) + (self.filled0 + self.names.index(name) + 1)

    def _emptied(self, p, j, back):
        e = self.units[j][1]
        order = sum(1 for _, k in self.units[:j + 1] if k == e)
        return self.sems[e], p * self.per[e] + (self.base[e] + order - back * self.per[e])

    def emptied(self, p, name):
        return self._emptied(p, self.names.index(name), 0)

    def emptied_before(self, p, name):
        return self._emptied(p, self.names.index(name), 1)

    def bank_free(self, p, name):
        j = self.names.index(name)
        if j >= self.ring:
            return self._emptied(p, j - self.ring, 0)
        last = max(k for k in range(len(self.units)) if k % self.ring == j % self.ring)
        return self._emptied(p, last, 1)


def build_program(nc, wpack, x_in, ctx_in, ctxT_in, rows_in, moeb_in, lens_in, mask_in, tern_in, scale_in, out,
                  layers=8):
    es = ExitStack()
    with es:
        def sb(name, shape, dt=F32):
            return es.enter_context(nc.sbuf_tensor(name, shape, dt))

        def sem(name):
            return es.enter_context(nc.semaphore(name))

        W = sb("weights", [P, WIDTH])
        wcol, at = {}, 0
        for name, n in SECTIONS:
            wcol[name] = (at, n)
            at += n

        def w(name):
            a, n = wcol[name]
            return W[:, a:a + n]

        x_all = sb("x_all", [P, TILES, D])
        xT_all = sb("xT_all", [P, T])
        ctxT_all = sb("ctxT_all", [P, T])
        tok_all = sb("tok_all", [P, TILES, D])
        neg_len = sb("neg_len", [P, T])
        neg_mask = sb("neg_mask", [P, T])
        rows = sb("rows", [P, len(ROWS), D])
        moeb = sb("moeb", [9, 2, D])
        ternw = sb("ternw", [P, D])
        ident = sb("ident", [P, P])
        xs = sb("xs", [P, PT])
        cs = sb("cs", [P, PT])
        xn = sb("xn", [P, 2, D])
        xr = sb("xr", [P, 2, D])
        st = sb("st", [P, 2, 6])
        mv = sb("mv", [P, 2, 2])
        var = sb("var", [P, 2])
        rstd = sb("rstd", [P, 2])
        nhalf = sb("nhalf", [P, 32])
        euler = sb("euler", [P, 16])
        work = sb("work", [P, 12288])
        small = sb("small", [P, 512])
        iota8 = sb("iota8", [P, 16])
        ix = sb("ix", [P, 2, 8], U32)
        row1 = sb("row1", [P, 1])
        row2 = sb("row2", [P, 1])
        row1h = sb("row1h", [P, 4])
        negrow2 = sb("negrow2", [P, 4])
        quarter = sb("quarter", [P, 4])
        parity = sb("parity", [P, 2])
        headmask = sb("headmask", [P, 16])
        causal = sb("causal", [P, S])
        restart = sb("restart", [P, PT])
        restart_neg = sb("restart_neg", [P, PT])
        iseq = sb("iseq", [P, S])
        lensf = sb("lensf", [P, B])
        actscale = sb("actscale", [P, 2])
        amax = sb("amax", [P, 16])
        warm = sb("warm", [P, 2])
        big = es.enter_context(nc.psum_tensor("banks", [P, 8, 512], F32))

        def bank(i):
            return big[:, i, :]

        ybank = bank(6)[:, 0:PT].rearrange("p (u d) -> p u d", u=2)
        xtbank = bank(7)[:, 0:PT]
        lens_i = work[:, 10240:10240 + B].bitcast(I32)
        mask_u8 = work[:, 11264:11264 + T // 4].bitcast(U8)
        tern_i = work[:, 10304:10304 + D].bitcast(I32)

        def row(name, n=2):
            i = ROWS.index(name)
            return rows[:, i:i + 1, :].to_broadcast([P, n, D])

        def pair(ap3, p):
            return ap3[:, bass.ds(2 * p, 2), :]

        def cols(ap2, p):
            return ap2[:, bass.ds(PT * p, PT)]

        weights_in = [sem(f"weights_in{i}") for i in range(5)]
        x_in_done = sem("x_in_done")
        ctx_in_done = sem("ctx_in_done")
        rest_in = sem("rest_in")
        consts_made = sem("consts_made")
        converted = sem("converted")
        banks_filled = sem("banks_filled")
        act_emptied = sem("act_emptied")
        dve_emptied = sem("dve_emptied")
        y_filled = sem("y_filled")
        xn_ready = sem("xn_ready")
        xt_filled = sem("xt_filled")
        xt_stored = sem("xt_stored")
        staged = sem("staged")
        inputs_used = sem("inputs_used")
        var_ready = sem("var_ready")
        rstd_ready = sem("rstd_ready")
        gates_merged = sem("gates_merged")
        out_ready = sem("out_ready")
        out_stored = sem("out_stored")
        sems = {"a": act_emptied, "v": dve_emptied}

        stages = []

        def stage(units, reps=PAIRS):
            s = Stage(len(stages), units, stages[-1] if stages else None, sems, reps)
            stages.append(s)
            return s

        def pipelined(these, mixing, inputs, late, tail=[]):
            s = stage([])
            s.pro = stage(inputs + late, 1)
            s.body = stage(these + inputs + mixing + late + tail, PAIRS - 1)
            s.epi = stage(these + mixing + tail, 1)
            return s

        first = stage([("none", "a")])
        first.units = []
        first.per = {"a": 0, "v": 0}
        lstm = stage([])
        lstm_units = [("argD", "v"), ("maxD", "a"), ("qk", "v"), ("gates", "a"), ("num", "a")]
        lstm.pro = stage([("gates", "a")], 1)
        lstm.body = stage(lstm_units, PAIRS - 1)
        lstm.epi = stage([u for u in lstm_units if u[0] != "gates"], 1)

        def moe_units(nu, nd, lag):
            u = [("route", "v"), ("up0", "a"), ("up1", "a")]
            ups, downs = list(range(2, nu)), list(range(nd))
            per = nu / nd
            done = 2
            for d in downs:
                need = min(nu, int(per * (d + 1) + 0.99) + lag)
                while done < need:
                    u.append((f"up{done}", "a"))
                    done += 1
                if d == nd - 1:
                    u.append(("combT", "v"))
                u.append((f"down{d}", "v"))
            return u

        moe0 = stage(moe_units(8, 4, 2))
        scores4 = [(f"s{u}{half}", "v") for u in range(2) for half in range(2)]
        mixing8 = [(f"{k}{u}{n}", "a") for k in "po" for u in range(2) for n in range(2)]
        values4 = [(f"v{c}", "a") for c in range(4)]
        att1 = pipelined(scores4, mixing8, [(f"tok{u}{c}", "a") for u in range(2) for c in range(4)],
                         values4 + [(f"turn{u}{c}", "av"[c % 2]) for u in range(2) for c in range(4)])
        moe1 = stage(moe_units(5, 5, 2))
        satt = pipelined(scores4, mixing8, [(f"qk{c}", "a") for c in range(8)], values4)
        catt = pipelined(scores4, mixing8, [(f"qk{c}", "a") for c in range(8)], values4)
        ffn2 = stage([("up0", "a"), ("up1", "a")])
        tern = stage([])
        turned4 = [("p00", "a"), ("p01", "a"), ("p10", "a"), ("p11", "a")]
        att3 = stage([])
        att3.pro = stage([("qk", "a")], 1)
        att3.one = stage(scores4 + [("qk", "a"), ("v", "v")] + turned4, 1)
        att3.body = stage(scores4 + [("qk", "a"), ("o", "a"), ("v", "v"), ("oT", "a")] + turned4, PAIRS - 2)
        att3.epi = stage(scores4 + [("o", "a"), ("v", "v"), ("oT", "a")] + turned4 + [("o_last", "a"),
                                                                                  ("oT_last", "a")], 1)
        hid3 = stage([("up0", "a"), ("up1", "a")])
        out3 = stage([])

        plan = {0: [], 1: [lstm], 2: [moe0], 3: [att1], 4: [moe1], 5: [satt, catt, ffn2], 6: [tern], 7: [att3],
                8: [hid3, out3]}
        run = [s for k in range(layers + 1) for s in plan[k]]
        weight_group = {lstm: 0, moe0: 1, att1: 2, moe1: 3}

        class Handoff:
            def __init__(self, name, n):
                self.sem, self.n = sem(name), n

            def at(self, p, k):
                return self.sem, p * self.n + k

        def norm_stats(v, src):
            for u in range(2):
                v.bn_stats(st[:, u, :], src[:, u, :])
            v.drain()
            for u in range(2):
                v.bn_aggr(mv[:, u, :], st[:, u, :])
            v.drain()
            v.tensor_scalar(var[:], mv[:, :, 1], 1e-5, None, ALU.add).then_inc(var_ready, 1)

        def norm_apply(v, src, dst, value):
            v.wait_ge(rstd_ready, value)
            for u in range(2):
                ins = v.tensor_scalar(dst[:, u, :], src[:, u, :], mv[:, u, 0:1], rstd[:, u:u + 1],
                                      ALU.subtract, ALU.mult)
            return ins

        def norm_rows(v, src, dst, value):
            norm_stats(v, src)
            return norm_apply(v, src, dst, value)

        roots = {}
        count = 0
        for s in [first] + run:
            per = {ffn2: 2, lstm: 1}.get(s, 1)
            if s in (hid3, out3):
                per = 0
            roots[s] = (count, per)
            count += 1 if s is first else per * PAIRS

        def root(s, p, k):
            return p * roots[s][1] + (roots[s][0] + k)

        def take_root(g, s, p, k):
            g.wait_ge(var_ready, root(s, p, k))
            g.tensor_tensor(rstd[:], var[:], nhalf[:, 0:2], ALU.pow).then_inc(rstd_ready, 1)

        def store_normed(v, s, p):
            pass

        def turn_normed(pe, g):
            pe.wait_ge(xn_ready, g)
            pe.wait_ge(xt_stored, g)
            for u in range(2):
                ins = pe.transpose(xtbank[:, u * P:(u + 1) * P], xn[:, u, :], ident[:])
            ins.then_inc(xt_filled, 1)

        settled = sem("settled")

        def settle(pe):
            pe.sem_inc(settled, 1)

        def store_turned(act, g, p):
            act.wait_ge(xt_filled, g + BUMP)
            act.activation(cols(xT_all, p), xtbank, ACT.Copy).then_inc(xt_stored, 1)

        def g_of(s, p):
            return p + PAIRS * stages_run.index(s)

        stages_run = [first] + run

        def prev_pair(p):
            return p + (PAIRS - 1) if isinstance(p, int) else p + (PAIRS - 1)

        def before(eng, p):
            return eng.snap((p + (PAIRS - 1)) & (PAIRS - 1))

        st16 = small[:, 256:352].rearrange("p (t e) -> p t e", e=6)
        mv16 = small[:, 352:384].rearrange("p (t e) -> p t e", e=2)
        var16 = small[:, 384:400]
        rstd16 = small[:, 400:416]

        def first_vector(v):
            v.wait_ge(x_in_done, 16)
            for t in range(TILES):
                v.bn_stats(st16[:, t, :], x_all[:, t, :])
            v.drain()
            for t in range(TILES):
                v.bn_aggr(mv16[:, t, :], st16[:, t, :])
            v.drain()
            v.tensor_scalar(var16, mv16[:, :, 1], 1e-5, None, ALU.add).then_inc(var_ready, 1)
            v.wait_ge(weights_in[0], 16)
            gw = w("gates").rearrange("p (g k n) -> p g k n", g=2, k=3)
            v.tensor_tensor(gw[:, :, 1, :], gw[:, :, 1, :], gw[:, :, 2, :], ALU.add).then_inc(gates_merged, 1)
            v.wait_ge(rstd_ready, 1)
            for p in range(PAIRS):
                if p:
                    v.wait_ge(xt_filled, p + BUMP)
                for u in range(2):
                    t = 2 * p + u
                    ins = v.tensor_scalar(xn[:, u, :], x_all[:, t, :], mv16[:, t, 0:1], rstd16[:, t:t + 1],
                                          ALU.subtract, ALU.mult)
                ins.then_inc(xn_ready, 1)

        lstm_z = work[:, 0:256]
        lstm_e = work[:, 256:512]
        lstm_ig = work[:, 512:768]
        lstm_lf = work[:, 768:1024]
        lstm_cs = work[:, 1024:1280]
        lstm_g = work[:, 1280:1536]
        lstm_G = work[:, 1536:1792]
        lstm_m = work[:, 1792:2048]
        lstm_L = work[:, 2048:2304]
        lstm_R = work[:, 5120:6144].rearrange("p (h t) -> p h t", h=4)
        lstm_q = work[:, 6144:7168].rearrange("p (h t) -> p h t", h=4)
        lstm_D = work[:, 2560:3072]
        lstm_C = work[:, 3072:3584]
        lstm_v = work[:, 7168:7168 + 264].rearrange("p (u h e) -> p u h e", u=2, h=4)
        lstm_h = work[:, 4096:4096 + 264].rearrange("p (u h e) -> p (u h) e", u=2, h=4)
        lstm_n = work[:, 4608:4864].rearrange("p (g e) -> p g e", g=8)
        lstm_n2 = work[:, 4864:5120].rearrange("p (g e) -> p g e", g=8)
        lstm_hv = small[:, 0:8]
        lstm_hr = small[:, 8:16]
        lstm_hm = small[:, 16:24]
        lstm_hs = small[:, 24:32]
        lstm_hq = small[:, 32:40]
        lstm_em = small[:, 40:48]
        lstm_ow = work[:, 9472:9472 + PT].rearrange("p (u d) -> p u d", u=2)
        h_lstm = {}

        def steps_lstm(eng, part):
            s = lstm
            for ring, this, nxt in ((s.pro, False, True), (s.body, True, True), (s.epi, True, False)):
                if eng is nc.tensor:
                    eng.wait_ge(act_emptied, ring.base["a"])
                    eng.wait_ge(dve_emptied, ring.base["v"])
                if ring is s.body:
                    if eng is nc.vector:
                        part(ring, 0, 0, this, nxt, last=False)
                    with eng.Fori(1 if eng is nc.vector else 0, PAIRS - 1) as p:
                        part(ring, p, p, this, nxt)
                else:
                    part(ring, 0, PAIRS - 1 if this else -1, this, nxt)

        def lstm_tensor(pe):
            s = lstm
            gw = w("gates").rearrange("p (k n) -> p k n", k=6)

            def part(ring, i, p, this, nxt):
                if this:
                    pe.wait_ge(*h_lstm["operands"].at(p, 1))
                    pe.wait_ge(*h_lstm["rows"].at(p, 1))
                    settle(pe)
                    pe.wait_ge(*ring.bank_free(i, "argD"))
                    for u in range(2):
                        for b in range(2):
                            c = (2 * u + b) * S
                            ins = pe.matmul(bank(ring.bank("argD"))[b * S:(b + 1) * S, u * 256:(u + 1) * 256],
                                            lstm_L[:, c:c + S], lstm_R[:, :, c:c + S], start=True, stop=True)
                    ins.then_inc(banks_filled, 1)
                    pe.wait_ge(*ring.bank_free(i, "maxD"))
                    for u in range(2):
                        ins = pe.transpose(bank(ring.bank("maxD"))[:, u * P:(u + 1) * P],
                                           lstm_m[:, u * P:(u + 1) * P], ident[:])
                    ins.then_inc(banks_filled, 1)
                    pe.wait_ge(staged, g_of(s, p) + 1 - PAIRS)
                    settle(pe)
                    pe.wait_ge(*ring.bank_free(i, "qk"))
                    for u in range(2):
                        for b in range(2):
                            c = (2 * u + b) * S
                            ins = pe.matmul(bank(ring.bank("qk"))[b * S:(b + 1) * S, u * 256:(u + 1) * 256],
                                            cs[:, c:c + S], lstm_q[:, :, c:c + S], start=True, stop=True)
                    ins.then_inc(banks_filled, 1)
                    pe.drain().then_inc(inputs_used, 1)
                if nxt:
                    pe.wait_ge(xt_stored, g_of(s, p) + 3 - PAIRS)
                    settle(pe)
                    pe.wait_ge(*ring.bank_free(i, "gates"))
                    bk = bank(ring.bank("gates"))
                    for gate in range(2):
                        for k in range(2):
                            ins = pe.matmul(bk[:, gate * PT:(gate + 1) * PT], gw[:, 3 * gate + k, :],
                                            cols(ctxT_all if k else xT_all, p + 1), start=(k == 0), stop=(k == 1))
                    ins.then_inc(banks_filled, 1)
                if this:
                    pe.wait_ge(*ring.emptied(i, "qk"))
                    settle(pe)
                    pe.wait_ge(*ring.bank_free(i, "num"))
                    settle(pe)
                    bk = bank(ring.bank("num"))
                    for u in range(2):
                        for h in range(4):
                            for b in range(2):
                                a = (u * 4 + h) * 33
                                ins = pe.matmul(bk[b * S:(b + 1) * S, a:a + 33],
                                                lstm_C[b * S:(b + 1) * S, (u * 4 + h) * S:(u * 4 + h + 1) * S],
                                                lstm_v[b * S:(b + 1) * S, u, h, :],
                                                start=True, stop=True)
                    ins.then_inc(banks_filled, 1)
                    turn_normed(pe, g_of(s, p))

            pe.wait_ge(gates_merged, 1)
            pe.wait_ge(ctx_in_done, 32)
            steps_lstm(pe, part)

        def lstm_scalar(act):
            s = lstm

            def part(ring, i, p, this, nxt):
                if this:
                    act.wait_ge(*ring.emptied(i, "argD"))
                    act.wait_ge(banks_filled, ring.filled(i, "maxD"))
                    m8 = bank(ring.bank("maxD"))[:, 0:PT].rearrange("p (u h r) -> p u h r", u=2, h=4)
                    act.activation(lstm_em.rearrange("p (u h) -> p u h", u=2), m8[:, :, :, 0], ACT.Exp,
                                   scale=-1.0).then_inc(act_emptied, 1)
                    act.activation(lstm_D, lstm_D, ACT.Exp).then_inc(h_lstm["D"].sem, 1)
                if nxt:
                    act.wait_ge(banks_filled, ring.filled(i, "gates"))
                    bk = bank(ring.bank("gates"))
                    act.activation(lstm_ig, bk[:, 0:PT], ACT.Identity, bias=w("gate_bias")[:, 0:1])
                    act.activation(lstm_z, bk[:, PT:2 * PT], ACT.Identity,
                                   bias=w("gate_bias")[:, 1:2]).then_inc(act_emptied, 1)
                if nxt:
                    act.wait_ge(*h_lstm["abs"].at(p + 1, 1))
                    act.activation(lstm_e, lstm_e, ACT.Exp, scale=-1.0)
                    act.drain()
                    act.activation(lstm_e, lstm_e, ACT.Ln, bias=1.0).then_inc(h_lstm["ln"].sem, 1)
                if this:
                    act.wait_ge(banks_filled, ring.filled(i, "num"))
                    act.activation(lstm_h, bank(ring.bank("num"))[:, 0:264].rearrange("p (g e) -> p g e", e=33),
                                   ACT.Copy).then_inc(act_emptied, 1)
                if nxt:
                    act.activation(lstm_v[:, :, :, 0:32], pair(tok_all, p + 1).rearrange("p u (h e) -> p u h e", h=4),
                                   ACT.Copy)
                    act.wait_ge(*h_lstm["scans"].at(p + 1, 1))
                    act.activation(lstm_L, lstm_g, ACT.Identity, scale=row1[:], bias=row2[:])
                    for h in range(2):
                        ins = act.activation(lstm_R[:, h, :], lstm_G, ACT.Identity, scale=negrow2[:, h:h + 1],
                                             bias=row1h[:, h:h + 1])
                    ins.then_inc(h_lstm["operands"].sem, 1)
                    act.activation(warm[:, 1:2], warm[:, 0:1], ACT.Exp)
                if this:
                    store_turned(act, g_of(s, p), before(act, p))
            act.wait_ge(weights_in[0], 16)
            act.wait_ge(ctx_in_done, 32)
            steps_lstm(act, part)

        def lstm_vector(v):
            s = lstm

            def magnitude(ring, i, p):
                v.wait_ge(*ring.emptied(i, "gates"))
                v.scalar_tensor_tensor(out=lstm_e, in0=lstm_z, scalar=-1.0, in1=lstm_z, op0=ALU.mult,
                                       op1=ALU.max).then_inc(h_lstm["abs"].sem, 1)

            def scans(p):
                v.wait_ge(*h_lstm["ln"].at(p, 1))
                v.scalar_tensor_tensor(out=lstm_lf, in0=lstm_z, scalar=0.0, in1=lstm_e, op0=ALU.min,
                                       op1=ALU.subtract)
                v.drain()
                v.tensor_tensor_scan(lstm_cs, restart[:], lstm_lf, 0.0, ALU.mult, ALU.add)
                v.tensor_tensor(lstm_ig, lstm_ig, lstm_lf, ALU.add)
                v.drain()
                v.tensor_tensor(lstm_g, lstm_ig, lstm_cs, ALU.subtract)
                v.drain()
                v.tensor_tensor_scan(lstm_G, restart_neg[:], lstm_g, -NEG, ALU.add, ALU.max) \
                    .then_inc(h_lstm["scans"].sem, 1)
                v.drain()
                for h in range(2, 4):
                    v.tensor_scalar(lstm_R[:, h, :], lstm_G, negrow2[:, h:h + 1], row1h[:, h:h + 1], ALU.mult, ALU.add)
                v.tensor_tensor(lstm_m, lstm_cs, lstm_G, ALU.add).then_inc(h_lstm["rows"].sem, 1)

            def decayed(ring, i, p):
                v.wait_ge(banks_filled, ring.filled(i, "argD"))
                v.tensor_tensor(lstm_D.rearrange("p (g k) -> p g k", g=8),
                                bank(ring.bank("argD")).rearrange("p (g k) -> p g k", g=8),
                                causal[:, None, :].to_broadcast([P, 8, S]), ALU.add).then_inc(dve_emptied, 1)
                v.wait_ge(*h_lstm["D"].at(p, 1))
                v.wait_ge(banks_filled, ring.filled(i, "qk"))
                v.scalar_tensor_tensor(out=lstm_C, in0=bank(ring.bank("qk")), scalar=32.0 ** -0.5, in1=lstm_D,
                                       op0=ALU.mult, op1=ALU.mult).then_inc(dve_emptied, 1)

            def divided(ring, i, p):
                v.wait_ge(*ring.emptied(i, "num"))
                v.scalar_tensor_tensor(out=lstm_hv, in0=lstm_h[:, :, 32], scalar=-1.0, in1=lstm_h[:, :, 32],
                                       op0=ALU.mult, op1=ALU.max)
                v.drain()
                v.tensor_tensor(lstm_hv, lstm_hv, lstm_em, ALU.max)
                v.drain()
                v.tensor_scalar(lstm_hv, lstm_hv, 1e-8, None, ALU.add)
                v.drain()
                v.reciprocal(lstm_hr, lstm_hv)
                v.drain()
                v.tensor_tensor(lstm_n, lstm_h[:, :, 0:32], lstm_hr[:, :, None].to_broadcast([P, 8, 32]), ALU.mult)
                v.drain()
                v.reduce_sum(lstm_hm, lstm_n, AX)
                v.drain()
                v.tensor_scalar(lstm_hm, lstm_hm, 1.0 / 32, None, ALU.mult)
                v.drain()
                v.tensor_tensor(lstm_n, lstm_n, lstm_hm[:, :, None].to_broadcast([P, 8, 32]), ALU.subtract)
                v.drain()
                v.tensor_tensor(lstm_n2, lstm_n, lstm_n, ALU.mult)
                v.drain()
                v.reduce_sum(lstm_hs, lstm_n2, AX)
                v.drain()
                v.tensor_scalar(lstm_hs, lstm_hs, 1.0 / 32, 1e-5, ALU.mult, ALU.add).then_inc(h_lstm["hvar"].sem, 1)

            def scaled(p):
                v.wait_ge(*h_lstm["hroot"].at(p, 1))
                v.tensor_tensor(lstm_n, lstm_n, lstm_hq[:, :, None].to_broadcast([P, 8, 32]), ALU.mult)
                v.drain()
                v.tensor_tensor(lstm_n2, lstm_n, lstm_ow.rearrange("p u (h e) -> p (u h) e", h=4), ALU.mult)
                v.drain()
                v.tensor_tensor(xr[:], lstm_n2.rearrange("p (u h) e -> p u (h e)", u=2), pair(x_all, p), ALU.add)
                v.drain()
                v.tensor_copy(pair(x_all, p), xr[:])
                norm_stats(v, xr)

            def ending(p):
                v.wait_ge(xt_filled, g_of(s, p) + BUMP)
                norm_apply(v, xr, xn, root(s, p, 1)).then_inc(xn_ready, 1)

            def part(ring, i, p, this, nxt, last=True):
                v.drain()
                if this:
                    decayed(ring, i, p)
                if nxt:
                    magnitude(ring, i, p + 1)
                if this and last:
                    scaled(p - 1)
                if nxt:
                    scans(p + 1)
                if this:
                    if last:
                        ending(p - 1)
                    divided(ring, i, p)
            steps_lstm(v, part)
            scaled(PAIRS - 1)
            ending(PAIRS - 1)

        def finish(v, s, p, g, bias):
            v.drain()
            keep_stream(v, p, bias)
            v.wait_ge(xt_filled, g + BUMP)
            norm_rows(v, xr, xn, root(s, p, roots[s][1])).then_inc(xn_ready, 1)

        lg = small[:, 0:16].rearrange("p (u e) -> p u e", u=2)
        mx8 = small[:, 16:32].rearrange("p (u e) -> p u e", u=2)
        ds8 = small[:, 32:48].rearrange("p (u e) -> p u e", u=2)
        es8 = small[:, 48:64].rearrange("p (u e) -> p u e", u=2)
        idxf = small[:, 64:68].rearrange("p (u e) -> p u e", u=2)
        tsum = small[:, 68:70]
        wtop = small[:, 70:74].rearrange("p (u e) -> p u e", u=2)
        comb = small[:, 80:98].rearrange("p (u e) -> p u e", u=2)
        comb2 = small[:, 100:116].rearrange("p (u e) -> p u e", u=2)
        combT = small[:, 128:384]
        hT = work[:, 0:4096].rearrange("p (c t) -> p c t", t=PT)
        prod = work[:, 4096:4096 + 2304]

        def moe(tag, s, pre, experts, chunks, func, layer):
            nch = experts * chunks
            ups = [n for n in s.names if n.startswith("up")]
            downs = [n for n in s.names if n.startswith("down")]
            per_down = 2
            pr = prod[:, 0:2 * experts * D].rearrange("p (u e d) -> p u e d", u=2, e=experts)
            asked = Handoff(f"{tag}_exp_asked", 1)
            given = Handoff(f"{tag}_exp_given", 1)
            comb_ready = Handoff(f"{tag}_comb_ready", 1)
            upw = w(pre + "_up").rearrange("p (c f) -> p c f", f=P)
            dnw = w(pre + "_down").rearrange("p (c f) -> p c f", f=D)

            def tensor(pe):
                pe.wait_ge(weights_in[weight_group[s]], 16)
                with pe.Fori(0, PAIRS) as p:
                    g = g_of(s, p)
                    pe.wait_ge(staged, g + 1 - PAIRS)
                    for n, name in enumerate(s.names):
                        if name == "combT":
                            pe.wait_ge(*comb_ready.at(p, 1))
                        pe.wait_ge(*s.bank_free(p, name))
                        bk = bank(s.bank(name))
                        if name == "route":
                            for u in range(2):
                                ins = pe.matmul(bk[:, 8 * u:8 * u + 8], xs[:, u * P:(u + 1) * P], w(pre + "_router"),
                                                start=True, stop=True)
                        elif name == "combT":
                            for u in range(2):
                                ins = pe.transpose(bk[0:experts, u * P:(u + 1) * P], comb[:, u, 0:experts], ident[:])
                        elif name.startswith("up"):
                            j = int(name[2:])
                            for c in range(2 * j, min(2 * j + 2, nch)):
                                ins = pe.matmul(bk[:, (c % 2) * PT:(c % 2 + 1) * PT], upw[:, c, :], xs[:],
                                                start=True, stop=True)
                        else:
                            j = int(name[4:])
                            last = min((j + 1) * per_down * chunks, nch) - 1
                            settle(pe)
                            pe.wait_ge(*s.emptied(p, f"up{last // 2}"))
                            for u in range(2):
                                for e in range(2 * j, min(2 * j + 2, experts)):
                                    for c in range(chunks):
                                        ins = pe.matmul(bk[:, (2 * u + e % 2) * D:(2 * u + e % 2 + 1) * D],
                                                        hT[:, e * chunks + c, u * P:(u + 1) * P],
                                                        dnw[:, e * chunks + c, :], start=(c == 0),
                                                        stop=(c == chunks - 1))
                        ins.then_inc(banks_filled, 1)
                        if name == downs[-2]:
                            turn_normed(pe, g)
                    pe.drain().then_inc(inputs_used, 1)
                    pe.wait_ge(*s.emptied(p, "combT"))
                    for u in range(2):
                        ins = pe.matmul(ybank[:, u, :], combT[0:experts, u * P:(u + 1) * P],
                                        moeb[0:experts, layer, :], start=True, stop=True)
                    ins.then_inc(y_filled, 1)

            def scalar(act):
                with act.Fori(0, PAIRS) as p:
                    for name in ups:
                        j = int(name[2:])
                        act.wait_ge(banks_filled, s.filled(p, name))
                        for c in range(2 * j, min(2 * j + 2, nch)):
                            ins = act.activation(hT[:, c, :], bank(s.bank(name))[:, (c % 2) * PT:(c % 2 + 1) * PT],
                                                 func, bias=w(pre + "_upb")[:, c:c + 1])
                        ins.then_inc(act_emptied, 1)
                    store_turned(act, g_of(s, p), before(act, p))

            def vector(v):
                def sort(p):
                    v.wait_ge(banks_filled, s.filled(p, "route"))
                    v.tensor_copy(lg, bank(s.bank("route"))[:, 0:16].rearrange("p (u e) -> p u e", u=2)) \
                        .then_inc(dve_emptied, 1)
                    v.drain()
                    for u in range(2):
                        v.max(mx8[:, u, :], lg[:, u, :])
                    v.drain()
                    v.tensor_tensor(ds8, mx8, mx8[:, :, 0:1].to_broadcast([P, 2, 8]), ALU.subtract) \
                        .then_inc(asked.sem, 1)
                    for u in range(2):
                        v.max_index(ix[:, u, :], mx8[:, u, :], lg[:, u, :])
                    v.drain()
                    v.tensor_copy(idxf, ix[:, :, 0:2])

                def weigh(p):
                    v.wait_ge(*given.at(p, 1))
                    if experts == 9:
                        v.reduce_sum(tsum, es8, AX)
                        v.drain()
                        v.reciprocal(tsum, tsum)
                        v.drain()
                        v.tensor_tensor(wtop, es8[:, :, 0:2], tsum[:, :, None].to_broadcast([P, 2, 2]), ALU.mult)
                        v.drain()
                        v.tensor_tensor(tsum, wtop[:, :, 0], wtop[:, :, 1], ALU.add)
                        v.drain()
                        v.tensor_scalar(tsum, tsum, 1e-20, None, ALU.add)
                        top = wtop
                    else:
                        v.tensor_tensor(tsum, es8[:, :, 0], es8[:, :, 1], ALU.add)
                        top = es8[:, :, 0:2]
                    v.drain()
                    v.reciprocal(tsum, tsum)
                    v.drain()
                    v.tensor_tensor(wtop, top, tsum[:, :, None].to_broadcast([P, 2, 2]), ALU.mult)
                    v.drain()
                    for u in range(2):
                        v.tensor_scalar(comb[:, u, 0:8], iota8[:, 0:8], idxf[:, u, 0:1], wtop[:, u, 0:1],
                                        ALU.is_equal, ALU.mult)
                        v.tensor_scalar(comb2[:, u, :], iota8[:, 0:8], idxf[:, u, 1:2], wtop[:, u, 1:2],
                                        ALU.is_equal, ALU.mult)
                    v.drain()
                    v.tensor_tensor(comb[:, :, 0:8], comb[:, :, 0:8], comb2, ALU.add).then_inc(comb_ready.sem, 1)

                def combine(p):
                    v.drain()
                    for name in s.names[1:]:
                        if name.startswith("up"):
                            continue
                        v.wait_ge(banks_filled, s.filled(p, name))
                        if name == "combT":
                            v.tensor_copy(combT[0:experts, :], bank(s.bank(name))[0:experts, 0:PT]) \
                                .then_inc(dve_emptied, 1)
                            continue
                        j = int(name[4:])
                        n = min(2 * j + 2, experts) - 2 * j
                        bk = bank(s.bank(name)).rearrange("p (u e d) -> p u e d", u=2, e=2)
                        for u in range(2):
                            ins = v.tensor_tensor(pr[:, u, 2 * j:2 * j + n, :], bk[:, u, 0:n, :],
                                                  comb[:, u, 2 * j:2 * j + n, None].to_broadcast([P, n, D]), ALU.mult)
                        ins.then_inc(dve_emptied, 1)
                    v.drain()

                def add_up(p):
                    for u in range(2):
                        v.reduce_sum(xr[:, u, :], pr[:, u, :, :].rearrange("p e d -> p d e"), AX)
                    v.drain()
                    v.tensor_tensor(xr[:], xr[:], pair(x_all, p), ALU.add)
                    v.drain()
                    v.wait_ge(y_filled, p + yb(s))
                    v.tensor_tensor(xr[:], ybank, xr[:], ALU.add)
                    v.drain()
                    v.tensor_copy(pair(x_all, p), xr[:])
                    norm_stats(v, xr)

                def ending(p):
                    v.wait_ge(xt_filled, g_of(s, p) + BUMP)
                    ins = norm_apply(v, xr, xn, root(s, p, 1))
                    if layer == 1:
                        v.drain()
                        ins = v.tensor_tensor(pair(tok_all, p), xn[:], row("sa_bo"), ALU.add)
                    ins.then_inc(xn_ready, 1)

                def step(p, last=True):
                    v.drain()
                    sort(p)
                    if last:
                        add_up(p - 1)
                    weigh(p)
                    if last:
                        ending(p - 1)
                    combine(p)

                if experts == 9:
                    v.memset(comb[:, :, 8:9], 1.0)
                step(0, last=False)
                with v.Fori(1, PAIRS) as p:
                    step(p)
                add_up(PAIRS - 1)
                ending(PAIRS - 1)

            def pool(g, p):
                g.wait_ge(*asked.at(p, 1))
                g.tensor_tensor(es8, euler[:].rearrange("p (u e) -> p u e", u=2), ds8, ALU.pow).then_inc(given.sem, 1)

            return tensor, scalar, vector, pool

        ystages = [s for s in run if s is not lstm and s is not hid3]

        def yb(s):
            return ystages.index(s) * PAIRS + 1

        qT = work[:, 0:2048].rearrange("p (c t) -> p c t", t=PT)
        kT = work[:, 2048:4096].rearrange("p (c t) -> p c t", t=PT)
        vv = work[:, 4096:6144].rearrange("p (u n) -> p u n", u=2)
        sm = work[:, 6144:8192].rearrange("p (u n) -> p u n", u=2)
        pT = work[:, 8192:10240].rearrange("p (u c t) -> p u c t", u=2, c=8)
        oT = work[:, 10240:12288].rearrange("p (u c t) -> p u c t", u=2, c=8)
        mxs = small[:, 0:32].rearrange("p (u g) -> p u g", u=2)
        rs = small[:, 32:64].rearrange("p (u g) -> p u g", u=2)
        ssq = small[:, 64:128]
        rsq = small[:, 128:192]

        def soft_in(v, s, i, p, u, neg, h):
            every = sm[:, u, :].rearrange("p (g k) -> p g k", k=S)
            if neg is not None:
                for half in range(2):
                    v.wait_ge(banks_filled, s.filled(i, f"s{u}{half}"))
                    v.tensor_tensor(sm[:, u, 512 * half:512 * half + 512].rearrange("p (c k) -> p c k", k=P),
                                    bank(s.bank(f"s{u}{half}")).rearrange("p (c k) -> p c k", k=P),
                                    cols(neg, p)[:, None, u * P:(u + 1) * P].to_broadcast([P, 4, P]), ALU.add) \
                        .then_inc(dve_emptied, 1)
                v.drain()
                v.reduce_max(mxs[:, u, :], every, AX)
                v.drain()
                v.tensor_tensor(every, every, mxs[:, u, :, None].to_broadcast([P, 16, S]), ALU.subtract) \
                    .then_inc(h["arg"].sem, 1)
                return
            for half in range(2):
                v.wait_ge(banks_filled, s.filled(i, f"s{u}{half}"))
                v.reduce_max(mxs[:, u, 8 * half:8 * half + 8],
                             bank(s.bank(f"s{u}{half}")).rearrange("p (g k) -> p g k", k=S), AX)
            v.drain()
            for half in range(2):
                v.tensor_tensor(every[:, 8 * half:8 * half + 8, :],
                                bank(s.bank(f"s{u}{half}")).rearrange("p (g k) -> p g k", k=S),
                                mxs[:, u, 8 * half:8 * half + 8, None].to_broadcast([P, 8, S]), ALU.subtract) \
                    .then_inc(dve_emptied, 1)
            v.drain().then_inc(h["arg"].sem, 1)

        def soft_exp(act, p, u, scale, h):
            act.wait_ge(*h["arg"].at(p, u + 1))
            act.activation(sm[:, u, :], sm[:, u, :], ACT.Exp, scale=scale).then_inc(h["exp"].sem, 1)

        def soft_out(v, p, u, h):
            every = sm[:, u, :].rearrange("p (g k) -> p g k", k=S)
            v.wait_ge(*h["exp"].at(p, u + 1))
            v.reduce_sum(rs[:, u, :], every, AX)
            v.drain()
            v.reciprocal(rs[:, u, :], rs[:, u, :])
            v.drain()
            v.tensor_tensor(every, every, rs[:, u, :, None].to_broadcast([P, 16, S]), ALU.mult) \
                .then_inc(h["prob"].sem, 1)

        def probs_turned(pe, s, i, p, u, h):
            pe.wait_ge(*h["prob"].at(p, u + 1))
            for half in range(2):
                name = f"p{u}{half}"
                pe.wait_ge(*s.bank_free(i, name))
                for c in range(4):
                    ins = pe.transpose(bank(s.bank(name))[:, c * P:(c + 1) * P],
                                       sm[:, u, 512 * half + c * P:512 * half + (c + 1) * P], ident[:])
                ins.then_inc(banks_filled, 1)

        def store_probs(act, s, i, u):
            for half in range(2):
                act.wait_ge(banks_filled, s.filled(i, f"p{u}{half}"))
                act.activation(pT[:, u, 4 * half:4 * half + 4, :].rearrange("p c t -> p (c t)"),
                               bank(s.bank(f"p{u}{half}")), ACT.Copy).then_inc(act_emptied, 1)

        def steps(eng, s, part):
            for ring, this, nxt in ((s.pro, False, True), (s.body, True, True), (s.epi, True, False)):
                if eng is nc.tensor:
                    eng.wait_ge(act_emptied, ring.base["a"])
                    eng.wait_ge(dve_emptied, ring.base["v"])
                if ring is s.body:
                    part(ring, 0, 0, this, nxt, last=False)
                    with eng.Fori(1, PAIRS - 1) as p:
                        part(ring, p, p, this, nxt)
                else:
                    part(ring, 0, PAIRS - 1 if this else -1, this, nxt)

        def attention(tag, s, wq, wk, wv, wo, normed, group, neg, end):
            h = {k: Handoff(f"{tag}_{k}", 2) for k in ("arg", "exp", "prob")}
            if normed:
                h["var"] = Handoff(f"{tag}_variances", 1)
                h["root"] = Handoff(f"{tag}_roots", 1)
                h["scaled"] = Handoff(f"{tag}_scaled", 2)
            wq, wk, wv = (w(n).rearrange("p (c f) -> p c f", f=P) for n in (wq, wk, wv))
            wo = w(wo).rearrange("p (c f) -> p c f", f=D)
            scale = 64.0 ** -0.5
            vsrc = xs if tag == "sa" else cs
            tokw = W[:, wcol["m0_up"][0]:wcol["m0_up"][0] + 2048], W[:, wcol["m0_down"][0]:wcol["m0_down"][0] + 2048]

            def tok(u, k):
                return tokw[k][:, 1024 * u:1024 * u + 1024]

            def squares(u, k):
                return work[:, 2048 * k + 1024 * u:2048 * k + 1024 * u + 1024]

            def scores(pe, s, i, u):
                for half in range(2):
                    name = f"s{u}{half}"
                    pe.wait_ge(*s.bank_free(i, name))
                    settle(pe)
                    bk = bank(s.bank(name))
                    for c in range(4):
                        hp = 4 * half + c
                        for b in range(2):
                            for par in range(2):
                                r0, t0 = par * S, (2 * u + b) * S
                                ins = pe.matmul(bk[r0:r0 + S, (2 * c + b) * S:(2 * c + b + 1) * S],
                                                qT[r0:r0 + S, hp, t0:t0 + S], kT[r0:r0 + S, hp, t0:t0 + S],
                                                start=True, stop=True)
                    ins.then_inc(banks_filled, 1)

            def project(pe, s, i):
                if normed:
                    for u in range(2):
                        for c in range(4):
                            src, wt = (xs, wq) if c < 2 else (cs, wk)
                            pe.wait_ge(*s.bank_free(i, f"tok{u}{c}"))
                            pe.matmul(bank(s.bank(f"tok{u}{c}")), src[:, u * P:(u + 1) * P],
                                      wt[:, 4 * (c % 2):4 * (c % 2) + 4, :].rearrange("p c f -> p (c f)"),
                                      start=True, stop=True).then_inc(banks_filled, 1)
                    return
                for c in range(8):
                    wt, src = (wq, xs) if c < 4 else (wk, vsrc)
                    pe.wait_ge(*s.bank_free(i, f"qk{c}"))
                    for j in range(2):
                        ins = pe.matmul(bank(s.bank(f"qk{c}"))[:, j * PT:(j + 1) * PT],
                                        wt[:, 2 * (c % 4) + j, :], src[:], start=True, stop=True)
                    ins.then_inc(banks_filled, 1)

            def values(pe, s, i):
                for c in range(4):
                    u, n = c // 2, c % 2
                    pe.wait_ge(*s.bank_free(i, f"v{c}"))
                    pe.matmul(bank(s.bank(f"v{c}")), vsrc[:, u * P:(u + 1) * P],
                              wv[:, 4 * n:4 * n + 4, :].rearrange("p c f -> p (c f)"), start=True, stop=True) \
                        .then_inc(banks_filled, 1)
                pe.drain().then_inc(inputs_used, 1)

            def turn_qk(pe, s, i, p):
                for u in range(2):
                    pe.wait_ge(*h["scaled"].at(p, u + 1))
                    for c in range(4):
                        pe.wait_ge(*s.bank_free(i, f"turn{u}{c}"))
                        for j in range(4):
                            a = (4 * (c % 2) + j) * P
                            ins = pe.transpose(bank(s.bank(f"turn{u}{c}"))[:, j * P:(j + 1) * P],
                                               tok(u, c // 2)[:, a:a + P], ident[:])
                        ins.then_inc(banks_filled, 1)

            def mix(pe, s, i, u):
                pe.wait_ge(*s.emptied(i, f"p{u}1"))
                settle(pe)
                for b in range(2):
                    name = f"o{u}{b}"
                    pe.wait_ge(*s.bank_free(i, name))
                    settle(pe)
                    bk = bank(s.bank(name))
                    for hp in range(8):
                        for par in range(2):
                            ins = pe.matmul(bk[par * S:(par + 1) * S, hp * S:(hp + 1) * S],
                                            vv[b * S:(b + 1) * S, u, (2 * hp + par) * S:(2 * hp + par + 1) * S],
                                            pT[b * S:(b + 1) * S, u, hp, par * S:(par + 1) * S],
                                            start=True, stop=True)
                    ins.then_inc(banks_filled, 1)

            def tensor(pe):
                def result(ring, i):
                    for u in range(2):
                        if i is not None:
                            pe.wait_ge(*ring.emptied(i, f"o{u}1"))
                        for c in range(8):
                            ins = pe.matmul(ybank[:, u, :], oT[:, u, c, :], wo[:, c, :], start=(c == 0),
                                            stop=(c == 7))
                    ins.then_inc(y_filled, 1)

                def part(ring, i, p, this, nxt, last=True):
                    if this:
                        if ring is s.body:
                            pe.wait_ge(*ring.emptied_before(i, "turn12" if normed else "qk7"))
                            if normed:
                                pe.wait_ge(*ring.emptied_before(i, "turn13"))
                        settle(pe)
                        scores(pe, ring, i, 0)
                        scores(pe, ring, i, 1)
                    if nxt:
                        pe.wait_ge(staged, g_of(s, p) + 2 - PAIRS)
                        project(pe, ring, i)
                    if this:
                        if not nxt:
                            result(ring, None)
                        probs_turned(pe, ring, i, p, 0, h)
                        if last and nxt:
                            pe.wait_ge(*ring.emptied_before(i, "o11"))
                            result(ring, None)
                        probs_turned(pe, ring, i, p, 1, h)
                        mix(pe, ring, i, 0)
                        mix(pe, ring, i, 1)
                    if nxt:
                        values(pe, ring, i)
                    if nxt and normed:
                        turn_qk(pe, ring, i, p + 1)
                    if this:
                        turn_normed(pe, g_of(s, p))
                    if not nxt:
                        result(ring, i)
                pe.wait_ge(weights_in[group], 16)
                steps(pe, s, part)

            def scalar(act):
                def part(ring, i, p, this, nxt, last=True):
                    def projected(name):
                        if not nxt:
                            return
                        c = int(name[-1])
                        act.wait_ge(banks_filled, ring.filled(i, name))
                        if normed:
                            u, k, half = int(name[3]), c // 2, 512 * (c % 2)
                            act.activation(tok(u, k)[:, half:half + 512], bank(ring.bank(name)), ACT.Copy)
                            act.activation(squares(u, k)[:, half:half + 512], bank(ring.bank(name)), ACT.Square) \
                                .then_inc(act_emptied, 1)
                        else:
                            dst = (qT if c < 4 else kT)[:, 2 * (c % 4):2 * (c % 4) + 2, :]
                            act.activation(dst.rearrange("p c t -> p (c t)"), bank(ring.bank(name)), ACT.Copy) \
                                .then_inc(act_emptied, 1)

                    names = [n for n in s.pro.names if n.startswith("tok" if normed else "qk")]
                    for name in names[0:1]:
                        projected(name)
                    if this:
                        soft_exp(act, p, 0, scale, h)
                    for name in names[1:4]:
                        projected(name)
                    if this:
                        soft_exp(act, p, 1, scale, h)
                    for name in names[4:]:
                        projected(name)
                    if this:
                        store_probs(act, ring, i, 0)
                        store_probs(act, ring, i, 1)
                    if nxt:
                        if normed:
                            act.wait_ge(*h["var"].at(p + 1, 1))
                            act.activation(rsq, ssq, ACT.Ln)
                            act.drain()
                            act.activation(rsq, rsq, ACT.Exp, scale=-0.5).then_inc(h["root"].sem, 1)
                    if this:
                        for u in range(2):
                            for b in range(2):
                                act.wait_ge(banks_filled, ring.filled(i, f"o{u}{b}"))
                                act.activation(oT[:, u, :, b * S:(b + 1) * S],
                                               bank(ring.bank(f"o{u}{b}")).rearrange("p (c q) -> p c q", q=S),
                                               ACT.Copy).then_inc(act_emptied, 1)
                    if nxt:
                        if ring is s.pro and tag == "sa":
                            act.wait_ge(xn_ready, g_of(s, 0))
                        for c in range(4):
                            act.wait_ge(banks_filled, ring.filled(i, f"v{c}"))
                            act.activation(vv[:, c // 2, 512 * (c % 2):512 * (c % 2) + 512], bank(ring.bank(f"v{c}")),
                                           ACT.Copy).then_inc(act_emptied, 1)
                    if nxt and normed:
                        for u in range(2):
                            for c in (0, 2):
                                name = f"turn{u}{c}"
                                act.wait_ge(banks_filled, ring.filled(i, name))
                                dst = (qT if c < 2 else kT)[:, 0:4, u * P:(u + 1) * P]
                                act.activation(dst, bank(ring.bank(name)).rearrange("p (c t) -> p c t", t=P),
                                               ACT.Copy, scale=w("a1_norm")[:, c // 2:c // 2 + 1]) \
                                    .then_inc(act_emptied, 1)
                    if this:
                        store_turned(act, g_of(s, p), before(act, p))
                steps(act, s, part)

            def vector(v):
                def mean_squares(ring, i, p):
                    for u in range(2):
                        v.wait_ge(*ring.emptied(i, f"tok{u}3"))
                        for k in range(2):
                            v.reduce_sum(ssq[:, 32 * u + 16 * k:32 * u + 16 * k + 16],
                                         squares(u, k).rearrange("p (g e) -> p g e", e=64), AX)
                    v.drain()
                    v.tensor_scalar(ssq, ssq, 1.0 / 64, 1e-5, ALU.mult, ALU.add).then_inc(h["var"].sem, 1)

                def divide(p):
                    v.wait_ge(*h["root"].at(p, 1))
                    for u in range(2):
                        for k in range(2):
                            t3 = tok(u, k).rearrange("p (g e) -> p g e", e=64)
                            ins = v.tensor_tensor(t3, t3, rsq[:, 32 * u + 16 * k:32 * u + 16 * k + 16, None]
                                                  .to_broadcast([P, 16, 64]), ALU.mult)
                        ins.then_inc(h["scaled"].sem, 1)

                def turned(ring, i):
                    for u in range(2):
                        for c in (1, 3):
                            name = f"turn{u}{c}"
                            v.wait_ge(banks_filled, ring.filled(i, name))
                            dst = (qT if c < 2 else kT)[:, 4:8, u * P:(u + 1) * P]
                            v.tensor_scalar(dst, bank(ring.bank(name)).rearrange("p (c t) -> p c t", t=P),
                                            w("a1_norm")[:, c // 2:c // 2 + 1], None, ALU.mult) \
                                .then_inc(dve_emptied, 1)

                def step(ring, i, p, this, nxt, last=True):
                    v.drain()
                    if this:
                        soft_in(v, ring, i, p, 0, neg, h)
                        soft_in(v, ring, i, p, 1, neg, h)
                        soft_out(v, p, 0, h)
                        soft_out(v, p, 1, h)
                    if normed and nxt:
                        mean_squares(ring, i, p + 1)
                    if this and last:
                        end[0](v, s, p - 1)
                    if normed and nxt:
                        divide(p + 1)
                    if this and last:
                        end[1](v, s, p - 1)
                    if normed and nxt:
                        turned(ring, i)

                step(s.pro, 0, -1, False, True)
                step(s.body, 0, 0, True, True, last=False)
                with v.Fori(1, PAIRS - 1) as p:
                    step(s.body, p, p, True, True)
                step(s.epi, 0, PAIRS - 1, True, False)
                v.drain()
                end[0](v, s, PAIRS - 1)
                end[1](v, s, PAIRS - 1)

            return tensor, scalar, vector, None

        def keep_stream(v, p, bias):
            if bias:
                v.tensor_tensor(pair(x_all, p), xr[:], row(bias), ALU.add)
            else:
                v.tensor_copy(pair(x_all, p), xr[:])

        def end_residual(bias=None):
            def first_part(v, s, p):
                v.wait_ge(y_filled, p + yb(s))
                v.tensor_tensor(xr[:], ybank, pair(x_all, p), ALU.add)
                v.drain()
                keep_stream(v, p, bias)
                norm_stats(v, xr)

            def second_part(v, s, p):
                v.wait_ge(xt_filled, g_of(s, p) + BUMP)
                norm_apply(v, xr, xn, root(s, p, 1)).then_inc(xn_ready, 1)
            return first_part, second_part

        def end_decoder(gain, shift, bias):
            def first_part(v, s, p):
                v.wait_ge(y_filled, p + yb(s))
                v.tensor_tensor(xr[:], ybank, pair(tok_all, p), ALU.add)
                v.drain()
                norm_stats(v, xr)

            def second_part(v, s, p):
                v.wait_ge(xt_filled, g_of(s, p) + BUMP)
                norm_apply(v, xr, xn, root(s, p, 1))
                v.drain()
                v.tensor_tensor(xn[:], xn[:], row(gain), ALU.mult)
                v.drain()
                v.tensor_tensor(xn[:], xn[:], row(shift), ALU.add)
                v.drain()
                v.tensor_tensor(pair(tok_all, p), xn[:], row(bias), ALU.add).then_inc(xn_ready, 1)
            return first_part, second_part

        y_read = Handoff("y_read", 1)

        def ffn_tensor(pe):
            s = ffn2
            pe.wait_ge(xn_ready, g_of(s, 0))
            with pe.Fori(0, PAIRS) as p:
                g = g_of(s, p)
                pe.wait_ge(staged, g + 1 - PAIRS)
                up_product(pe, s, p, w("fc1"), xs)
                pe.drain().then_inc(inputs_used, 1)
                pe.wait_ge(*s.emptied(p, "up1"))
                pe.wait_ge(*y_read.at(p, 1))
                down_product(pe, w("fc2"), hT)
                turn_normed(pe, g)

        def up_product(pe, s, p, weights, src):
            wv = weights.rearrange("p (c f) -> p c f", f=P)
            for j in range(2):
                pe.wait_ge(*s.bank_free(p, f"up{j}"))
                for i in range(2):
                    ins = pe.matmul(bank(s.bank(f"up{j}"))[:, i * PT:(i + 1) * PT], wv[:, 2 * j + i, :], src[:],
                                    start=True, stop=True)
                ins.then_inc(banks_filled, 1)

        def down_product(pe, weights, hidden, y=None):
            y = ybank if y is None else y
            wv = weights.rearrange("p (c f) -> p c f", f=D)
            for u in range(2):
                for c in range(4):
                    ins = pe.matmul(y[:, u, :], hidden[:, c, u * P:(u + 1) * P], wv[:, c, :], start=(c == 0),
                                    stop=(c == 3))
            ins.then_inc(y_filled, 1)

        def ffn_scalar(act):
            s = ffn2
            with act.Fori(0, PAIRS) as p:
                for j in range(2):
                    act.wait_ge(banks_filled, s.filled(p, f"up{j}"))
                    for i in range(2):
                        ins = act.activation(hT[:, 2 * j + i, :], bank(s.bank(f"up{j}"))[:, i * PT:(i + 1) * PT],
                                             ACT.Gelu, bias=w("fc1b")[:, 2 * j + i:2 * j + i + 1])
                    ins.then_inc(act_emptied, 1)
                store_turned(act, g_of(s, p), before(act, p))

        def ffn_vector(v):
            s = ffn2
            with v.Fori(0, PAIRS) as p:
                v.drain()
                v.wait_ge(y_filled, p + yb(s))
                v.tensor_tensor(xr[:], ybank, pair(tok_all, p), ALU.add).then_inc(y_read.sem, 1)
                v.drain()
                norm_rows(v, xr, xr, root(s, p, 1))
                v.drain()
                v.tensor_tensor(xr[:], xr[:], row("ln3_g"), ALU.mult)
                v.drain()
                v.tensor_tensor(xr[:], xr[:], row("ln3_b"), ALU.add)
                v.drain()
                v.tensor_tensor(xr[:], xr[:], pair(x_all, p), ALU.add)
                finish(v, s, p, g_of(s, p), "tern_b")

        tq = work[:, 0:PT]
        tz = work[:, PT:2 * PT]
        tm = work[:, 2 * PT:3 * PT]
        tc = work[:, 3 * PT:4 * PT]
        td = work[:, 4 * PT:5 * PT]
        over = work[:, 5 * PT:6 * PT]
        under = work[:, 6 * PT:7 * PT]
        tern_ready = Handoff("tern_ready", 1)

        def tern_tensor(pe):
            s = tern
            pe.wait_ge(converted, 1)
            with pe.Fori(0, PAIRS) as p:
                pe.wait_ge(*tern_ready.at(p, 1))
                for u in range(2):
                    ins = pe.matmul(ybank[:, u, :], tz[:, u * P:(u + 1) * P], ternw[:], start=True, stop=True)
                ins.then_inc(y_filled, 1)
                turn_normed(pe, g_of(s, p))

        def tern_scalar(act):
            with act.Fori(0, PAIRS) as p:
                store_turned(act, g_of(tern, p), before(act, p))

        def tern_vector(v):
            s = tern
            v.memset(tc, 1.0e4)
            v.memset(td, -1.0e4)
            v.wait_ge(rest_in, 96)
            v.tensor_scalar(actscale[:, 0:1], actscale[:, 0:1], 1e-5, None, ALU.max)
            v.drain()
            v.reciprocal(actscale[:, 1:2], actscale[:, 0:1])

            def quantised(p):
                v.wait_ge(staged, g_of(s, p) + 1 - PAIRS)
                v.tensor_scalar(tq, xs[:], actscale[:, 1:2], ROUND, ALU.mult, ALU.add)
                v.memset(tz, 0.0)
                v.drain()
                v.tensor_scalar(tq, tq, ROUND, -127.0, ALU.subtract, ALU.max).then_inc(inputs_used, 1)
                v.drain()
                v.tensor_scalar(tq, tq, 127.0, actscale[:, 0:1], ALU.min, ALU.mult)
                v.drain()
                v.tensor_tensor(tm, tq, tq, ALU.is_equal)
                v.tensor_scalar(over, tq, FLT_MAX, None, ALU.is_gt)
                v.tensor_scalar(under, tq, -FLT_MAX, None, ALU.is_lt)
                v.drain()
                v.copy_predicated(tz, tm.bitcast(U32), tq)
                v.drain()
                v.copy_predicated(tz, over.bitcast(U32), tc)
                v.drain()
                v.copy_predicated(tz, under.bitcast(U32), td).then_inc(tern_ready.sem, 1)

            def step(p, nxt=True):
                v.drain()
                v.wait_ge(y_filled, p + yb(s))
                v.tensor_tensor(xr[:], ybank, pair(x_all, p), ALU.add)
                v.drain()
                keep_stream(v, p, "l3_bo")
                norm_stats(v, xr)
                if nxt:
                    quantised(p + 1)
                v.wait_ge(xt_filled, g_of(s, p) + BUMP)
                norm_apply(v, xr, xn, root(s, p, 1)).then_inc(xn_ready, 1)

            v.drain()
            quantised(0)
            with v.Fori(0, PAIRS - 1) as p:
                step(p)
            step(PAIRS - 1, nxt=False)

        q3 = work[:, 0:256]
        k3 = work[:, 256:512]
        v3 = work[:, 512:1024]
        vx = work[:, 1024:1536].rearrange("p (u b n) -> p u b n", u=2, b=2)
        o3 = work[:, 1536:1792].rearrange("p (u d) -> p u d", u=2)
        o3T = work[:, 1792:2048]
        kx = work[:, 2048:6144].rearrange("p (u b h k) -> p u b h k", u=2, b=2, h=16)
        h3 = {k: Handoff(f"l3_{k}", 2) for k in ("arg", "exp", "prob")}
        h3["values"] = Handoff("l3_values", 1)
        h3["spread"] = Handoff("l3_spread", 2)
        end3 = end_residual("l3_bout")


        def steps3(eng, part):
            s = att3
            for ring in (s.pro, s.one, s.body, s.epi):
                if eng is nc.tensor:
                    eng.wait_ge(act_emptied, ring.base["a"])
                    eng.wait_ge(dve_emptied, ring.base["v"])
                if ring is s.pro:
                    part(ring, 0, -1, None)
                elif ring is s.one:
                    part(ring, 0, 0, 1)
                elif ring is s.body:
                    part(ring, 0, 1, None)
                    with eng.Fori(2, PAIRS - 1) as p:
                        part(ring, p - 1, p, 2)
                else:
                    part(ring, 0, PAIRS - 1, 2)

        def att3_tensor(pe):
            s = att3

            def heads(ring, i, p, name):
                pe.wait_ge(*h3["values"].at(p, 1))
                settle(pe)
                pe.wait_ge(*ring.bank_free(i, name))
                settle(pe)
                for u in range(2):
                    for b in range(2):
                        for hp in range(8):
                            a = u * D + hp * 16
                            ins = pe.matmul(bank(ring.bank(name))[b * S:(b + 1) * S, a:a + 16],
                                            pT[:, u, hp, b * S:(b + 1) * S], vx[:, u, b, hp * 16:hp * 16 + 16],
                                            start=True, stop=True)
                ins.then_inc(banks_filled, 1)

            def heads_turned(ring, i, name, source):
                pe.wait_ge(*ring.emptied(i, source))
                settle(pe)
                pe.wait_ge(*ring.bank_free(i, name))
                for u in range(2):
                    ins = pe.transpose(bank(ring.bank(name))[:, u * P:(u + 1) * P], o3[:, u, :], ident[:])
                ins.then_inc(banks_filled, 1)

            def result(ring, i, name):
                pe.wait_ge(*ring.emptied(i, name))
                for u in range(2):
                    ins = pe.matmul(ybank[:, u, :], o3T[:, u * P:(u + 1) * P], w("l3_wo"), start=True, stop=True)
                ins.then_inc(y_filled, 1)

            def part(ring, i, p, turn):
                if ring is not s.pro:
                    for u in range(2):
                        pe.wait_ge(*h3["spread"].at(p, u + 1))
                        for half in range(2):
                            pe.wait_ge(*ring.bank_free(i, f"s{u}{half}"))
                            settle(pe)
                            for b in range(2):
                                t0 = (2 * u + b) * S
                                ins = pe.matmul(bank(ring.bank(f"s{u}{half}"))[b * S:(b + 1) * S, :],
                                                q3[:, t0:t0 + S],
                                                kx[:, u, b, 8 * half:8 * half + 8, :].rearrange("p h k -> p (h k)"),
                                                start=True, stop=True)
                            ins.then_inc(banks_filled, 1)
                if turn:
                    turn_normed(pe, g_of(s, p) + (1 - turn))
                if ring is not s.epi:
                    pe.wait_ge(xt_stored, g_of(s, p) + 3 - PAIRS)
                    settle(pe)
                    pe.wait_ge(*ring.bank_free(i, "qk"))
                    bk = bank(ring.bank("qk"))
                    pe.matmul(bk[:, 0:PT], w("l3_wq"), cols(xT_all, p + 1), start=True, stop=True)
                    pe.matmul(bk[:, PT:2 * PT], w("l3_wk"), cols(ctxT_all, p + 1), start=True, stop=True) \
                        .then_inc(banks_filled, 1)
                if ring is s.pro:
                    return
                if ring is not s.one:
                    if ring is s.body:
                        pe.wait_ge(*ring.emptied_before(i, "p11"))
                        settle(pe)
                    heads(ring, i, p - 1, "o")
                pe.wait_ge(staged, g_of(s, p) + 1 - PAIRS)
                settle(pe)
                pe.wait_ge(*ring.bank_free(i, "v"))
                settle(pe)
                for c in range(4):
                    for half in range(2):
                        ins = pe.matmul(bank(ring.bank("v"))[half * S:(half + 1) * S, c * D:(c + 1) * D],
                                        cs[:, c * S:(c + 1) * S], w("l3_wv"), start=True, stop=True)
                ins.then_inc(banks_filled, 1)
                pe.drain().then_inc(inputs_used, 1)
                if ring is not s.one:
                    heads_turned(ring, i, "oT", "o")
                probs_turned(pe, ring, i, p, 0, h3)
                if ring is not s.one:
                    result(ring, i, "oT")
                probs_turned(pe, ring, i, p, 1, h3)
                if ring is s.epi:
                    turn_normed(pe, g_of(s, p))
                    pe.wait_ge(*ring.emptied(i, "p11"))
                    settle(pe)
                    heads(ring, i, p, "o_last")
                    heads_turned(ring, i, "oT_last", "o_last")
                    result(ring, i, "oT_last")
            steps3(pe, part)

        def att3_scalar(act):
            s = att3

            def heads(ring, i, name):
                act.wait_ge(banks_filled, ring.filled(i, name))
                act.activation(o3.rearrange("p u d -> p (u d)"), bank(ring.bank(name))[:, 0:PT], ACT.Copy) \
                    .then_inc(act_emptied, 1)

            def heads_turned(ring, i, name):
                act.wait_ge(banks_filled, ring.filled(i, name))
                act.activation(o3T, bank(ring.bank(name))[:, 0:PT], ACT.Copy).then_inc(act_emptied, 1)

            def part(ring, i, p, turn):
                if ring is not s.epi:
                    act.wait_ge(banks_filled, ring.filled(i, "qk"))
                    bk = bank(ring.bank("qk"))
                    act.activation(q3, bk[:, 0:PT], ACT.Identity, bias=w("l3_qkb")[:, 0:1])
                    act.activation(k3, bk[:, PT:2 * PT], ACT.Identity, bias=w("l3_qkb")[:, 1:2]) \
                        .then_inc(act_emptied, 1)
                if ring is s.pro:
                    return
                if turn:
                    store_turned(act, g_of(s, p) + (1 - turn), before(act, p) if turn == 1 else p - 2)
                soft_exp(act, p, 0, 8.0 ** -0.5, h3)
                soft_exp(act, p, 1, 8.0 ** -0.5, h3)
                if ring is not s.one:
                    heads(ring, i, "o")
                    heads_turned(ring, i, "oT")
                store_probs(act, ring, i, 0)
                store_probs(act, ring, i, 1)
                if ring is s.epi:
                    store_turned(act, g_of(s, p), p - 1)
                    heads(ring, i, "o_last")
                    heads_turned(ring, i, "oT_last")
            steps3(act, part)

        def att3_pool(g, ring, i):
            g.wait_ge(*ring.emptied(i, "qk"))
            for u in range(2):
                for b in range(2):
                    t0 = (2 * u + b) * S
                    ins = g.tensor_tensor(kx[:, u, b, :, :], k3[:, None, t0:t0 + S].to_broadcast([P, 16, S]),
                                          headmask[:, :, None].to_broadcast([P, 16, S]), ALU.mult)
                ins.then_inc(h3["spread"].sem, 1)

        def att3_vector(v):
            s = att3

            def part(ring, i, p, turn):
                if ring is s.pro:
                    return
                v.drain()
                soft_in(v, ring, i, p, 0, None, h3)
                soft_in(v, ring, i, p, 1, None, h3)
                soft_out(v, p, 0, h3)
                soft_out(v, p, 1, h3)
                v.wait_ge(banks_filled, ring.filled(i, "v"))
                v.tensor_tensor(v3.rearrange("p (c d) -> p c d", d=D),
                                bank(ring.bank("v")).rearrange("p (c d) -> p c d", d=D), row("l3_bv", 4),
                                ALU.add).then_inc(dve_emptied, 1)
                v.drain()
                v.tensor_tensor(vx.rearrange("p u b (c a e) -> p (u b c) a e", c=8, a=2),
                                v3.rearrange("p (g a e) -> p g a e", a=2, e=8),
                                parity[:, None, :, None].to_broadcast([P, 32, 2, 8]), ALU.mult)
                v.drain().then_inc(h3["values"].sem, 1)
                if ring is not s.one:
                    end3[0](v, s, p - 1)
                    end3[1](v, s, p - 1)

            steps3(v, part)
            v.drain()
            end3[0](v, s, PAIRS - 1)
            end3[1](v, s, PAIRS - 1)

        hid = work[:, 0:4 * T].rearrange("p (c t) -> p c t", c=4)
        hqs = [work[:, 4 * T + 1024 * k:4 * T + 1024 * k + 4 * PT].rearrange("p (c t) -> p c t", c=4) for k in range(2)]
        wsc = w("m0_up")[:, 0:1536]
        q_ready = Handoff("q_ready", 1) if layers == 8 else None
        hq_ready = Handoff("hq_ready", 1) if layers == 8 else None
        amax_asked = sem("amax_asked")
        amax_given = sem("amax_given")
        LAST = PAIRS * (len(run) - 1)

        def round16(v, ap, src, sc):
            v.tensor_scalar(ap, src, sc, ROUND, ALU.mult, ALU.add)
            v.drain()
            return v.tensor_scalar(ap, ap, ROUND, -32768.0, ALU.subtract, ALU.max)

        def hid3_tensor(pe):
            s = hid3
            turn_normed(pe, LAST)
            for k in range(2):
                pe.wait_ge(q_ready.sem, k + 1)
                with pe.Fori(PAIRS // 2 * k, PAIRS // 2 * (k + 1)) as p:
                    up_product(pe, s, p, w("l3_in"), cols(xT_all, p))

        def hid3_scalar(act):
            s = hid3
            store_turned(act, LAST, PAIRS - 1)
            with act.Fori(0, PAIRS // 4) as quad:
                for k in range(4):
                    p = quad * 4 + k
                    for j in range(2):
                        act.wait_ge(banks_filled, s.filled(p, f"up{j}"))
                        for i in range(2):
                            ins = act.activation(hid[:, 2 * j + i, bass.ds(PT * p, PT)],
                                                 bank(s.bank(f"up{j}"))[:, i * PT:(i + 1) * PT],
                                                 ACT.Gelu, bias=w("l3_inb")[:, 2 * j + i:2 * j + i + 1])
                        ins.then_inc(act_emptied, 1)

        def scales(v, m, sc, inv, top):
            v.tensor_scalar(m, m, 1e-8, None, ALU.max)
            v.drain()
            v.reciprocal(sc, m)
            v.tensor_scalar(inv, m, 1.0 / top, None, ALU.mult)
            v.drain()
            v.tensor_scalar(sc, sc, top, None, ALU.mult)
            v.drain()

        def quantise_weights(v):
            v.wait_ge(weights_in[4], 16)
            wo4 = w("l3_out").rearrange("p (c f) -> p c f", f=D)
            v.tensor_reduce(amax[:, 4:8], wo4, AX, ALU.max, apply_absolute_value=True)
            v.drain()
            scales(v, amax[:, 4:8], amax[:, 8:12], amax[:, 12:16], 127.0)
            for c in range(4):
                v.tensor_scalar(wo4[:, c, :], wo4[:, c, :], amax[:, 8 + c:9 + c], ROUND, ALU.mult, ALU.add)
            v.drain()
            v.tensor_scalar(w("l3_out"), w("l3_out"), ROUND, -128.0, ALU.subtract, ALU.max)
            v.drain()
            for c in range(4):
                v.tensor_scalar(wo4[:, c, :], wo4[:, c, :], 127.0, amax[:, 12 + c:13 + c], ALU.min, ALU.mult)
            v.wait_ge(amax_given, 1)
            m, sc, inv = (wsc[:, 512 * i:512 * i + 512] for i in range(3))
            scales(v, m, sc, inv, 127.0)
            v.tensor_tensor(w("l3_in"), w("l3_in"), sc, ALU.mult)
            v.drain()
            v.tensor_scalar(w("l3_in"), w("l3_in"), ROUND, None, ALU.add)
            v.drain()
            v.tensor_scalar(w("l3_in"), w("l3_in"), ROUND, -128.0, ALU.subtract, ALU.max)
            v.drain()
            v.tensor_scalar(w("l3_in"), w("l3_in"), 127.0, None, ALU.min)
            v.drain()
            v.tensor_tensor(w("l3_in"), w("l3_in"), inv, ALU.mult)

        def columns_max(g):
            g.wait_ge(weights_in[4], 16)
            g.partition_all_reduce(wsc[:, 0:512], w("l3_in"), P, ABSMAX).then_inc(amax_given, 1)

        def hid3_vector(v):
            s = hid3
            v.wait_ge(xt_stored, LAST + 1)
            v.tensor_reduce(amax[:, 0:1], xT_all[:], AX, ALU.max, apply_absolute_value=True).then_inc(amax_asked, 1)
            v.wait_ge(amax_given, 2)
            scales(v, amax[:, 1:2], amax[:, 2:3], amax[:, 3:4], 32767.0)
            for k in range(2):
                half = xT_all[:, T // 2 * k:T // 2 * (k + 1)]
                round16(v, half, half, amax[:, 2:3])
                v.drain()
                v.tensor_scalar(half, half, 32767.0, amax[:, 3:4], ALU.min, ALU.mult).then_inc(q_ready.sem, 1)
            with v.Fori(0, PAIRS) as p:
                v.wait_ge(*s.emptied(p, "up1"))
                v.tensor_reduce(small[:, bass.ds(p, 1)], hid[:, :, bass.ds(PT * p, PT)], mybir.AxisListType.XY,
                                ALU.max, apply_absolute_value=True)
            v.drain()
            v.tensor_reduce(amax[:, 0:1], small[:, 0:PAIRS], AX, ALU.max).then_inc(amax_asked, 1)
            v.wait_ge(amax_given, 3)
            scales(v, amax[:, 1:2], amax[:, 2:3], amax[:, 3:4], 32767.0)

        def hid3_pool(g):
            g.wait_ge(amax_asked, 1)
            g.partition_all_reduce(amax[:, 1:2], amax[:, 0:1], P, ABSMAX).then_inc(amax_given, 1)
            g.wait_ge(amax_asked, 2)
            g.partition_all_reduce(amax[:, 1:2], amax[:, 0:1], P, ABSMAX).then_inc(amax_given, 1)

        def out3_tensor(pe):
            with pe.Fori(0, PAIRS // 2) as j:
                for k in range(2):
                    pe.wait_ge(*hq_ready.at(2 * j + k, 1))
                    down_product(pe, w("l3_out"), hqs[k], (ybank, xtbank.rearrange("p (u d) -> p u d", u=2))[k])

        def out3_vector(v):
            s = out3

            def rounding(p, k):
                round16(v, hqs[k], hid[:, :, bass.ds(PT * p, PT)], amax[:, 2:3])
                v.drain()
                v.tensor_scalar(hqs[k], hqs[k], 32767.0, amax[:, 3:4], ALU.min, ALU.mult).then_inc(hq_ready.sem, 1)

            def output(p, k):
                v.wait_ge(y_filled, p + yb(s))
                y = (ybank, xtbank.rearrange("p (u d) -> p u d", u=2))[k]
                v.tensor_tensor(pair(x_all, p), y, pair(x_all, p), ALU.add).then_inc(out_ready, 1)

            rounding(0, 0)
            rounding(1, 1)
            with v.Fori(0, PAIRS // 2 - 1) as j:
                for k in range(2):
                    output(2 * j + k, k)
                    rounding(2 * j + (2 + k), k)
            for k in range(2):
                output(PAIRS - 2 + k, k)

        prog = {}
        if lstm in run:
            for k, n in (("rows", 1), ("operands", 1), ("scans", 1), ("abs", 1), ("ln", 1), ("D", 1), ("hvar", 1), ("hroot", 1)):
                h_lstm[k] = Handoff("lstm_" + k, n)

            def lstm_pool(g, p):
                g.wait_ge(*h_lstm["hvar"].at(p, 1))
                g.tensor_tensor(lstm_hq, lstm_hs, nhalf[:, 0:8], ALU.pow).then_inc(h_lstm["hroot"].sem, 1)
            prog[lstm] = (lstm_tensor, lstm_scalar, lstm_vector, lstm_pool)
        if moe0 in run:
            prog[moe0] = moe("m0", moe0, "m0", 8, 2, ACT.Gelu, 0)
        if att1 in run:
            prog[att1] = attention("a1", att1, "a1_wq", "a1_wk", "a1_wv", "a1_wo", True, 2, neg_len, end_residual())
        if moe1 in run:
            prog[moe1] = moe("m1", moe1, "m1", 9, 1, ACT.Silu, 1)
        if satt in run:
            prog[satt] = attention("sa", satt, "sa_wq", "sa_wk", "sa_wv", "sa_wo", False, 4, neg_mask,
                                   end_decoder("ln1_g", "ln1_b", "ca_bo"))
            prog[catt] = attention("ca", catt, "ca_wq", "ca_wk", "ca_wv", "ca_wo", False, 4, neg_mask,
                                   end_decoder("ln2_g", "ln2_b", "fc2_b"))
            prog[ffn2] = (ffn_tensor, ffn_scalar, ffn_vector, None)
        if tern in run:
            prog[tern] = (tern_tensor, tern_scalar, tern_vector, None)
        if att3 in run:
            prog[att3] = (att3_tensor, att3_scalar, att3_vector, None)
        if hid3 in run:
            prog[hid3] = (hid3_tensor, hid3_scalar, hid3_vector, None)
            prog[out3] = (out3_tensor, lambda act: None, out3_vector, None)

        def stage_inputs(g, s, p):
            k = g_of(s, p)
            g.wait_ge(xt_stored, k + 2 - PAIRS)
            g.wait_ge(inputs_used, k + 1 - PAIRS)
            if s not in (att3, lstm):
                g.tensor_copy(xs[:], cols(xT_all, p))
            if s in (lstm, att1, catt, att3):
                g.tensor_copy(cs[:], cols(ctxT_all, p))
            if s is lstm:
                g.tensor_tensor(lstm_q, cols(xT_all, p)[:, None, :].to_broadcast([P, 4, PT]),
                                quarter[:, :, None].to_broadcast([P, 4, PT]), ALU.mult)
            g.drain().then_inc(staged, 1)

        def masks(v):
            v.tensor_copy(lensf[:], lens_i)
            v.tensor_copy(ternw[:], tern_i)
            v.drain()
            v.tensor_tensor(neg_len[:].rearrange("p (b k) -> p b k", k=S), iseq[:, None, :].to_broadcast([P, B, S]),
                            lensf[:, :, None].to_broadcast([P, B, S]), ALU.is_ge)
            v.tensor_scalar(neg_mask[:], mask_u8, -NEG, None, ALU.mult)
            v.tensor_scalar(ternw[:], ternw[:], -1.0, None, ALU.add)
            v.drain()
            v.tensor_scalar(neg_len[:], neg_len[:], -NEG, None, ALU.mult)
            v.drain().then_inc(converted, 1)

        def take_last(g, pending):
            s, early = pending
            if early:
                early(g, PAIRS - 1)
            for k in range(roots[s][1] if s is not first else 0):
                take_root(g, s, PAIRS - 1, k + 1)

        block = es.enter_context(nc.Block())

        @block.sync
        def _(sp):
            sp.dma_start(x_all[:], x_in.rearrange("(t p) d -> p t d", p=P)).then_inc(x_in_done, 16)
            bounds = ["gates", "m0_router", "a1_wq", "m1_router", "sa_wq", None]
            for i in range(5):
                a = wcol[bounds[i]][0]
                z = wcol[bounds[i + 1]][0] if bounds[i + 1] else WIDTH
                if i == 1:
                    sp.dma_start(ctxT_all[:], ctxT_in).then_inc(ctx_in_done, 16)
                    sp.dma_start(tok_all[:], ctx_in.rearrange("(t p) d -> p t d", p=P)).then_inc(ctx_in_done, 16)
                    sp.dma_start(rows[:], rows_in.partition_broadcast(P)).then_inc(rest_in, 16)
                    sp.dma_start(moeb[:], moeb_in).then_inc(rest_in, 16)
                    sp.dma_start(lens_i, lens_in.partition_broadcast(P)).then_inc(rest_in, 16)
                    sp.dma_start(mask_u8, mask_in.partition_broadcast(P)).then_inc(rest_in, 16)
                    sp.dma_start(tern_i, tern_in).then_inc(rest_in, 16)
                    sp.dma_start(actscale[:, 0:1], scale_in.partition_broadcast(P)).then_inc(rest_in, 16)
                sp.dma_start(W[:, a:z], wpack[:, a:z]).then_inc(weights_in[i], 16)
            if layers < 8:
                sp.wait_ge(xn_ready, PAIRS * len(stages_run))
                sp.dma_start(out.rearrange("(t p) d -> p t d", p=P), x_all[:]).then_inc(out_stored, 16)
                sp.wait_ge(out_stored, 16)
            else:
                with sp.Fori(0, PAIRS) as p:
                    sp.wait_ge(out_ready, p + 1)
                    sp.dma_start(out[bass.ds(PT * p, PT), :].rearrange("(u p) d -> p u d", p=P),
                                 pair(x_all, p)).then_inc(out_stored, 16)
                sp.wait_ge(out_stored, 16 * PAIRS)

        @block.gpsimd
        def _(g):
            g.memset(ident[:], 0.0)
            g.memset(nhalf[:], -0.5)
            g.memset(warm[:], 0.0)
            g.memset(euler[:], 2.718281828459045)
            g.memset(headmask[:], 1.0)
            g.memset(causal[:], 0.0)
            g.iota(ix[:].rearrange("p u e -> p (u e)").bitcast(I32), [[1, 16]], base=0, channel_multiplier=0)
            g.drain()
            g.affine_select(out=ident[:], in_=ident[:], compare_op=ALU.not_equal, fill=1.0, base=0,
                            pattern=[[-1, P]], channel_multiplier=1)
            g.affine_select(out=headmask[:], in_=headmask[:], compare_op=ALU.is_ge, fill=0.0, base=0,
                            pattern=[[-8, 16]], channel_multiplier=1)
            g.drain()
            for b in range(2):
                g.affine_select(out=causal[b * S:(b + 1) * S, :], in_=causal[b * S:(b + 1) * S, :],
                                compare_op=ALU.is_ge, fill=-NEG, base=0, pattern=[[1, S]], channel_multiplier=-1)
                g.drain()
            g.tensor_copy(iota8[:], ix[:].rearrange("p u e -> p (u e)").bitcast(I32))
            g.iota(xs[:, 0:S].bitcast(I32), [[1, S]], base=0, channel_multiplier=0)
            g.drain()
            g.affine_select(out=headmask[:], in_=headmask[:], compare_op=ALU.is_ge, fill=0.0, base=7,
                            pattern=[[8, 16]], channel_multiplier=-1)
            g.tensor_copy(iseq[:], xs[:, 0:S].bitcast(I32))
            g.memset(lstm_v[:, :, :, 32:33], 1.0)
            g.drain()
            g.drain().then_inc(consts_made, 1)
            g.drain().then_inc(inputs_used, 1)
            g.wait_ge(var_ready, 1)
            g.tensor_tensor(rstd16, var16, nhalf[:, 0:TILES], ALU.pow).then_inc(rstd_ready, 1)
            g.wait_ge(ctx_in_done, 32)
            pending = (first, None)
            for s in run + [None]:
                if s in (hid3, out3):
                    if s is hid3:
                        take_last(g, pending)
                        hid3_pool(g)
                        pending = None
                    continue
                if s is None:
                    if pending:
                        take_last(g, pending)
                    continue
                if pending[1]:
                    pending[1](g, PAIRS - 1)
                stage_inputs(g, s, 0)
                if s is satt and hid3 in run:
                    columns_max(g)
                take_last(g, (pending[0], None))
                if s is att3:
                    att3_pool(g, s.pro, 0)
                    att3_pool(g, s.one, 0)
                    stage_inputs(g, s, 1)
                    att3_pool(g, s.body, 0)
                    stage_inputs(g, s, 2)
                    take_root(g, s, 0, 1)
                    with g.Fori(2, PAIRS - 1) as p:
                        att3_pool(g, s.body, p - 1)
                        stage_inputs(g, s, p + 1)
                        take_root(g, s, p - 1, 1)
                    take_root(g, s, PAIRS - 2, 1)
                    pending = (s, None)
                    continue
                if s in (att1, satt, catt):
                    stage_inputs(g, s, 1)
                    with g.Fori(1, PAIRS - 1) as p:
                        stage_inputs(g, s, p + 1)
                        take_root(g, s, p - 1, 1)
                    take_root(g, s, PAIRS - 2, 1)
                    pending = (s, None)
                    continue
                early = prog[s][3]
                if s is lstm:
                    stage_inputs(g, s, 1)
                    early(g, 0)
                    with g.Fori(1, PAIRS - 1) as p:
                        stage_inputs(g, s, p + 1)
                        take_root(g, s, p - 1, 1)
                        early(g, p)
                    take_root(g, s, PAIRS - 2, 1)
                    early(g, PAIRS - 1)
                    pending = (s, None)
                    continue
                if s in (moe0, moe1):
                    early(g, 0)
                    stage_inputs(g, s, 1)
                    with g.Fori(1, PAIRS - 1) as p:
                        early(g, p)
                        take_root(g, s, p - 1, 1)
                        stage_inputs(g, s, p + 1)
                    early(g, PAIRS - 1)
                    take_root(g, s, PAIRS - 2, 1)
                    pending = (s, None)
                    continue
                with g.Fori(0, PAIRS - 1) as p:
                    if early:
                        early(g, p)
                    stage_inputs(g, s, p + 1)
                    for k in range(roots[s][1]):
                        take_root(g, s, p, k + 1)
                pending = (s, early)

        @block.vector
        def _(v):
            v.memset(parity[:], 0.0)
            v.memset(restart[:], 1.0)
            v.memset(restart_neg[:], 0.0)
            v.drain()
            v.memset(parity[0:S, 0:1], 1.0)
            v.memset(parity[S:P, 1:2], 1.0)
            v.memset(quarter[:], 0.0)
            v.drain()
            for h in range(4):
                v.memset(quarter[32 * h:32 * h + 32, h:h + 1], 1.0)
            v.memset(restart[:, 0:PT:S], 0.0)
            v.memset(restart_neg[:, 0:PT:S], -NEG)
            v.wait_ge(consts_made, 1)
            v.reduce_sum(row1[:], ident[:, 0:P:32], AX)
            v.reduce_sum(row2[:], ident[:, 1:P:32], AX)
            v.tensor_copy(row1h[:], ident[:, 0:P:32])
            v.tensor_scalar(negrow2[:], ident[:, 1:P:32], -1.0, None, ALU.mult)
            v.drain().then_inc(xt_filled, BUMP)
            v.drain().then_inc(y_read.sem, 1)
            v.drain().then_inc(dve_emptied, BUMP)
            first_vector(v)
            v.wait_ge(rest_in, 96)
            v.tensor_scalar(lstm_ow, row("out_w"), 1.0, None, ALU.add)
            masks(v)
            for s in run:
                if s is catt and hid3 in run:
                    quantise_weights(v)
                prog[s][2](v)

        @block.scalar
        def _(act):
            act.drain().then_inc(xt_stored, 1)
            act.wait_ge(consts_made, 1)
            act.drain().then_inc(act_emptied, BUMP)
            for p in range(PAIRS - 1):
                store_turned(act, p + 1, p)
            for s in run:
                prog[s][1](act)

        @block.tensor
        def _(pe):
            pe.wait_ge(consts_made, 1)
            with pe.Fori(0, PAIRS - 1) as p:
                turn_normed(pe, p + 1)
            for s in run:
                pe.wait_ge(act_emptied, s.base["a"])
                pe.wait_ge(dve_emptied, s.base["v"])
                prog[s][0](pe)


def pack(i):
    import numpy as np

    def chunks(a, n):
        return np.asarray(a).reshape(n, P, -1).transpose(1, 0, 2).reshape(P, -1)

    a = {k: np.asarray(v) for k, v in i.items()}
    ig, fg = a["L0_xattn_igate_w"], a["L0_xattn_fgate_w"]
    parts = {
        "gates": np.concatenate([np.repeat(g[:, 128 * k:128 * k + 128].T, 32, axis=1) for g in (ig, fg)
                                 for k in range(3)], axis=1),
        "gate_bias": np.stack([np.repeat(a["L0_xattn_igate_b"], 32), np.repeat(a["L0_xattn_fgate_b"], 32)], axis=1),
        "m0_router": a["L0_ffn_router_w"].T,
        "m0_up": a["L0_ffn_w1"].transpose(2, 0, 1).reshape(P, -1),
        "m0_upb": a["L0_ffn_b1"].reshape(16, P).T,
        "m0_down": chunks(a["L0_ffn_w2"].transpose(0, 2, 1).reshape(2048, P), 16),
        "a1_wq": a["L1_xattn_Wq"], "a1_wk": a["L1_xattn_Wk"], "a1_wv": a["L1_xattn_Wv"],
        "a1_wo": chunks(a["L1_xattn_Wo"], 8),
        "a1_norm": np.stack([np.tile(a["L1_xattn_q_norm_w"], 2), np.tile(a["L1_xattn_k_norm_w"], 2)], axis=1),
        "m1_router": a["L1_ffn_gate_w"].T,
        "m1_up": np.concatenate([chunks(a["L1_ffn_up_w"].reshape(1024, P), 8), a["L1_ffn_sh_up_w"]], axis=1),
        "m1_upb": np.concatenate([a["L1_ffn_up_b"], a["L1_ffn_sh_up_b"][None]]).T,
        "m1_down": np.concatenate([chunks(a["L1_ffn_down_w"].reshape(1024, P), 8), a["L1_ffn_sh_down_w"]], axis=1),
        "sa_wq": a["L2_xattn_sa_wq"], "sa_wk": a["L2_xattn_sa_wk"], "sa_wv": a["L2_xattn_sa_wv"],
        "sa_wo": chunks(a["L2_xattn_sa_wo"], 8),
        "ca_wq": a["L2_xattn_ca_wq"], "ca_wk": a["L2_xattn_ca_wk"], "ca_wv": a["L2_xattn_ca_wv"],
        "ca_wo": chunks(a["L2_xattn_ca_wo"], 8),
        "fc1": a["L2_xattn_fc1_w"], "fc1b": a["L2_xattn_fc1_b"].reshape(4, P).T, "fc2": chunks(a["L2_xattn_fc2_w"], 4),
        "l3_wq": a["L3_xattn_Wq"].T, "l3_wk": a["L3_xattn_Wk"].T, "l3_wv": a["L3_xattn_Wv"].T,
        "l3_wo": a["L3_xattn_Wo"].T, "l3_qkb": np.stack([a["L3_xattn_bq"], a["L3_xattn_bk"]], axis=1),
        "l3_in": a["L3_ffn_W_in"], "l3_inb": a["L3_ffn_b_in"].reshape(4, P).T, "l3_out": chunks(a["L3_ffn_W_out"], 4),
    }
    rows = {"out_w": "L0_xattn_out_w", "sa_bo": "L2_xattn_sa_bo", "ca_bo": "L2_xattn_ca_bo", "fc2_b": "L2_xattn_fc2_b",
            "tern_b": "L2_ffn_bias", "l3_bv": "L3_xattn_bv", "l3_bo": "L3_xattn_bo", "l3_bout": "L3_ffn_b_out"}
    for k in "123":
        rows[f"ln{k}_g"], rows[f"ln{k}_b"] = f"L2_xattn_ln{k}_g", f"L2_xattn_ln{k}_b"
    moeb = np.zeros((9, 2, D), np.float32)
    moeb[0:8, 0] = a["L0_ffn_b2"]
    moeb[0:8, 1] = a["L1_ffn_down_b"]
    moeb[8, 1] = a["L1_ffn_sh_down_b"]
    ctx = a["ctx_1024"].reshape(T, D)
    return {
        "wpack": np.concatenate([parts[n] for n, _ in SECTIONS], axis=1),
        "x_in": a["x"].reshape(T, D), "ctx_in": ctx, "ctxT_in": ctx.T,
        "rows_in": np.stack([a[rows[n]] for n in ROWS]), "moeb_in": moeb,
        "lens_in": a["_lenS2"], "mask_in": a["mask_BxS2_bk0"].reshape(T),
        "tern_in": a["L2_ffn_ternary_weight"].T, "scale_in": a["L2_ffn_act_scale"].reshape(1),
    }


LAYERS = 8


def kernel(**inputs):
    import numpy as np
    import concourse.bacc as bacc
    from concourse.bass_utils import run_bass_kernel_spmd

    nc = bacc.Bacc("TRN2", target_bir_lowering=False, num_devices=1)
    arrays = {k: np.ascontiguousarray(v) for k, v in pack(inputs).items()}
    aps = [nc.dram_tensor(k, v.shape, mybir.dt.from_np(v.dtype), kind="ExternalInput").ap() for k, v in arrays.items()]
    out = nc.dram_tensor("out", (T, D), F32, kind="ExternalOutput").ap()
    build_program(nc, *aps, out, layers=LAYERS)
    r = run_bass_kernel_spmd(nc, [arrays], core_ids=[0])
    return r.results[0]["out"].reshape(B, S, D)
```
